# Optimizing a Trainium2 kernel written in Bass

```python
import numpy as np
import jax
import jax.numpy as jnp

def _softmax(x, axis=-1):
    return jax.nn.softmax(x, axis=axis)

def _gelu(x):
    return jax.nn.gelu(x, approximate=True)

def _silu(x):
    return jax.nn.silu(x)

def _sigmoid(x):
    return jax.nn.sigmoid(x)

def _layernorm(x, axis=-1, eps=1e-05):
    m = jnp.mean(x, axis=axis, keepdims=True)
    v = jnp.var(x, axis=axis, keepdims=True)
    return (x - m) / jnp.sqrt(v + eps)

def _scatter_add(tgt, idx, src, axis=0):
    return tgt.at[idx].add(src)

def _segment_sum(src, seg, n):
    return jax.ops.segment_sum(src, seg, n)
kernel_name = 'mk_seq_preln_d1_jaxref_r8_150055'

def setup_inputs(seed: int=0):
    np.random.seed(seed)
    _w = jnp.asarray

    def _L0_attn_setup():
        import jax, jax.numpy as jnp
        from jax import lax
        import numpy as np
        D = 128
        H = 16
        DK = 64
        DV = 128
        KDIM = H * DK
        VDIM = H * DV
        CONV_K = 4
        B, T = (2, 512)
        EPS = 1e-05

        def _causal_conv_silu(x, w):
            C = x.shape[-1]
            Kw = w.shape[-1]
            xp = jnp.pad(x, ((0, 0), (Kw - 1, 0), (0, 0))).transpose(0, 2, 1)
            y = lax.conv_general_dilated(xp, w[:, None, :], window_strides=(1,), padding='VALID', feature_group_count=C, dimension_numbers=('NCH', 'OIH', 'NCH'))
            return jax.nn.silu(y.transpose(0, 2, 1))

        def _l2norm(x, eps=1e-06):
            return x * lax.rsqrt(jnp.sum(x * x, axis=-1, keepdims=True) + eps)

        def _gated_delta_rule(q, k, v, g, beta):
            scale = q.shape[-1] ** (-0.5)
            qs = jnp.moveaxis(q, 1, 0)
            ks_ = jnp.moveaxis(k, 1, 0)
            vs = jnp.moveaxis(v, 1, 0)
            gs = jnp.moveaxis(g, 1, 0)
            bs = jnp.moveaxis(beta, 1, 0)

            def step(S, inp):
                q_t, k_t, v_t, g_t, b_t = inp
                S = S * jnp.exp(g_t)[..., None, None]
                mem = jnp.einsum('bhk,bhkv->bhv', k_t, S)
                delta = (v_t - mem) * b_t[..., None]
                S = S + jnp.einsum('bhk,bhv->bhkv', k_t, delta)
                o_t = jnp.einsum('bhk,bhkv->bhv', q_t * scale, S)
                return (S, o_t)
            S0 = jnp.zeros((q.shape[0], q.shape[2], q.shape[3], v.shape[3]), q.dtype)
            _, o = lax.scan(step, S0, (qs, ks_, vs, gs, bs))
            return jnp.moveaxis(o, 0, 1)
        key = jax.random.key(seed)
        ks = jax.random.split(key, 14)

        def w(k, shape, s=0.02):
            return jax.random.normal(k, shape, jnp.float32) * s
        return {'x': jax.random.normal(ks[0], (B, T, D), jnp.float32), 'w_q': w(ks[1], (D, KDIM)), 'w_k': w(ks[2], (D, KDIM)), 'w_v': w(ks[3], (D, VDIM)), 'w_a': w(ks[4], (D, H)), 'w_b': w(ks[5], (D, H)), 'w_g': w(ks[6], (D, VDIM)), 'w_out': w(ks[7], (VDIM, D)), 'A_log': jnp.log(jax.random.uniform(ks[8], (H,), jnp.float32, 1.0, 16.0)), 'dt_bias': jax.random.uniform(ks[9], (H,), jnp.float32, -4.0, -1.0), 'conv_q': w(ks[10], (KDIM, CONV_K), 0.1), 'conv_k': w(ks[11], (KDIM, CONV_K), 0.1), 'conv_v': w(ks[12], (VDIM, CONV_K), 0.1), 'norm_w': jnp.ones((DV,), jnp.float32)}
    _L0_attn_in = _L0_attn_setup()

    def _L0_ffn_setup():
        import jax, jax.numpy as jnp
        import numpy as np
        HIDDEN = 128
        N_EXPERTS = 8
        TOP_K = 2
        INTER = 176
        N_SHARED = 2
        SCALE = 1.0
        key = jax.random.key(seed)
        ks = jax.random.split(key, 9)
        s_h = 1.0 / np.sqrt(HIDDEN)
        s_i = 1.0 / np.sqrt(INTER)
        x = jax.random.normal(ks[0], (2, 256, HIDDEN), dtype=jnp.float32)
        gate_w = jax.random.uniform(ks[1], (N_EXPERTS, HIDDEN), jnp.float32, -s_h, s_h)
        wg = jax.random.uniform(ks[2], (N_EXPERTS, HIDDEN, INTER), jnp.float32, -s_h, s_h)
        wu = jax.random.uniform(ks[3], (N_EXPERTS, HIDDEN, INTER), jnp.float32, -s_h, s_h)
        wd = jax.random.uniform(ks[4], (N_EXPERTS, INTER, HIDDEN), jnp.float32, -s_i, s_i)
        si = INTER * N_SHARED
        s_si = 1.0 / np.sqrt(si)
        swg = jax.random.uniform(ks[5], (HIDDEN, si), jnp.float32, -s_h, s_h)
        swu = jax.random.uniform(ks[6], (HIDDEN, si), jnp.float32, -s_h, s_h)
        swd = jax.random.uniform(ks[7], (si, HIDDEN), jnp.float32, -s_si, s_si)
        return {'x': x, 'gate_w': gate_w, 'wg': wg, 'wu': wu, 'wd': wd, 'swg': swg, 'swu': swu, 'swd': swd}
    _L0_ffn_in = _L0_ffn_setup()
    _d = {'L0_attn_x': _L0_attn_in['x'], 'L0_attn_w_q': _L0_attn_in['w_q'], 'L0_attn_w_k': _L0_attn_in['w_k'], 'L0_attn_w_v': _L0_attn_in['w_v'], 'L0_attn_w_a': _L0_attn_in['w_a'], 'L0_attn_w_b': _L0_attn_in['w_b'], 'L0_attn_w_g': _L0_attn_in['w_g'], 'L0_attn_w_out': _L0_attn_in['w_out'], 'L0_attn_A_log': _L0_attn_in['A_log'], 'L0_attn_dt_bias': _L0_attn_in['dt_bias'], 'L0_attn_conv_q': _L0_attn_in['conv_q'], 'L0_attn_conv_k': _L0_attn_in['conv_k'], 'L0_attn_conv_v': _L0_attn_in['conv_v'], 'L0_attn_norm_w': _L0_attn_in['norm_w'], 'L0_ffn_gate_w': _L0_ffn_in['gate_w'], 'L0_ffn_wg': _L0_ffn_in['wg'], 'L0_ffn_wu': _L0_ffn_in['wu'], 'L0_ffn_wd': _L0_ffn_in['wd'], 'L0_ffn_swg': _L0_ffn_in['swg'], 'L0_ffn_swu': _L0_ffn_in['swu'], 'L0_ffn_swd': _L0_ffn_in['swd']}
    _x0 = _d['L0_attn_x']
    _d['L0_attn_x'] = jax.random.normal(jax.random.fold_in(jax.random.key(seed), 1), (16, 256, 128), dtype=_x0.dtype)
    del _x0
    return _d

def reference(L0_attn_x, L0_attn_w_q, L0_attn_w_k, L0_attn_w_v, L0_attn_w_a, L0_attn_w_b, L0_attn_w_g, L0_attn_w_out, L0_attn_A_log, L0_attn_dt_bias, L0_attn_conv_q, L0_attn_conv_k, L0_attn_conv_v, L0_attn_norm_w, L0_ffn_gate_w, L0_ffn_wg, L0_ffn_wu, L0_ffn_wd, L0_ffn_swg, L0_ffn_swu, L0_ffn_swd):

    def _L0_attn_ref(x, w_q, w_k, w_v, w_a, w_b, w_g, w_out, A_log, dt_bias, conv_q, conv_k, conv_v, norm_w):
        import jax, jax.numpy as jnp
        from jax import lax
        import numpy as np
        D = 128
        H = 16
        DK = 64
        DV = 128
        KDIM = H * DK
        VDIM = H * DV
        CONV_K = 4
        B, T = (2, 512)
        EPS = 1e-05

        def _causal_conv_silu(x, w):
            C = x.shape[-1]
            Kw = w.shape[-1]
            xp = jnp.pad(x, ((0, 0), (Kw - 1, 0), (0, 0))).transpose(0, 2, 1)
            y = lax.conv_general_dilated(xp, w[:, None, :], window_strides=(1,), padding='VALID', feature_group_count=C, dimension_numbers=('NCH', 'OIH', 'NCH'))
            return jax.nn.silu(y.transpose(0, 2, 1))

        def _l2norm(x, eps=1e-06):
            return x * lax.rsqrt(jnp.sum(x * x, axis=-1, keepdims=True) + eps)

        def _gated_delta_rule(q, k, v, g, beta):
            scale = q.shape[-1] ** (-0.5)
            qs = jnp.moveaxis(q, 1, 0)
            ks_ = jnp.moveaxis(k, 1, 0)
            vs = jnp.moveaxis(v, 1, 0)
            gs = jnp.moveaxis(g, 1, 0)
            bs = jnp.moveaxis(beta, 1, 0)

            def step(S, inp):
                q_t, k_t, v_t, g_t, b_t = inp
                S = S * jnp.exp(g_t)[..., None, None]
                mem = jnp.einsum('bhk,bhkv->bhv', k_t, S)
                delta = (v_t - mem) * b_t[..., None]
                S = S + jnp.einsum('bhk,bhv->bhkv', k_t, delta)
                o_t = jnp.einsum('bhk,bhkv->bhv', q_t * scale, S)
                return (S, o_t)
            S0 = jnp.zeros((q.shape[0], q.shape[2], q.shape[3], v.shape[3]), q.dtype)
            _, o = lax.scan(step, S0, (qs, ks_, vs, gs, bs))
            return jnp.moveaxis(o, 0, 1)
        Bx, Tx, _ = x.shape
        q = x @ w_q
        k = x @ w_k
        v = x @ w_v
        beta = jax.nn.sigmoid(x @ w_b) * 2.0
        g = -jnp.exp(A_log) * jax.nn.softplus(x @ w_a + dt_bias)
        q = _causal_conv_silu(q, conv_q)
        k = _causal_conv_silu(k, conv_k)
        v = _causal_conv_silu(v, conv_v)
        q = q.reshape(Bx, Tx, H, DK)
        k = k.reshape(Bx, Tx, H, DK)
        v = v.reshape(Bx, Tx, H, DV)
        q = _l2norm(q)
        k = _l2norm(k)
        o = _gated_delta_rule(q, k, v, g, beta)
        g_gate = (x @ w_g).reshape(Bx, Tx, H, DV)
        rms = o * lax.rsqrt(jnp.mean(o * o, axis=-1, keepdims=True) + EPS)
        y = rms * norm_w * jax.nn.silu(g_gate)
        return y.reshape(Bx, Tx, VDIM) @ w_out

    def _L0_ffn_ref(x, gate_w, wg, wu, wd, swg, swu, swd):
        import jax, jax.numpy as jnp
        import numpy as np
        HIDDEN = 128
        N_EXPERTS = 8
        TOP_K = 2
        INTER = 176
        N_SHARED = 2
        SCALE = 1.0
        B, S, H = x.shape
        xf = x.reshape(-1, H)
        T = xf.shape[0]
        logits = xf.astype(jnp.float32) @ gate_w.astype(jnp.float32).T
        scores = jax.nn.softmax(logits, axis=-1)
        topw, topi = jax.lax.top_k(scores, TOP_K)
        denom = topw.sum(axis=-1, keepdims=True) + 1e-20
        topw = topw / denom * SCALE
        wdense = jnp.zeros((T, N_EXPERTS), jnp.float32).at[jnp.arange(T)[:, None], topi].set(topw)
        hg = jnp.einsum('th,ehi->eti', xf, wg)
        hu = jnp.einsum('th,ehi->eti', xf, wu)
        eo = jnp.einsum('eti,eih->eth', jax.nn.silu(hg) * hu, wd)
        y = jnp.einsum('te,eth->th', wdense, eo)
        shared = jax.nn.silu(xf @ swg) * (xf @ swu) @ swd
        return (y + shared).reshape(B, S, H)
    x = L0_attn_x
    x = x + _L0_attn_ref(_layernorm(x, axis=-1), L0_attn_w_q, L0_attn_w_k, L0_attn_w_v, L0_attn_w_a, L0_attn_w_b, L0_attn_w_g, L0_attn_w_out, L0_attn_A_log, L0_attn_dt_bias, L0_attn_conv_q, L0_attn_conv_k, L0_attn_conv_v, L0_attn_norm_w)
    x = x + _L0_ffn_ref(_layernorm(x, axis=-1), L0_ffn_gate_w, L0_ffn_wg, L0_ffn_wu, L0_ffn_wd, L0_ffn_swg, L0_ffn_swu, L0_ffn_swd)
    return x

_drawn_inputs = setup_inputs


def setup_inputs(seed=0):
    import zlib

    import numpy as np

    out = dict(_drawn_inputs(seed))
    spreads = {'L0_attn_norm_w': (1.0, 0.6)}
    factors = {'L0_attn_w_q': 2.896,
     'L0_attn_w_k': 2.913,
     'L0_attn_w_v': 2.914,
     'L0_attn_w_a': 8.0,
     'L0_attn_w_b': 8.0,
     'L0_attn_w_g': 2.944,
     'L0_attn_w_out': 2.913,
     'L0_attn_A_log': 7.654,
     'L0_attn_dt_bias': 5.843,
     'L0_attn_conv_q': 2.942,
     'L0_attn_conv_k': 2.91,
     'L0_attn_conv_v': 2.904}
    for name, (base, spread) in spreads.items():
        noise = np.random.default_rng([zlib.crc32(name.encode()), seed]).standard_normal(out[name].shape)
        drawn = base * np.exp(spread * noise) if base else spread * noise
        out[name] = jnp.asarray(drawn.astype(out[name].dtype))
    for name, factor in factors.items():
        out[name] = (out[name] * factor).astype(out[name].dtype)
    return out
```

```python
from contextlib import ExitStack

import concourse.bass as bass
from concourse import mybir

F32 = mybir.dt.float32
I32 = mybir.dt.int32
ALU = mybir.AluOpType
ACT = mybir.ActivationFunctionType
AX_X = mybir.AxisListType.X

P = 128
HEADS = 16
DK = 64
DV = 128
TAPS = 4
TILES = 2
TOK = TILES * P
PAD = TAPS - 1
BLOCKS = 2 * HEADS * DK // P
QBLOCKS = BLOCKS // 2
GROUPS = 8
SUPERS = 4
HALF = P // 2
LEVELS = (2, 4, 8, 16, 32)
EXPERTS = 8
INTER = 176
UNIT = 2 * INTER
CHUNKS = EXPERTS // 2 + 1
HID = CHUNKS * UNIT
RSQRT_MAGIC = float(0x5F3759DF)
LN_EPS = 1e-5
L2_EPS = 1e-6
RMS_EPS = 1e-5
Q_SCALE = DK ** -0.5

C_ID, C_LE, C_GT, C_I64, C_WM, C_YM = 0, 128, 256, 384, 448, 512
C_IND = C_YM + 64 * len(LEVELS)
C_END = C_IND + 2


def build_layer(nc, x, w_q, w_k, w_v, w_a, w_b, w_g, w_out, A_log, dt_bias, conv_q, conv_k, conv_v,
                norm_w, gate_w, wg, wu, wd, swg, swu, swd, consts, out):
    batches = x.shape[0]

    with ExitStack() as ctx:
        def sb(name, shape, dt=F32):
            return ctx.enter_context(nc.sbuf_tensor(name, shape, dt))

        def sem(name):
            return ctx.enter_context(nc.semaphore(name))

        w_qk = sb("w_qk", [P, 2 * HEADS * DK])
        w_vtap = sb("w_vtap", [P, TAPS, HEADS * DV])
        w_gate = sb("w_gate", [P, HEADS * DV])
        w_o = sb("w_o", [P, HEADS, P])
        w_ab = sb("w_ab", [P, 2 * HEADS])
        w_up1 = sb("w_up1", [P, HID])
        w_up2 = sb("w_up2", [P, HID])
        w_down = sb("w_down", [P, CHUNKS, 3, P])
        w_route = sb("w_route", [P, EXPERTS])
        taps = sb("taps", [P, BLOCKS, TAPS])
        norm_col = sb("norm_col", [P, 1])
        dt_row = sb("dt_row", [P, HEADS])
        decay_row = sb("decay_row", [P, HEADS])
        con = sb("con", [P, C_END])
        rank_row = sb("rank_row", [P, EXPERTS])
        ident = con[:, C_ID:C_ID + P]
        le_mask = con[:, C_LE:C_LE + P]
        gt_mask = con[:, C_GT:C_GT + P]
        i64 = con[:, C_I64:C_I64 + HALF]
        first_mask = con[:, C_WM:C_WM + HALF]
        ind2 = con[:, C_IND:C_IND + 2]

        xin = sb("xin", [P, TILES, P])
        xn = sb("xn", [P, TILES, P])
        xT = sb("xT", [P, PAD + TOK])
        qkT = sb("qkT", [P, BLOCKS, TOK])
        eb = sb("eb", [P, GROUPS, 4, P])
        nt = sb("nt", [P, GROUPS, 4, P])
        tinv = sb("tinv", [P, SUPERS, 8, HALF])
        winv = sb("winv", [P, SUPERS, 8, HALF])
        ymid = sb("ymid", [P, SUPERS, 8, HALF])
        vr = sb("vr", [P, TILES, HEADS, DV])
        ysol = sb("ysol", [P, TILES, HEADS, DV])
        state = sb("state", [P, HEADS // 2, DV])
        ktok = sb("ktok", [P, HEADS, DK])
        kscale = sb("kscale", [P, HEADS])
        small = sb("small", [P, 26, 2 * 32])
        stats = sb("stats", [P, TILES, 8])
        mv = sb("mv", [P, TILES, 2])
        x2 = sb("x2", [P, TILES, P])
        yo = sb("yo", [P, TILES, P])

        flat_y = ysol[:, :, :, :].rearrange("p c h d -> p (c h d)")
        flat_v = vr[:, :, :, :].rearrange("p c h d -> p (c h d)")
        sq = flat_y.rearrange("p (j t) -> p j t", t=TOK)
        flat_ymid = ymid[:, :, :, :].rearrange("p s i t -> p (s i t)")
        gm = [flat_ymid[:, 512 * i:512 * (i + 1)].rearrange("p (h t) -> p h t", h=4) for i in range(2)]
        bm = [flat_ymid[:, 1024 + 512 * i:1024 + 512 * (i + 1)].rearrange("p (h t) -> p h t", h=4) for i in range(2)]
        sgate = nt[:, :, :, :].rearrange("p g k t -> p (g k t)").rearrange("p (c h d) -> p c h d", c=TILES, h=HEADS)
        oT = eb
        sgf = [flat_y[:, UNIT * i:UNIT * (i + 1)] for i in range(2)]
        sgw = [flat_y[:, UNIT * (2 + i):UNIT * (3 + i)] for i in range(2)]
        zf = [flat_y[:, UNIT * (4 + i):UNIT * (5 + i)] for i in range(2)]
        zT = [flat_y[:, UNIT * 6 + 384 * i:UNIT * 6 + 384 * (i + 1)] for i in range(2)]
        hT = flat_y[:, UNIT * 6 + 768:UNIT * 6 + 768 + TOK]

        def heads_of(g):
            q, par = (g % 4) // 2, g % 2
            return [8 * q + par + 2 * k for k in range(4)]

        def by_group(t, g):
            c, q, par = g // 4, (g % 4) // 2, g % 2
            v = t[:, c]
            v = v[:, 8 * q:8 * q + 8]
            if len(v.shape) == 3:
                return v.rearrange("p (k two) d -> p two k d", two=2)[:, par]
            return v.rearrange("p (k two) -> p two k", two=2)[:, par]

        def over_cols(v, n):
            return v.unsqueeze(2).broadcast_to([P, v.shape[1], n])

        def over_heads(v, n):
            return v.unsqueeze(1).broadcast_to([P, n, v.shape[1]])

        banks = [ctx.enter_context(nc.psum_tensor(f"bank{i}", [P, 512], F32)) for i in range(8)]
        order = [("xT", 0), ("ab", 0)]
        order += [("qk", i) for i in range(BLOCKS // 2)]
        order += [("v", i) for i in range(GROUPS)]
        order += [("gam", 0)] + [("decay", g) for g in range(GROUPS)]
        order += [("norms", 0)]
        order += [("kk", g) for g in range(GROUPS)]
        order += [("first", s) for s in range(SUPERS)]
        order += [("qk_", g) for g in range(GROUPS)]
        order += [("ktok", q) for q in range(2)]
        for n in LEVELS:
            order += [("Y", n, s) for s in range(SUPERS)]
            order += [(k, n, s) for s in range(SUPERS) for k in ("TY", "WY")]
        order += [("Y64", s) for s in range(SUPERS)] + [("W64", s) for s in range(SUPERS)]
        order += [("y", g) for g in range(4)] + [("state", q) for q in range(2)] + [("o", g) for g in range(4)]
        order += [("ks", g) for g in range(4, 8)]
        order += [("y", g) for g in range(4, 8)]
        order += [(k, g) for g in range(4, 8) for k in ("o", "qs")]
        order += [("gate", i) for i in range(GROUPS)]
        order += [("oT", g) for g in range(GROUPS)]
        order += [("attn", c) for c in range(TILES)]
        order += [("hT", 0), ("route", 0)]
        order += [("down", 0), ("down", 1)]
        fill_at = {k: (i % 8, i // 8) for i, k in enumerate(order)}
        before = {k: order[i - 8] for i, k in enumerate(order) if i >= 8}
        units = [(k, c) for k in range(CHUNKS) for c in range(TILES)]
        turn = {b: sum(1 for k in order if fill_at[k][0] == b) for b in range(8)}
        held = {fill_at[("down", 0)][0], fill_at[("down", 1)][0]}
        free = [b % 8 for b in range(len(order), len(order) + 8) if b % 8 not in held]
        last_in = {fill_at[k][0]: k for k in order}
        n = 0
        for k, c in units:
            for what in ("up1", "up2", "zT"):
                b = free[n % len(free)]
                fill_at[(what, k, c)] = (b, turn[b])
                before[(what, k, c)] = last_in[b]
                last_in[b] = (what, k, c)
                turn[b] += 1
                n += 1

        bank_filled = [sem(f"bank_filled{i}") for i in range(8)]

        def bank(*key):
            return banks[fill_at[key][0]]

        def full(*key):
            return bank_filled[fill_at[key][0]]

        def await_fill(eng, *key):
            b, t = fill_at[key]
            eng.wait_ge(bank_filled[b], t + 1)

        x_loaded = sem("x_loaded")
        x_normed = sem("x_normed")
        xT_ready = sem("xT_ready")
        ab_args = sem("ab_args")
        ab_exps = sem("ab_exps")
        g_ready = sem("g_ready")
        tap3_done = sem("tap3_done")
        conv_done = sem("conv_done")
        qk_ready = sem("qk_ready")
        sq_ready = sem("sq_ready")
        v_ready = sem("v_ready")
        gm_ready = sem("gm_ready")
        gamma_ready = sem("gamma_ready")
        decay_ready = sem("decay_ready")
        b_ready = sem("b_ready")
        bm_ready = sem("bm_ready")
        B_ready = sem("B_ready")
        nt_ready = sem("nt_ready")
        winit_part = sem("winit_part")
        w_ready = sem("w_ready")
        t_ready = sem("t_ready")
        y_masked = sem("y_masked")
        p_ready = sem("p_ready")
        kscale_ready = sem("kscale_ready")
        ktok_ready = sem("ktok_ready")
        y64_ready = sem("y64_ready")
        full_ready = sem("full_ready")
        r_ready = sem("r_ready")
        r1_ready = sem("r1_ready")
        y_ready = sem("y_ready")
        state_ready = sem("state_ready")
        o_copied = sem("o_copied")
        o_ready = sem("o_ready")
        o_squares = sem("o_squares")
        sgate_ready = sem("sgate_ready")
        gated = sem("gated")
        oT_ready = sem("oT_ready")
        x2_normed = sem("x2_normed")
        hT_ready = sem("hT_ready")
        route_args = sem("route_args")
        route_exps = sem("route_exps")
        w_exp_ready = sem("w_exp_ready")
        sg_ready = sem("sg_ready")
        sgw_ready = sem("sgw_ready")
        z_ready = sem("z_ready")
        zT_ready = sem("zT_ready")
        out_ready = sem("out_ready")
        out_stored = sem("out_stored")
        dve_step = sem("dve_step")
        conv_step = sem("conv_step")
        norms_read = sem("norms_read")
        x2_done = sem("x2_done")
        zT_used = sem("zT_used")
        w_part = sem("w_part")
        loop_sems = bank_filled + [
            conv_step, norms_read, x2_done, zT_used, w_part, x_loaded, x_normed, xT_ready, ab_args, ab_exps, g_ready, tap3_done, conv_done, qk_ready, sq_ready,
            v_ready, gm_ready, gamma_ready, decay_ready, b_ready, bm_ready, B_ready, nt_ready, winit_part,
            w_ready, t_ready, y_masked, p_ready, kscale_ready, ktok_ready, y64_ready, full_ready, r_ready, r1_ready,
            y_ready, state_ready, o_copied, o_ready, o_squares, sgate_ready, gated, oT_ready, x2_normed, hT_ready,
            route_args, route_exps, w_exp_ready, sg_ready, sgw_ready, z_ready, zT_ready, out_ready, out_stored,
            dve_step]
        weights_in = sem("weights_in")
        raw_in = sem("raw_in")
        prep_done = sem("prep_done")

        def level(n):
            return LEVELS.index(n)

        read_by = {
            "xT": lambda i: (xT_ready, 1), "ab": lambda i: (ab_args, 1), "qk": lambda i: (conv_done, i + 1),
            "v": lambda i: (v_ready, i + 1), "gam": lambda i: (gamma_ready, 1), "decay": lambda g: (decay_ready, g + 1),
            "norms": lambda i: (norms_read, 1), "kk": lambda g: (nt_ready, g + 1), "first": lambda s: (t_ready, s + 1),
            "qk_": lambda g: (p_ready, g + 1), "ktok": lambda q: (ktok_ready, q + 1),
            "Y": lambda n, s: (y_masked, SUPERS * level(n) + s + 1),
            "TY": lambda n, s: (t_ready, SUPERS * (level(n) + 1) + s + 1),
            "WY": lambda n, s: (w_ready, SUPERS * (level(n) + 1) + s + 1),
            "Y64": lambda s: (y64_ready, s + 1), "W64": lambda s: (full_ready, s + 1),
            "y": lambda g: (y_ready, g + 1), "state": lambda q: (state_ready, q + 1), "o": lambda g: (o_copied, g + 1),
            "ks": lambda g: (r1_ready, g - 3), "qs": lambda g: (o_ready, g - 3), "gate": lambda i: (sgate_ready, i + 1),
            "oT": lambda g: (oT_ready, g + 1), "attn": lambda c: (x2_done, c + 1), "hT": lambda i: (hT_ready, 1),
            "route": lambda i: (route_args, 1), "down": lambda c: (out_ready, c + 1),
            "up1": lambda k, c: (sg_ready, TILES * k + c + 1), "up2": lambda k, c: (z_ready, TILES * k + c + 1),
            "zT": lambda k, c: (zT_ready, TILES * k + c + 1),
        }

        def claim(pe, *key):
            if key in before:
                what, *at = before[key]
                pe.wait_ge(*read_by[what](*at))

        def sm(i, n=32):
            return small[:, i, 0:TILES * n].rearrange("p (c n) -> p c n", c=TILES)

        ab_arg, ab_exp, abt1, abt2, abt3, abt4 = (sm(i) for i in range(6))
        g_tok, beta_tok, m_tok, b_tok = (sm(6 + i, HEADS) for i in range(4))
        z_qk, rs_qk = sm(10), sm(11)
        gamma = small[:, 12, 0:HEADS]
        neg_gamma = small[:, 12, HEADS:2 * HEADS]
        o_ssq, o_fac, o_z = sm(13, HEADS), sm(14, HEADS), sm(15, HEADS)
        nw1, nw2 = small[:, 16, :], small[:, 17, :]
        rt = [sm(18 + i, EXPERTS) for i in range(7)]
        rtmax = small[:, 25, 0:2]
        rtsum = small[:, 25, 2:4]
        wexp = sb("wexp", [P, TILES, EXPERTS + 2])

        conv_rows = flat_v
        conv_all = qkT[:, :, :].rearrange("p j t -> p (j t)")
        wv_raw = nt[:, :, :, :].rearrange("p g k t -> p (g k t)")[:, 0:HEADS * DV]
        with nc.Block() as block:
            @block.sync
            def _(sp):
                loads = [
                    (w_qk[:, 0:HEADS * DK], w_q), (w_qk[:, HEADS * DK:], w_k), (w_gate[:, :], w_g),
                    (w_ab[:, 0:HEADS], w_a), (w_ab[:, HEADS:], w_b),
                    (taps[:, 0:QBLOCKS, :], conv_q.rearrange("(j p) w -> p j w", p=P)),
                    (taps[:, QBLOCKS:, :], conv_k.rearrange("(j p) w -> p j w", p=P)),
                    (dt_row[:, :], dt_bias.partition_broadcast(P)),
                    (w_up1[:, 0:EXPERTS * INTER].rearrange("p (e i) -> p e i", e=EXPERTS), wg.rearrange("e h i -> h e i")),
                    (w_up2[:, 0:EXPERTS * INTER].rearrange("p (e i) -> p e i", e=EXPERTS), wu.rearrange("e h i -> h e i")),
                    (w_up1[:, EXPERTS * INTER:], swg), (w_up2[:, EXPERTS * INTER:], swu),
                    (con[:, :], consts),
                    (w_route[:, :], gate_w.rearrange("e h -> h e")),
                ]
                flat_wd = wd.rearrange("e i h -> (e i) h")
                for k in range(CHUNKS):
                    src = flat_wd[UNIT * k:UNIT * (k + 1), :] if k < CHUNKS - 1 else swd
                    loads.append((w_down[:, k, 0:2, :], src[0:2 * P, :].rearrange("(j p) h -> p j h", p=P)))
                    loads.append((w_down[0:UNIT - 2 * P, k, 2, :], src[2 * P:UNIT, :]))
                with nc.allow_non_contiguous_dma(reason="the router's weights are small"):
                    for dst, src in loads:
                        sp.dma_start(dst, src).then_inc(weights_in, 16)
                sp.wait_ge(weights_in, 16 * len(loads))

            @block.scalar
            def _(act):
                raw = [
                    (wv_raw, w_v), (w_o[:, :, :], w_out.rearrange("(h d) n -> d h n", d=DV)),
                    (norm_col[:, :], norm_w.rearrange("(d one) -> d one", one=1)),
                    (decay_row[:, :], A_log.partition_broadcast(P)),
                    (conv_rows, conv_v.rearrange("c w -> (c w)")[0:4096].partition_broadcast(P)),
                    (conv_all, conv_v.rearrange("c w -> (c w)")[4096:8192].partition_broadcast(P)),
                ]
                for dst, src in raw:
                    act.dma_start(dst, src).then_inc(raw_in, 16)
                act.wait_ge(raw_in, 16 * len(raw))
                nc.scalar.activation(decay_row[:, :], decay_row[:, :], ACT.Exp).then_inc(prep_done, 1)

            @block.vector
            def _(dve):
                nc.vector.memset(xT[:, 0:PAD], 0.0)
                nc.vector.memset(wexp[:, :, EXPERTS:EXPERTS + 2], 1.0)
                for e in range(EXPERTS):
                    nc.vector.memset(rank_row[:, e:e + 1], float(EXPERTS - e))
                dve.wait_ge(raw_in, 16 * 6)
                nc.vector.tensor_scalar(w_o[:, :, :], w_o[:, :, :], norm_col[:, 0:1], None, ALU.mult)
                for half, rows in enumerate((conv_rows, conv_all)):
                    lo = half * 1024
                    r = rows.rearrange("p (c w) -> p w c", w=TAPS)
                    for j in range(TAPS):
                        nc.vector.tensor_tensor(w_vtap[:, j, lo:lo + 1024], wv_raw[:, lo:lo + 1024], r[:, j, :], ALU.mult)
                dve.wait_ge(prep_done, 1)
                nc.vector.tensor_scalar(decay_row[:, :], decay_row[:, :], -1.0, None, ALU.mult)

        with nc.Fori(0, batches) as b:
            with nc.Block() as block:
                @block.sync
                def _(sp):
                    xb = x[bass.ds(b, 1), :, :].rearrange("o (c p) d -> p (o c) d", p=P)
                    sp.dma_start(xin[:, :, :], xb).then_inc(x_loaded, 16)
                    ob = out[bass.ds(b, 1), :, :].rearrange("o (c p) d -> p (o c) d", p=P)
                    sp.wait_ge(out_ready, TILES)
                    sp.dma_start(ob, yo[:, :, :]).then_inc(out_stored, 16)
                    sp.wait_ge(out_stored, 16)

                @block.tensor
                def _(pe):
                    T = nc.tensor

                    def mm(o, l, r, start=True, stop=True):
                        return T.matmul(o, l, r, start=start, stop=stop)

                    claim(pe, "xT", 0)
                    pe.wait_ge(x_normed, 1)
                    for c in range(TILES):
                        last = T.transpose(bank("xT", 0)[:, c * P:(c + 1) * P], xn[:, c, :], ident)
                    last.then_inc(full("xT", 0), 1)
                    claim(pe, "ab", 0)
                    pe.wait_ge(xT_ready, 1)
                    for c in range(TILES):
                        last = mm(bank("ab", 0)[:, 32 * c:32 * (c + 1)], xT[:, PAD + c * P:PAD + (c + 1) * P], w_ab[:, :])
                    last.then_inc(full("ab", 0), 1)
                    for i in range(BLOCKS // 2):
                        claim(pe, "qk", i)
                        for j in range(2):
                            last = mm(bank("qk", i)[:, TOK * j:TOK * (j + 1)], w_qk[:, (2 * i + j) * P:(2 * i + j + 1) * P],
                                      xT[:, PAD:])
                        last.then_inc(full("qk", i), 1)
                    for i in range(GROUPS):
                        c, n = i // 4, i % 4
                        claim(pe, "v", i)
                        for j in range(TAPS):
                            last = mm(bank("v", i)[:, :], xT[:, c * P + j:c * P + j + P], w_vtap[:, j, 512 * n:512 * (n + 1)],
                                      start=(j == 0), stop=(j == TAPS - 1))
                        last.then_inc(full("v", i), 1)
                    claim(pe, "gam", 0)
                    pe.wait_ge(g_ready, 1)
                    mm(bank("gam", 0)[:, 0:HEADS], le_mask, g_tok[:, 1, :]).then_inc(full("gam", 0), 1)
                    for g in range(GROUPS):
                        claim(pe, "decay", g)
                        pe.wait_ge(gm_ready, g + 1)
                        mm(bank("decay", g)[:, :], gt_mask, gm[g % 2].rearrange("p h t -> p (h t)")).then_inc(full("decay", g), 1)
                    claim(pe, "norms", 0)
                    pe.wait_ge(sq_ready, BLOCKS // 2)
                    for c in range(TILES):
                        for j in range(BLOCKS):
                            at = 32 * c + 2 * j
                            last = mm(bank("norms", 0)[:, at:at + 2], sq[:, j, c * P:(c + 1) * P], ind2)
                    last.then_inc(full("norms", 0), 1)

                    def head_T(h, c, block0):
                        po = DK * (h % 2)
                        return qkT[po:po + DK, block0 + h // 2, c * P:(c + 1) * P]

                    for g in range(GROUPS):
                        claim(pe, "kk", g)
                        pe.wait_ge(qk_ready, BLOCKS // 2)
                        for k, h in enumerate(heads_of(g)):
                            kT = head_T(h, g // 4, QBLOCKS)
                            last = mm(bank("kk", g)[:, k * P:(k + 1) * P], kT, kT)
                        last.then_inc(full("kk", g), 1)
                    for s in range(SUPERS):
                        claim(pe, "first", s)
                        pe.wait_ge(w_ready, s + 1)
                        for i in range(8):
                            for lo in (0, HALF):
                                r = slice(lo, lo + HALF)
                                last = mm(bank("first", s)[r, HALF * i:HALF * (i + 1)], winv[r, s, i, :], i64[r, :])
                        last.then_inc(full("first", s), 1)
                    for g in range(GROUPS):
                        claim(pe, "qk_", g)
                        for k, h in enumerate(heads_of(g)):
                            last = mm(bank("qk_", g)[:, k * P:(k + 1) * P], head_T(h, g // 4, QBLOCKS), head_T(h, g // 4, 0))
                        last.then_inc(full("qk_", g), 1)
                    for q in range(2):
                        claim(pe, "ktok", q)
                        for j in range(4):
                            last = T.transpose(bank("ktok", q)[:, j * P:(j + 1) * P], qkT[:, QBLOCKS + 4 * q + j, 0:P], ident)
                        last.then_inc(full("ktok", q), 1)
                    for l, n in enumerate(LEVELS):
                        for s in range(SUPERS):
                            claim(pe, "Y", n, s)
                            pe.wait_ge(t_ready, SUPERS * l + s + 1)
                            for i in range(8):
                                for lo in (0, HALF):
                                    r = slice(lo, lo + HALF)
                                    last = mm(bank("Y", n, s)[r, HALF * i:HALF * (i + 1)],
                                              nt[r, 2 * s + i // 4, i % 4, lo:lo + HALF], tinv[r, s, i, :])
                            last.then_inc(full("Y", n, s), 1)
                        for s in range(SUPERS):
                            claim(pe, "TY", n, s)
                            pe.wait_ge(y_masked, SUPERS * l + s + 1)
                            pe.wait_ge(w_ready, SUPERS * (l + 1) + s + 1 - SUPERS)
                            for i in range(8):
                                for lo in (0, HALF):
                                    r = slice(lo, lo + HALF)
                                    last = mm(bank("TY", n, s)[r, HALF * i:HALF * (i + 1)], winv[r, s, i, :], ymid[r, s, i, :])
                            last.then_inc(full("TY", n, s), 1)
                            claim(pe, "WY", n, s)
                            for i in range(8):
                                for lo in (0, HALF):
                                    r = slice(lo, lo + HALF)
                                    last = mm(bank("WY", n, s)[r, HALF * i:HALF * (i + 1)], ymid[r, s, i, :], winv[r, s, i, :])
                            last.then_inc(full("WY", n, s), 1)
                    hi = slice(HALF, P)
                    lo_ = slice(0, HALF)
                    for s in range(SUPERS):
                        claim(pe, "Y64", s)
                        pe.wait_ge(t_ready, SUPERS * (len(LEVELS) + 0) + s + 1)
                        for i in range(8):
                            last = mm(bank("Y64", s)[hi, HALF * i:HALF * (i + 1)], nt[lo_, 2 * s + i // 4, i % 4, hi], tinv[lo_, s, i, :])
                        last.then_inc(full("Y64", s), 1)
                    for s in range(SUPERS):
                        claim(pe, "W64", s)
                        pe.wait_ge(y64_ready, s + 1)
                        pe.wait_ge(w_ready, SUPERS * len(LEVELS) + s + 1)
                        for i in range(8):
                            last = mm(bank("W64", s)[lo_, HALF * i:HALF * (i + 1)], ymid[hi, s, i, :], nt[hi, 2 * s + i // 4, i % 4, hi])
                        last.then_inc(full("W64", s), 1)

                    def solve(g):
                        claim(pe, "y", g)
                        pe.wait_ge(full_ready, g // 2 + 1)
                        if g < 4:
                            pe.wait_ge(r_ready, g + 1)
                        else:
                            pe.wait_ge(r1_ready, g - 3)
                        for k, h in enumerate(heads_of(g)):
                            last = mm(bank("y", g)[:, k * P:(k + 1) * P], nt[:, g, k, :], vr[:, g // 4, h, :])
                        last.then_inc(full("y", g), 1)

                    def attend(g):
                        claim(pe, "o", g)
                        pe.wait_ge(p_ready, g + 1)
                        pe.wait_ge(y_ready, g + 1)
                        for k, h in enumerate(heads_of(g)):
                            last = mm(bank("o", g)[:, k * P:(k + 1) * P], eb[:, g, k, :], ysol[:, g // 4, h, :])
                        last.then_inc(full("o", g), 1)

                    for g in range(4):
                        solve(g)
                    for q in range(2):
                        claim(pe, "state", q)
                        pe.wait_ge(ktok_ready, q + 1)
                        pe.wait_ge(y_ready, 2 * q + 2)
                        for h in range(8 * q, 8 * q + 8):
                            po, j = DK * (h % 2), (h % 8) // 2
                            last = mm(bank("state", q)[po:po + DK, j * DV:(j + 1) * DV], ktok[:, h, :], ysol[:, 0, h, :])
                        last.then_inc(full("state", q), 1)
                    for g in range(4):
                        attend(g)
                    for g in range(4, 8):
                        claim(pe, "ks", g)
                        pe.wait_ge(state_ready, (g - 4) // 2 + 1)
                        for k, h in enumerate(heads_of(g)):
                            po = DK * (h % 2)
                            last = mm(bank("ks", g)[:, k * P:(k + 1) * P], head_T(h, 1, QBLOCKS), state[po:po + DK, h // 2, :])
                        last.then_inc(full("ks", g), 1)
                    for g in range(4, 8):
                        solve(g)
                    for g in range(4, 8):
                        attend(g)
                        claim(pe, "qs", g)
                        for k, h in enumerate(heads_of(g)):
                            po = DK * (h % 2)
                            last = mm(bank("qs", g)[:, k * P:(k + 1) * P], head_T(h, 1, 0), state[po:po + DK, h // 2, :])
                        last.then_inc(full("qs", g), 1)
                    for i in range(GROUPS):
                        c, n = i // 4, i % 4
                        claim(pe, "gate", i)
                        mm(bank("gate", i)[:, :], xT[:, PAD + c * P:PAD + (c + 1) * P],
                           w_gate[:, 512 * n:512 * (n + 1)]).then_inc(full("gate", i), 1)
                    for g in range(GROUPS):
                        claim(pe, "oT", g)
                        pe.wait_ge(gated, g + 1)
                        for k, h in enumerate(heads_of(g)):
                            last = T.transpose(bank("oT", g)[:, k * P:(k + 1) * P], vr[:, g // 4, h, :], ident)
                        last.then_inc(full("oT", g), 1)
                    for c in range(TILES):
                        claim(pe, "attn", c)
                        for g in range(4 * c, 4 * c + 4):
                            pe.wait_ge(oT_ready, g + 1)
                            for k, h in enumerate(heads_of(g)):
                                last = mm(bank("attn", c)[:, 0:P], oT[:, g, k, :], w_o[:, h, :],
                                          start=(g % 4 == 0 and k == 0), stop=(g % 4 == 3 and k == 3))
                        last.then_inc(full("attn", c), 1)
                    claim(pe, "hT", 0)
                    pe.wait_ge(x2_normed, 1)
                    for c in range(TILES):
                        last = T.transpose(bank("hT", 0)[:, c * P:(c + 1) * P], xn[:, c, :], ident)
                    last.then_inc(full("hT", 0), 1)
                    claim(pe, "route", 0)
                    pe.wait_ge(hT_ready, 1)
                    for c in range(TILES):
                        last = mm(bank("route", 0)[:, EXPERTS * c:EXPERTS * (c + 1)], hT[:, c * P:(c + 1) * P], w_route[:, :])
                    last.then_inc(full("route", 0), 1)
                    claim(pe, "down", 0)
                    claim(pe, "down", 1)

                    def up(u):
                        k, c = units[u]
                        for what, w in (("up1", w_up1), ("up2", w_up2)):
                            claim(pe, what, k, c)
                            mm(bank(what, k, c)[:, 0:UNIT], hT[:, c * P:(c + 1) * P],
                               w[:, UNIT * k:UNIT * (k + 1)]).then_inc(full(what, k, c), 1)

                    def flip(u):
                        k, c = units[u]
                        claim(pe, "zT", k, c)
                        pe.wait_ge(z_ready, u + 1)
                        for j in range(3):
                            w = min(P, UNIT - j * P)
                            last = T.transpose(bank("zT", k, c)[0:w, j * P:(j + 1) * P], zf[u % 2][:, j * P:j * P + w], ident)
                        last.then_inc(full("zT", k, c), 1)

                    def down(u):
                        k, c = units[u]
                        pe.wait_ge(zT_ready, u + 1)
                        for j in range(3):
                            w = min(P, UNIT - j * P)
                            last = mm(bank("down", c)[:, 0:P], zT[u % 2][0:w, j * P:(j + 1) * P], w_down[0:w, k, j, :],
                                      start=(k == 0 and j == 0), stop=(k == CHUNKS - 1 and j == 2))
                        if k == CHUNKS - 1:
                            last.then_inc(full("down", c), 1)
                        else:
                            last.then_inc(zT_used, 1)

                    N = len(units)
                    for u in range(N + 2):
                        if u < N:
                            up(u)
                        if 1 <= u <= N:
                            flip(u - 1)
                        if u >= 2:
                            down(u - 2)

                @block.scalar
                def _(act):
                    A = nc.scalar
                    await_fill(act, "xT", 0)
                    A.activation(xT[:, PAD:], bank("xT", 0)[:, 0:TOK], ACT.Copy).then_inc(xT_ready, 1)
                    act.wait_ge(ab_args, 1)
                    A.activation(ab_exp, ab_arg, ACT.Exp, scale=-1.0).then_inc(ab_exps, 1)

                    def silu_qk(i):
                        act.wait_ge(conv_done, i + 1)
                        v = qkT[:, 2 * i:2 * i + 2, :]
                        A.activation(v, v, ACT.Silu).then_inc(qk_ready, 1)

                    for i in range(BLOCKS // 2):
                        await_fill(act, "qk", i)
                        for j in range(2):
                            last = A.activation(qkT[:, 2 * i + j, :], bank("qk", i)[:, TOK * j:TOK * (j + 1)], ACT.Copy,
                                                scale=taps[:, 2 * i + j, 3:4])
                        last.then_inc(tap3_done, 1)
                        if i:
                            silu_qk(i - 1)
                    silu_qk(BLOCKS // 2 - 1)
                    for i in range(GROUPS):
                        c, n = i // 4, i % 4
                        await_fill(act, "v", i)
                        A.activation(vr[:, c, 4 * n:4 * n + 4, :].rearrange("p h d -> p (h d)"), bank("v", i)[:, :],
                                     ACT.Silu).then_inc(v_ready, 1)
                    await_fill(act, "gam", 0)
                    A.activation(gamma, bank("gam", 0)[:, 0:HEADS], ACT.Exp).then_inc(gamma_ready, 1)
                    for g in range(GROUPS):
                        await_fill(act, "decay", g)
                        A.activation(eb[:, g, :, :].rearrange("p k t -> p (k t)"), bank("decay", g)[:, :],
                                     ACT.Exp).then_inc(decay_ready, 1)
                    for s in range(SUPERS):
                        await_fill(act, "first", s)
                        A.activation(tinv[:, s, :, :].rearrange("p i t -> p (i t)"), bank("first", s)[:, :],
                                     ACT.Copy).then_inc(t_ready, 1)
                    for s in range(SUPERS):
                        await_fill(act, "Y64", s)
                        A.activation(ymid[HALF:P, s, :, :].rearrange("p i t -> p (i t)"), bank("Y64", s)[HALF:P, :],
                                     ACT.Copy).then_inc(y64_ready, 1)
                    for s in range(SUPERS):
                        await_fill(act, "W64", s)
                        A.activation(nt[0:HALF, 2 * s:2 * s + 2, :, HALF:P].rearrange("p a k t -> p (a k) t"),
                                     bank("W64", s)[0:HALF, :].rearrange("p (i t) -> p i t", i=8),
                                     ACT.Copy).then_inc(full_ready, 1)
                    for g in range(4):
                        await_fill(act, "y", g)
                        A.activation(by_group(ysol, g), bank("y", g)[:, :].rearrange("p (k d) -> p k d", k=4),
                                     ACT.Copy).then_inc(y_ready, 1)
                    for q in range(2):
                        await_fill(act, "state", q)
                        A.activation(state[:, 4 * q:4 * q + 4, :].rearrange("p j d -> p (j d)"), bank("state", q)[:, :],
                                     ACT.Copy).then_inc(state_ready, 1)

                    def copy_o(g):
                        await_fill(act, "o", g)
                        A.activation(by_group(vr, g), bank("o", g)[:, :].rearrange("p (k d) -> p k d", k=4),
                                     ACT.Copy).then_inc(o_copied, 1)

                    def squares(g):
                        scratch = (winv if g < 4 else tinv)[:, g % 4].rearrange("p i t -> p (i t)")
                        for k, h in enumerate(heads_of(g)):
                            last = A.activation(scratch[:, k * DV:(k + 1) * DV], vr[:, g // 4, h, :], ACT.Square,
                                                accum_out=o_ssq[:, g // 4, h:h + 1])
                        last.then_inc(o_squares, 1)

                    for g in range(4):
                        copy_o(g)
                    for g in range(4):
                        act.wait_ge(o_copied, g + 1)
                        squares(g)
                    for g in range(4, 8):
                        await_fill(act, "y", g)
                        A.activation(by_group(ysol, g), bank("y", g)[:, :].rearrange("p (k d) -> p k d", k=4),
                                     ACT.Copy).then_inc(y_ready, 1)
                    for g in range(4, 8):
                        copy_o(g)
                    for g in range(4, 8):
                        act.wait_ge(o_ready, g - 3)
                        squares(g)
                    for i in range(GROUPS):
                        c, n = i // 4, i % 4
                        await_fill(act, "gate", i)
                        A.activation(sgate[:, c, 4 * n:4 * n + 4, :].rearrange("p h d -> p (h d)"), bank("gate", i)[:, :],
                                     ACT.Silu).then_inc(sgate_ready, 1)
                    for g in range(GROUPS):
                        await_fill(act, "oT", g)
                        A.activation(oT[:, g, :, :].rearrange("p k t -> p (k t)"), bank("oT", g)[:, :],
                                     ACT.Copy).then_inc(oT_ready, 1)
                    await_fill(act, "hT", 0)
                    A.activation(hT, bank("hT", 0)[:, 0:TOK], ACT.Copy).then_inc(hT_ready, 1)
                    act.wait_ge(route_args, 1)
                    A.activation(rt[1], rt[0], ACT.Exp).then_inc(route_exps, 1)
                    N = len(units)
                    for u in range(N + 1):
                        if u < N:
                            k, c = units[u]
                            await_fill(act, "up1", k, c)
                            if u >= 2:
                                act.wait_ge(sgw_ready, u - 1)
                            A.activation(sgf[u % 2], bank("up1", k, c)[:, 0:UNIT], ACT.Silu).then_inc(sg_ready, 1)
                        if u >= 1:
                            k, c = units[u - 1]
                            await_fill(act, "zT", k, c)
                            if u - 1 >= 2:
                                act.wait_ge(zT_used, u - 2)
                            A.activation(zT[(u - 1) % 2][:, 0:2 * P], bank("zT", k, c)[:, 0:2 * P], ACT.Copy)
                            w = UNIT - 2 * P
                            A.activation(zT[(u - 1) % 2][0:w, 2 * P:3 * P], bank("zT", k, c)[0:w, 2 * P:3 * P],
                                         ACT.Copy).then_inc(zT_ready, 1)

                @block.vector
                def _(dve):
                    V = nc.vector
                    steps = [0]

                    def link(ins):
                        steps[0] += 1
                        ins.then_inc(dve_step, 1)
                        dve.wait_ge(dve_step, steps[0])

                    def rsqrt(y, z, tmp):
                        link(V.tensor_scalar(tmp.bitcast(I32), z.bitcast(I32), 1, None, ALU.logical_shift_right))
                        link(V.tensor_scalar(y.bitcast(I32), tmp.bitcast(I32), -1.0, RSQRT_MAGIC, ALU.mult, ALU.add))
                        for _ in range(3):
                            link(V.tensor_tensor(tmp, y, y, ALU.mult))
                            link(V.scalar_tensor_tensor(out=tmp, in0=tmp, scalar=-0.5, in1=z, op0=ALU.mult, op1=ALU.mult))
                            link(V.scalar_tensor_tensor(out=y, in0=tmp, scalar=1.5, in1=y, op0=ALU.add, op1=ALU.mult))

                    def layernorm(src, done):
                        for c in range(TILES):
                            V.bn_stats(stats[:, c, 0:6], src[:, c, :]).then_inc(dve_step, 1)
                        steps[0] += TILES
                        dve.wait_ge(dve_step, steps[0])
                        for c in range(TILES):
                            V.bn_aggr(mv[:, c, :], stats[:, c, 0:6]).then_inc(dve_step, 1)
                        steps[0] += TILES
                        dve.wait_ge(dve_step, steps[0])
                        var, rstd, tmp = nw1[:, 0:TILES], nw1[:, 8:8 + TILES], nw1[:, 16:16 + TILES]
                        link(V.tensor_scalar(var, mv[:, :, 1], LN_EPS, None, ALU.add))
                        rsqrt(rstd, var, tmp)
                        for c in range(TILES):
                            last = V.tensor_scalar(xn[:, c, :], src[:, c, :], mv[:, c, 0:1], rstd[:, c:c + 1],
                                                   ALU.subtract, ALU.mult)
                        last.then_inc(done, 1)

                    dve.wait_ge(x_loaded, 16)
                    layernorm(xin, x_normed)
                    await_fill(dve, "ab", 0)
                    ab = bank("ab", 0)[:, 0:64].rearrange("p (c n) -> p c n", c=TILES)
                    lin = sm(2)[:, :, 0:HEADS]
                    link(V.tensor_tensor(lin, ab[:, :, 0:HEADS], over_heads(dt_row[:, :], TILES), ALU.add))
                    V.tensor_copy(ab_arg[:, :, HEADS:], ab[:, :, HEADS:])
                    V.scalar_tensor_tensor(out=ab_arg[:, :, 0:HEADS], in0=lin, scalar=-1.0, in1=lin, op0=ALU.mult,
                                           op1=ALU.max).then_inc(ab_args, 1)

                    def conv(i):
                        await_fill(dve, "qk", i)
                        dve.wait_ge(tap3_done, i + 1)
                        for d in range(1, TAPS):
                            for j in range(2):
                                blk = 2 * i + j
                                if d > 1:
                                    dve.wait_ge(conv_step, 5 * i + 2 * (d - 2) + j + 1)
                                ins = V.scalar_tensor_tensor(
                                    out=qkT[:, blk, d:], in0=bank("qk", i)[:, TOK * j:TOK * (j + 1) - d],
                                    scalar=taps[:, blk, TAPS - 1 - d:TAPS - d], in1=qkT[:, blk, d:], op0=ALU.mult, op1=ALU.add)
                                if d == TAPS - 1 and j == 1:
                                    ins.then_inc(conv_done, 1)
                                else:
                                    ins.then_inc(conv_step, 1)

                    conv(0)
                    conv(1)
                    dve.wait_ge(ab_exps, 1)
                    e_a, e_b = ab_exp[:, :, 0:HEADS], ab_exp[:, :, HEADS:]
                    t1, t2, t3 = (sm(i)[:, :, 0:HEADS] for i in (3, 4, 5))
                    tb = sm(3)[:, :, HEADS:]
                    link(V.tensor_scalar(tb, e_b, 1.0, None, ALU.add))
                    link(V.reciprocal(tb, tb))
                    link(V.tensor_scalar(beta_tok, tb, 2.0, None, ALU.mult))
                    link(V.tensor_scalar(t1, e_a, 2.0, None, ALU.add))
                    link(V.reciprocal(t1, t1))
                    link(V.tensor_tensor(t1, t1, e_a, ALU.mult))
                    link(V.tensor_tensor(t2, t1, t1, ALU.mult))
                    link(V.tensor_scalar(t3, t2, 1.0 / 17, None, ALU.mult))
                    for k in (15, 13, 11, 9, 7, 5, 3):
                        link(V.scalar_tensor_tensor(out=t3, in0=t3, scalar=1.0 / k, in1=t2, op0=ALU.add, op1=ALU.mult))
                    link(V.scalar_tensor_tensor(out=t3, in0=t3, scalar=1.0, in1=t1, op0=ALU.add, op1=ALU.mult))
                    link(V.tensor_scalar(lin, lin, 0.0, None, ALU.max))
                    link(V.scalar_tensor_tensor(out=t3, in0=t3, scalar=2.0, in1=lin, op0=ALU.mult, op1=ALU.add))
                    V.tensor_tensor(g_tok, t3, over_heads(decay_row[:, :], TILES), ALU.mult).then_inc(g_ready, 1)
                    for i in range(2, BLOCKS // 2):
                        conv(i)
                    await_fill(dve, "norms", 0)
                    V.tensor_scalar(z_qk, bank("norms", 0)[:, 0:64].rearrange("p (c n) -> p c n", c=TILES), L2_EPS, None,
                                    ALU.add).then_inc(norms_read, 1)
                    dve.wait_ge(norms_read, 1)
                    rsqrt(rs_qk, z_qk, sm(16))
                    zk, rk = z_qk[:, :, HEADS:], rs_qk[:, :, HEADS:]
                    link(V.tensor_tensor(m_tok, zk, rk, ALU.mult))
                    link(V.tensor_tensor(b_tok, rk, rk, ALU.mult))
                    V.tensor_tensor(b_tok, b_tok, beta_tok, ALU.mult).then_inc(b_ready, 1)
                    link(V.tensor_scalar(rs_qk[:, :, 0:HEADS], rs_qk[:, :, 0:HEADS], Q_SCALE, None, ALU.mult))
                    dve.wait_ge(gamma_ready, 1)
                    link(V.tensor_scalar(neg_gamma, gamma, -1.0, None, ALU.mult))
                    for g in range(GROUPS):
                        dve.wait_ge(decay_ready, g + 1)
                        dve.wait_ge(bm_ready, g + 1)
                        V.tensor_tensor(eb[:, g], eb[:, g], bm[g % 2], ALU.mult).then_inc(B_ready, 1)
                        await_fill(dve, "kk", g)
                        dve.wait_ge(B_ready, g + 1)
                        V.scalar_tensor_tensor(out=nt[:, g], in0=bank("kk", g)[:, :].rearrange("p (k t) -> p k t", k=4),
                                               scalar=-1.0, in1=eb[:, g], op0=ALU.mult, op1=ALU.mult).then_inc(nt_ready, 1)
                        if g < 4:
                            q, par = g // 2, g % 2
                            ks = kscale[:, 8 * q:8 * q + 8].rearrange("p (k two) -> p two k", two=2)[:, par]
                            V.tensor_copy(ks, eb[:, g, :, P - 1]).then_inc(kscale_ready, 1)
                    dve.wait_ge(kscale_ready, 4)
                    for g in range(GROUPS):
                        await_fill(dve, "qk_", g)
                        V.tensor_tensor(eb[:, g], bank("qk_", g)[:, :].rearrange("p (k t) -> p k t", k=4), eb[:, g],
                                        ALU.mult).then_inc(p_ready, 1)
                    for q in range(2):
                        await_fill(dve, "ktok", q)
                        V.tensor_tensor(ktok[:, 8 * q:8 * q + 8, :], bank("ktok", q)[:, :].rearrange("p (h d) -> p h d", h=8),
                                        over_cols(kscale[:, 8 * q:8 * q + 8], DK), ALU.mult).then_inc(ktok_ready, 1)

                    def as_halves(t):
                        return t.rearrange("p (i t) -> p i t", i=8)

                    for l, n in enumerate(LEVELS):
                        mask = con[:, C_YM + HALF * l:C_YM + HALF * (l + 1)]
                        for s in range(SUPERS):
                            await_fill(dve, "Y", n, s)
                            V.tensor_tensor(ymid[:, s], as_halves(bank("Y", n, s)[:, :]), over_heads(mask, 8),
                                            ALU.mult).then_inc(y_masked, 1)
                        for s in range(SUPERS):
                            await_fill(dve, "TY", n, s)
                            V.tensor_tensor(tinv[:, s], as_halves(bank("TY", n, s)[:, :]), tinv[:, s], ALU.add)\
                                .then_inc(t_ready, 1)
                            await_fill(dve, "WY", n, s)
                            if n < LEVELS[-1]:
                                V.tensor_tensor(winv[:, s], as_halves(bank("WY", n, s)[:, :]), winv[:, s], ALU.add)\
                                    .then_inc(w_ready, 1)
                            else:
                                for lo in (0, HALF):
                                    r = slice(lo, lo + HALF)
                                    last = V.tensor_tensor(
                                        nt[r, 2 * s:2 * s + 2, :, lo:lo + HALF].rearrange("p a k t -> p (a k) t"),
                                        as_halves(bank("WY", n, s)[r, :]), winv[r, s], ALU.add)
                                last.then_inc(w_ready, 1)
                    for g in range(4, 8):
                        await_fill(dve, "ks", g)
                        dve.wait_ge(r_ready, g + 1)
                        for k, h in enumerate(heads_of(g)):
                            last = V.scalar_tensor_tensor(out=vr[:, 1, h, :], in0=bank("ks", g)[:, k * P:(k + 1) * P],
                                                          scalar=neg_gamma[:, h:h + 1], in1=vr[:, 1, h, :],
                                                          op0=ALU.mult, op1=ALU.add)
                        last.then_inc(r1_ready, 1)

                    def factors(c):
                        a = rs_qk[:, c, 0:HEADS]
                        z, f = o_z[:, c, :], o_fac[:, c, :]
                        link(V.tensor_tensor(z, a, a, ALU.mult))
                        link(V.tensor_tensor(z, z, o_ssq[:, c, :], ALU.mult))
                        link(V.tensor_scalar(z, z, 1.0 / DV, RMS_EPS, ALU.mult, ALU.add))
                        rsqrt(f, z, nw2[:, 0:HEADS])
                        link(V.tensor_tensor(f, f, a, ALU.mult))

                    dve.wait_ge(o_squares, 4)
                    factors(0)
                    for g in range(4, 8):
                        await_fill(dve, "qs", g)
                        dve.wait_ge(o_copied, g + 1)
                        for k, h in enumerate(heads_of(g)):
                            last = V.scalar_tensor_tensor(out=vr[:, 1, h, :], in0=bank("qs", g)[:, k * P:(k + 1) * P],
                                                          scalar=gamma[:, h:h + 1], in1=vr[:, 1, h, :],
                                                          op0=ALU.mult, op1=ALU.add)
                        last.then_inc(o_ready, 1)
                    for g in range(GROUPS):
                        c, q = g // 4, (g % 4) // 2
                        if g == 4:
                            dve.wait_ge(o_squares, 8)
                            factors(1)
                        dve.wait_ge(sgate_ready, 4 * c + 2 * q + 2)
                        for h in heads_of(g):
                            last = V.scalar_tensor_tensor(out=vr[:, c, h, :], in0=vr[:, c, h, :], scalar=o_fac[:, c, h:h + 1],
                                                          in1=sgate[:, c, h, :], op0=ALU.mult, op1=ALU.mult)
                        last.then_inc(gated, 1)
                    for c in range(TILES):
                        await_fill(dve, "attn", c)
                        V.tensor_tensor(x2[:, c, :], bank("attn", c)[:, 0:P], xin[:, c, :], ALU.add).then_inc(x2_done, 1)
                    dve.wait_ge(x2_done, TILES)
                    layernorm(x2, x2_normed)
                    await_fill(dve, "route", 0)
                    logits = bank("route", 0)[:, 0:TILES * EXPERTS].rearrange("p (c e) -> p c e", c=TILES)

                    def row_max(dst, src):
                        link(V.tensor_reduce(out=dst, in_=src, axis=AX_X, op=ALU.max))

                    def row_sum(dst, src):
                        link(V.tensor_reduce(out=dst, in_=src, axis=AX_X, op=ALU.add))

                    row_max(rtmax, logits)
                    V.tensor_tensor(rt[0], logits, over_cols(rtmax, EXPERTS), ALU.subtract).then_inc(route_args, 1)
                    dve.wait_ge(route_exps, 1)
                    row_sum(rtsum, rt[1])
                    link(V.reciprocal(rtsum, rtsum))
                    link(V.tensor_tensor(rt[2], rt[1], over_cols(rtsum, EXPERTS), ALU.mult))

                    def pick(dst, scores):
                        row_max(rtmax, scores)
                        link(V.tensor_tensor(dst, scores, over_cols(rtmax, EXPERTS), ALU.is_equal))
                        link(V.tensor_tensor(dst, dst, over_heads(rank_row[:, :], TILES), ALU.mult))
                        row_max(rtmax, dst)
                        link(V.tensor_tensor(dst, dst, over_cols(rtmax, EXPERTS), ALU.is_equal))

                    pick(rt[3], rt[2])
                    link(V.scalar_tensor_tensor(out=rt[4], in0=rt[3], scalar=-2.0, in1=rt[2], op0=ALU.mult, op1=ALU.add))
                    pick(rt[5], rt[4])
                    link(V.tensor_tensor(rt[3], rt[3], rt[5], ALU.add))
                    link(V.tensor_tensor(rt[3], rt[3], rt[2], ALU.mult))
                    row_sum(rtsum, rt[3])
                    link(V.tensor_scalar(rtsum, rtsum, 1e-20, None, ALU.add))
                    link(V.reciprocal(rtsum, rtsum))
                    V.tensor_tensor(wexp[:, :, 0:EXPERTS], rt[3], over_cols(rtsum, EXPERTS), ALU.mult).then_inc(w_exp_ready, 1)
                    for u, (k, c) in enumerate(units):
                        await_fill(dve, "up2", k, c)
                        dve.wait_ge(sgw_ready, u + 1)
                        if u >= 2:
                            await_fill(dve, "zT", *units[u - 2])
                        V.tensor_tensor(zf[u % 2], bank("up2", k, c)[:, 0:UNIT], sgw[u % 2], ALU.mult).then_inc(z_ready, 1)
                    for c in range(TILES):
                        await_fill(dve, "down", c)
                        V.tensor_tensor(yo[:, c, :], bank("down", c)[:, 0:P], x2[:, c, :], ALU.add).then_inc(out_ready, 1)

                @block.gpsimd
                def _(pool):
                    G = nc.gpsimd
                    for i in range(BLOCKS // 2):
                        pool.wait_ge(qk_ready, i + 1)
                        G.tensor_tensor(sq[:, 2 * i:2 * i + 2, :], qkT[:, 2 * i:2 * i + 2, :], qkT[:, 2 * i:2 * i + 2, :],
                                        ALU.mult).then_inc(sq_ready, 1)
                    pool.wait_ge(g_ready, 1)
                    for g in range(GROUPS):
                        if g >= 2:
                            pool.wait_ge(decay_ready, g - 1)
                        G.tensor_tensor(gm[g % 2], over_heads(le_mask, 4), over_cols(by_group(g_tok, g), P),
                                        ALU.mult).then_inc(gm_ready, 1)
                    pool.wait_ge(b_ready, 1)
                    for g in range(GROUPS):
                        if g >= 2:
                            pool.wait_ge(B_ready, g - 1)
                        G.tensor_tensor(bm[g % 2], over_heads(le_mask, 4), over_cols(by_group(b_tok, g), P),
                                        ALU.mult).then_inc(bm_ready, 1)
                    for s in range(SUPERS):
                        pool.wait_ge(nt_ready, 2 * s + 2)
                        if s:
                            pool.wait_ge(w_ready, s)
                        else:
                            pool.wait_ge(bm_ready, GROUPS)
                        for lo in (0, HALF):
                            if lo:
                                pool.wait_ge(winit_part, 2 * s + 1)
                            r = slice(lo, lo + HALF)
                            src = nt[r, 2 * s:2 * s + 2, :, lo:lo + HALF].rearrange("p a k t -> p (a k) t")
                            G.tensor_tensor(winv[r, s], src, first_mask[r, :].unsqueeze(1).broadcast_to([HALF, 8, HALF]),
                                            ALU.mult).then_inc(winit_part, 1)
                        pool.wait_ge(winit_part, 2 * s + 2)
                        G.tensor_tensor(winv[:, s], winv[:, s], over_heads(i64, 8), ALU.add).then_inc(w_ready, 1)
                    for g in range(GROUPS):
                        c, q = g // 4, (g % 4) // 2
                        pool.wait_ge(v_ready, 4 * c + 2 * q + 2)
                        v = by_group(vr, g)
                        G.tensor_tensor(v, v, over_cols(by_group(m_tok, g), DV), ALU.mult).then_inc(r_ready, 1)
                    pool.wait_ge(w_exp_ready, 1)
                    for u, (k, c) in enumerate(units):
                        pool.wait_ge(sg_ready, u + 1)
                        if u >= 2:
                            pool.wait_ge(z_ready, u - 1)
                        G.tensor_tensor(sgw[u % 2].rearrange("p (e i) -> p e i", e=2),
                                        sgf[u % 2].rearrange("p (e i) -> p e i", e=2),
                                        over_cols(wexp[:, c, 2 * k:2 * k + 2], INTER), ALU.mult).then_inc(sgw_ready, 1)

            nc.all_engine_barrier()
            nums = sorted(s.num for s in loop_sems)
            assert nums == list(range(nums[0], nums[-1] + 1))
            nc.sync.sem_clear(range(nums[0], nums[-1] + 1))
            nc.all_engine_barrier()


def layout_constants():
    import numpy as np
    i = np.arange(P)[:, None]
    j = np.arange(P)[None, :]
    r, t = np.arange(P)[:, None] % HALF, np.arange(HALF)[None, :]
    parts = [i == j, i <= j, i > j, r == t, (r % 2 == 0) & (t == r + 1)]
    for n in LEVELS:
        parts.append((r // (2 * n) == t // (2 * n)) & (r // n % 2 == 1) & (t // n % 2 == 0))
    parts.append(i // HALF == np.arange(2)[None, :])
    return np.ascontiguousarray(np.concatenate([np.broadcast_to(p, (P, p.shape[1])) for p in parts], axis=1).astype(np.float32))


_INS = ["L0_attn_x", "L0_attn_w_q", "L0_attn_w_k", "L0_attn_w_v", "L0_attn_w_a", "L0_attn_w_b", "L0_attn_w_g",
        "L0_attn_w_out", "L0_attn_A_log", "L0_attn_dt_bias", "L0_attn_conv_q", "L0_attn_conv_k", "L0_attn_conv_v",
        "L0_attn_norm_w", "L0_ffn_gate_w", "L0_ffn_wg", "L0_ffn_wu", "L0_ffn_wd", "L0_ffn_swg", "L0_ffn_swu",
        "L0_ffn_swd"]


def kernel(**inputs):
    import numpy as np
    import concourse.bacc as bacc
    from concourse.bass_utils import run_bass_kernel_spmd

    nc = bacc.Bacc("TRN2", target_bir_lowering=False, num_devices=1)
    arrays, args = {}, []
    for name in _INS:
        a = np.ascontiguousarray(inputs[name])
        arrays[f"in_{name}"] = a
        args.append(nc.dram_tensor(f"in_{name}", a.shape, mybir.dt.from_np(a.dtype), kind="ExternalInput").ap())
    arrays["in_consts"] = layout_constants()
    args.append(nc.dram_tensor("in_consts", (P, C_END), F32, kind="ExternalInput").ap())
    args.append(nc.dram_tensor("out_x", inputs["L0_attn_x"].shape, F32, kind="ExternalOutput").ap())
    build_layer(nc, *args)
    r = run_bass_kernel_spmd(nc, [arrays], core_ids=[0])
    return r.results[0]["out_x"]
```

```python
from contextlib import ExitStack

import concourse.bass as bass
from concourse import mybir

F32 = mybir.dt.float32
I32 = mybir.dt.int32
ALU = mybir.AluOpType
ACT = mybir.ActivationFunctionType
AX_X = mybir.AxisListType.X

P = 128
HEADS = 16
DK = 64
DV = 128
TAPS = 4
TILES = 2
TOK = TILES * P
PAD = TAPS - 1
BLOCKS = 2 * HEADS * DK // P
QBLOCKS = BLOCKS // 2
GROUPS = 8
SUPERS = 4
HALF = P // 2
SUB = 16
SUBS = P // SUB
LEVELS = (16, 32)
EXPERTS = 8
INTER = 176
UNIT = 2 * INTER
CHUNKS = EXPERTS // 2 + 1
HID = CHUNKS * UNIT
RSQRT_MAGIC = float(0x5F3759DF)
LN_EPS = 1e-5
L2_EPS = 1e-6
RMS_EPS = 1e-5
Q_SCALE = DK ** -0.5

C_ID, C_LE, C_GT, C_YM = 0, 128, 256, 384
C_IND = C_YM + 64 * len(LEVELS)
C_SUB = C_IND + 4 * HEADS - 2
C_END = C_SUB + SUB * SUB


def build_layer(nc, x, w_q, w_k, w_v, w_a, w_b, w_g, w_out, A_log, dt_bias, conv_q, conv_k, conv_v,
                norm_w, gate_w, wg, wu, wd, swg, swu, swd, consts, out):
    batches = x.shape[0]

    with ExitStack() as ctx:
        def sb(name, shape, dt=F32):
            return ctx.enter_context(nc.sbuf_tensor(name, shape, dt))

        def sem(name):
            return ctx.enter_context(nc.semaphore(name))

        w_qk = sb("w_qk", [P, 2 * HEADS * DK])
        w_val = sb("w_val", [P, HEADS * DV])
        w_gate = sb("w_gate", [P, HEADS * DV])
        w_o = sb("w_o", [P, HEADS, P])
        w_ab = sb("w_ab", [P, 2 * HEADS])
        w_up1 = sb("w_up1", [P, HID])
        w_up2 = sb("w_up2", [P, HID])
        w_down = sb("w_down", [P, CHUNKS, 3, P])
        w_route = sb("w_route", [P, EXPERTS])
        taps = sb("taps", [P, BLOCKS + HEADS, TAPS])
        norm_col = sb("norm_col", [P, 1])
        dt_row = sb("dt_row", [P, HEADS])
        decay_row = sb("decay_row", [P, HEADS])
        con = sb("con", [P, C_END])
        rank_row = sb("rank_row", [P, EXPERTS])
        ident = con[:, C_ID:C_ID + P]
        le_mask = con[:, C_LE:C_LE + P]
        gt_mask = con[:, C_GT:C_GT + P]

        xin = sb("xin", [P, TILES, P])
        xn = sb("xn", [P, TILES, P])
        xT = sb("xT", [P, TOK])
        qkT = sb("qkT", [P, BLOCKS, TOK])
        eb = sb("eb", [P, GROUPS, 4, P])
        nt = sb("nt", [P, GROUPS, 4, P])
        tinv = sb("tinv", [P, SUPERS, 8, HALF])
        winv = sb("winv", [P, SUPERS, 8, HALF])
        ymid = sb("ymid", [P, SUPERS, 8, HALF])
        vr = sb("vr", [P, TILES, HEADS, DV])
        ysol = sb("ysol", [P, TILES, HEADS, DV])
        state = sb("state", [P, HEADS // 2, DV])
        ktok = sb("ktok", [P, HEADS, DK])
        kscale = sb("kscale", [P, HEADS])
        small = sb("small", [P, 26, 2 * 32])
        stats = sb("stats", [P, TILES, 8])
        mv = sb("mv", [P, TILES, 2])
        x2 = sb("x2", [P, TILES, P])
        xn2 = sb("xn2", [P, TILES, P])
        sgate = sb("sgate", [P, TILES, HEADS, DV])
        norm_rows = sb("norm_rows", [2 * HEADS, TOK])
        zbuf = sb("zbuf", [P, 2, UNIT])
        zTbuf = sb("zTbuf", [P, 2, 3 * P])
        hTbuf = sb("hTbuf", [P, TOK])

        flat_y = ysol[:, :, :, :].rearrange("p c h d -> p (c h d)")
        flat_v = vr[:, :, :, :].rearrange("p c h d -> p (c h d)")
        sq = nt[:, :, :, :].rearrange("p g k t -> p (g k t)").rearrange("p (j t) -> p j t", t=TOK)
        vT = flat_y.rearrange("p (j t) -> p j t", t=TOK)
        flat_ymid = ymid[:, :, :, :].rearrange("p s i t -> p (s i t)")
        gm = [flat_ymid[:, 512 * i:512 * (i + 1)].rearrange("p (h t) -> p h t", h=4) for i in range(2)]
        bm = [flat_ymid[:, 1024 + 512 * i:1024 + 512 * (i + 1)].rearrange("p (h t) -> p h t", h=4) for i in range(2)]
        oT = eb
        zf = [zbuf[:, i, :] for i in range(2)]
        zT = [zTbuf[:, i, :] for i in range(2)]
        hT = hTbuf[:, :]
        flat_state = state[:, :, :].rearrange("p j d -> p (j d)")
        flat_ktok = ktok[:, :, :].rearrange("p h d -> p (h d)")

        def sub_tile(t, i):
            return t[:, 512 * i:512 * (i + 1)].rearrange("p (q a b) -> p q a b", q=2, a=SUB)

        sub_n, sub_w = sub_tile(flat_state, 0), sub_tile(flat_state, 1)
        sub_t, sub_prod = sub_tile(flat_ktok, 0), flat_ktok[:, 512:1024]
        shape = (GROUPS * 4, SUBS, SUB, SUB)
        sub_in = nc.dram_tensor("sub_in", shape, F32, kind="Internal").ap()
        sub_out_w = nc.dram_tensor("sub_out_w", shape, F32, kind="Internal").ap()
        sub_out_t = nc.dram_tensor("sub_out_t", shape, F32, kind="Internal").ap()

        def by_partition(d):
            return d.rearrange("g b s t -> g (b s t)").rearrange("g (b n) -> (g b) n", b=4)\
                .rearrange("p (q s t) -> p q s t", q=2, s=SUB)

        def heads_of(g):
            q, par = (g % 4) // 2, g % 2
            return [8 * q + par + 2 * k for k in range(4)]

        def by_group(t, g):
            c, q, par = g // 4, (g % 4) // 2, g % 2
            v = t[:, c]
            v = v[:, 8 * q:8 * q + 8]
            if len(v.shape) == 3:
                return v.rearrange("p (k two) d -> p two k d", two=2)[:, par]
            return v.rearrange("p (k two) -> p two k", two=2)[:, par]

        def over_cols(v, n):
            return v.unsqueeze(2).broadcast_to([P, v.shape[1], n])

        def over_heads(v, n):
            return v.unsqueeze(1).broadcast_to([P, n, v.shape[1]])

        banks = [ctx.enter_context(nc.psum_tensor(f"bank{i}", [P, 512], F32)) for i in range(8)]
        units = [(k, c) for k in range(CHUNKS) for c in range(TILES)]
        def ffn_order():
            out_ = [("down", 0), ("down", 1)]
            for u in range(len(units) + 2):
                if u < len(units):
                    out_ += [("up1", *units[u]), ("up2", *units[u])]
                if 1 <= u <= len(units):
                    out_ += [("zT", *units[u - 1])]
            return out_

        def fill_order(attention, experts):
            if not attention:
                return [("hT", 0), ("route", 0)] + ffn_order()
            order = [("xT", 0), ("ab", 0)]
            order += [("qk", i) for i in range(BLOCKS // 2)]
            order += [("gate", i) for i in range(GROUPS)]
            order += [("gam", 0)] + [("decay", g) for g in range(GROUPS)]
            if experts:
                order += [("hT", 0), ("route", 0)]
            order += [("norms", 0), ("normsT", 0)]
            order += [("kk", g) for g in range(GROUPS)]
            order += [("v", i) for i in range(4)]
            order += [("qk_", g) for g in range(GROUPS)]
            order += [("v", i) for i in range(4, 8)]
            order += [("ktok", q) for q in range(2)]
            order += [("vt", i) for i in range(GROUPS)]
            if experts:
                order += ffn_order()
            for n in LEVELS:
                order += [("Y", n, s) for s in range(SUPERS)]
                order += [(k, n, s) for s in range(SUPERS) for k in ("TY", "WY")]
            order += [("Y64", s) for s in range(SUPERS)] + [("W64", s) for s in range(SUPERS)]
            order += [("y", g) for g in range(4)] + [("state", q) for q in range(2)]
            order += [("ks", g) for g in range(4, 8)]
            order += [("o", g) for g in range(4)]
            order += [("y", g) for g in range(4, 8)]
            order += [(k, g) for g in range(4, 8) for k in ("o", "qs")]
            order += [("oT", g) for g in range(4)] + [("attn", 0)]
            order += [("oT", g) for g in range(4, 8)] + [("attn", 1)]
            return order

        def assign(order):
            fill_at, before, last_in, turns, held = {}, {}, {}, [0] * 8, {}
            n = 0
            for key in order:
                while n % 8 in held:
                    n += 1
                b = n % 8
                n += 1
                fill_at[key] = (b, turns[b])
                turns[b] += 1
                if b in last_in:
                    before[key] = last_in[b]
                last_in[b] = key
                if key[0] == "down":
                    held[b] = key
                if key == ("zT", *units[-1]):
                    held = {}
            return fill_at, before

        fill_at, before = {}, {}

        bank_filled = [sem(f"bank_filled{i}") for i in range(8)]

        def bank(*key):
            return banks[fill_at[key][0]]

        def full(*key):
            return bank_filled[fill_at[key][0]]

        def await_fill(eng, *key):
            b, t = fill_at[key]
            eng.wait_ge(bank_filled[b], t + 1)

        x_loaded = sem("x_loaded")
        x_normed = sem("x_normed")
        xT_ready = sem("xT_ready")
        ab_args = sem("ab_args")
        ab_exps = sem("ab_exps")
        g_ready = sem("g_ready")
        tap3_done = sem("tap3_done")
        conv_done = sem("conv_done")
        qk_ready = sem("qk_ready")
        sq_ready = sem("sq_ready")
        v_ready = sem("v_ready")
        gm_ready = sem("gm_ready")
        gamma_ready = sem("gamma_ready")
        decay_ready = sem("decay_ready")
        b_ready = sem("b_ready")
        bm_ready = sem("bm_ready")
        B_ready = sem("B_ready")
        nt_ready = sem("nt_ready")
        w_ready = sem("w_ready")
        t_ready = sem("t_ready")
        y_masked = sem("y_masked")
        p_ready = sem("p_ready")
        kscale_ready = sem("kscale_ready")
        ktok_ready = sem("ktok_ready")
        y64_ready = sem("y64_ready")
        full_ready = sem("full_ready")
        r_ready = sem("r_ready")
        r1_ready = sem("r1_ready")
        v_tap3 = sem("v_tap3")
        v_conv_step = sem("v_conv_step")
        v_conv_done = sem("v_conv_done")
        vT_ready = sem("vT_ready")
        norm_copied = sem("norm_copied")
        sub_stored = sem("sub_stored")
        sub_loaded = sem("sub_loaded")
        sub_solved = sem("sub_solved")
        inv_stored = sem("inv_stored")
        inv_loaded = sem("inv_loaded")
        inv_zeroed = sem("inv_zeroed")
        y_ready = sem("y_ready")
        state_ready = sem("state_ready")
        o_copied = sem("o_copied")
        o_ready = sem("o_ready")
        o_squares = sem("o_squares")
        sgate_ready = sem("sgate_ready")
        gated = sem("gated")
        oT_ready = sem("oT_ready")
        x2_normed = sem("x2_normed")
        hT_ready = sem("hT_ready")
        route_args = sem("route_args")
        route_exps = sem("route_exps")
        w_exp_ready = sem("w_exp_ready")
        sg_ready = sem("sg_ready")
        sgw_ready = sem("sgw_ready")
        z_ready = sem("z_ready")
        zT_ready = sem("zT_ready")
        out_ready = sem("out_ready")
        out_stored = sem("out_stored")
        dve_step = sem("dve_step")
        conv_step = sem("conv_step")
        norms_read = sem("norms_read")
        x2_done = sem("x2_done")
        zT_used = sem("zT_used")
        w_part = sem("w_part")
        loop_sems = bank_filled + [
            v_tap3, v_conv_step, v_conv_done, vT_ready, norm_copied, sub_stored, sub_loaded, sub_solved,
            inv_stored, inv_loaded, inv_zeroed, conv_step, norms_read, x2_done, zT_used, w_part, x_loaded, x_normed, xT_ready, ab_args, ab_exps, g_ready, tap3_done, conv_done, qk_ready, sq_ready,
            v_ready, gm_ready, gamma_ready, decay_ready, b_ready, bm_ready, B_ready, nt_ready,
            w_ready, t_ready, y_masked, p_ready, kscale_ready, ktok_ready, y64_ready, full_ready, r_ready, r1_ready,
            y_ready, state_ready, o_copied, o_ready, o_squares, sgate_ready, gated, oT_ready, x2_normed, hT_ready,
            route_args, route_exps, w_exp_ready, sg_ready, sgw_ready, z_ready, zT_ready, out_ready, out_stored,
            dve_step]
        weights_in = sem("weights_in")
        raw_in = sem("raw_in")
        prep_done = sem("prep_done")

        def level(n):
            return LEVELS.index(n)

        read_by = {
            "xT": lambda i: (xT_ready, 1), "ab": lambda i: (ab_args, 1), "qk": lambda i: (conv_done, i + 1),
            "v": lambda i: (v_conv_done, i + 1), "vt": lambda i: (v_ready, i + 1), "gam": lambda i: (gamma_ready, 1), "decay": lambda g: (decay_ready, g + 1),
            "norms": lambda i: (norm_copied, 1), "normsT": lambda i: (norms_read, 1), "kk": lambda g: (nt_ready, g + 1),
            "qk_": lambda g: (p_ready, g + 1), "ktok": lambda q: (ktok_ready, q + 1),
            "Y": lambda n, s: (y_masked, SUPERS * level(n) + s + 1),
            "TY": lambda n, s: (t_ready, SUPERS * level(n) + s + 1),
            "WY": lambda n, s: (w_ready, SUPERS * level(n) + s + 1),
            "Y64": lambda s: (y64_ready, s + 1), "W64": lambda s: (full_ready, s + 1),
            "y": lambda g: (y_ready, g + 1), "state": lambda q: (state_ready, q + 1), "o": lambda g: (o_copied, g + 1),
            "ks": lambda g: (r1_ready, g - 3), "qs": lambda g: (o_ready, g - 3), "gate": lambda i: (sgate_ready, i + 1),
            "oT": lambda g: (oT_ready, g + 1), "attn": lambda c: (x2_done, c + 1), "hT": lambda i: (hT_ready, 1),
            "route": lambda i: (route_args, 1), "down": lambda c: (out_ready, c + 1),
            "up1": lambda k, c: (sg_ready, TILES * k + c + 1), "up2": lambda k, c: (z_ready, TILES * k + c + 1),
            "zT": lambda k, c: (zT_ready, TILES * k + c + 1),
        }

        def claim(pe, *key):
            if key in before:
                what, *at = before[key]
                pe.wait_ge(*read_by[what](*at))

        def sm(i, n=32):
            return small[:, i, 0:TILES * n].rearrange("p (c n) -> p c n", c=TILES)

        ab_arg, ab_exp, abt1, abt2, abt3, abt4 = (sm(i) for i in range(6))
        g_tok, beta_tok, m_tok, b_tok = (sm(6 + i, HEADS) for i in range(4))
        z_qk, rs_qk = sm(10), sm(11)
        gamma = small[:, 12, 0:HEADS]
        neg_gamma = small[:, 12, HEADS:2 * HEADS]
        o_ssq, o_fac, o_z = sm(13, HEADS), sm(14, HEADS), sm(15, HEADS)
        nw1, nw2 = small[:, 16, :], small[:, 17, :]
        rt = [sm(18 + i, EXPERTS) for i in range(7)]
        rtmax = small[:, 25, 0:2]
        rtsum = small[:, 25, 2:4]
        wexp = sb("wexp", [P, TILES, EXPERTS + 2])

        with nc.Block() as block:
            @block.sync
            def _(sp):
                loads = [
                    (w_qk[:, 0:HEADS * DK], w_q), (w_qk[:, HEADS * DK:], w_k), (w_gate[:, :], w_g),
                    (w_ab[:, 0:HEADS], w_a), (w_ab[:, HEADS:], w_b),
                    (taps[:, 0:QBLOCKS, :], conv_q.rearrange("(j p) w -> p j w", p=P)),
                    (taps[:, QBLOCKS:BLOCKS, :], conv_k.rearrange("(j p) w -> p j w", p=P)),
                    (w_val[:, :], w_v), (taps[:, BLOCKS:, :], conv_v.rearrange("(j p) w -> p j w", p=P)),
                    (dt_row[:, :], dt_bias.partition_broadcast(P)),
                    (w_up1[:, 0:EXPERTS * INTER].rearrange("p (e i) -> p e i", e=EXPERTS), wg.rearrange("e h i -> h e i")),
                    (w_up2[:, 0:EXPERTS * INTER].rearrange("p (e i) -> p e i", e=EXPERTS), wu.rearrange("e h i -> h e i")),
                    (w_up1[:, EXPERTS * INTER:], swg), (w_up2[:, EXPERTS * INTER:], swu),
                    (con[:, :], consts),
                    (w_route[:, :], gate_w.rearrange("e h -> h e")),
                ]
                flat_wd = wd.rearrange("e i h -> (e i) h")
                for k in range(CHUNKS):
                    src = flat_wd[UNIT * k:UNIT * (k + 1), :] if k < CHUNKS - 1 else swd
                    loads.append((w_down[:, k, 0:2, :], src[0:2 * P, :].rearrange("(j p) h -> p j h", p=P)))
                    loads.append((w_down[0:UNIT - 2 * P, k, 2, :], src[2 * P:UNIT, :]))
                with nc.allow_non_contiguous_dma(reason="the router's weights are small"):
                    for dst, src in loads:
                        sp.dma_start(dst, src).then_inc(weights_in, 16)
                sp.wait_ge(weights_in, 16 * len(loads))

            @block.scalar
            def _(act):
                raw = [
                    (w_o[:, :, :], w_out.rearrange("(h d) n -> d h n", d=DV)),
                    (norm_col[:, :], norm_w.rearrange("(d one) -> d one", one=1)),
                    (decay_row[:, :], A_log.partition_broadcast(P)),
                ]
                for dst, src in raw:
                    act.dma_start(dst, src).then_inc(raw_in, 16)
                act.wait_ge(raw_in, 16 * len(raw))
                nc.scalar.activation(decay_row[:, :], decay_row[:, :], ACT.Exp).then_inc(prep_done, 1)

            @block.vector
            def _(dve):
                nc.vector.memset(wexp[:, :, EXPERTS:EXPERTS + 2], 1.0)
                for e in range(EXPERTS):
                    nc.vector.memset(rank_row[:, e:e + 1], float(EXPERTS - e))
                dve.wait_ge(raw_in, 16 * 3)
                nc.vector.tensor_scalar(w_o[:, :, :], w_o[:, :, :], norm_col[:, 0:1], None, ALU.mult)
                dve.wait_ge(prep_done, 1)
                nc.vector.tensor_scalar(decay_row[:, :], decay_row[:, :], -1.0, None, ALU.mult)

        def turn_of(b_in, b_out):
            attention, experts = b_in is not None, b_out is not None
            order = fill_order(attention, experts)
            found = assign(order)
            fill_at.clear()
            fill_at.update(found[0])
            before.clear()
            before.update(found[1])

            def tiles_of_seq(t, b):
                at = slice(b, b + 1) if isinstance(b, int) else bass.ds(b, 1)
                return t[at, :, :].rearrange("o (c p) d -> p (o c) d", p=P)

            with nc.Block() as block:
                @block.sync
                def _(sp):
                    if attention:
                        sp.dma_start(xin[:, :, :], tiles_of_seq(x, b_in)).then_inc(x_loaded, 16)
                        sp.wait_ge(nt_ready, GROUPS)
                        n_rows = nt[:, :, :, :].rearrange("p g k t -> p (g k) t")
                        for k in range(SUBS):
                            rows = slice(SUB * k, SUB * (k + 1))
                            sp.dma_start(sub_in[:, k].rearrange("g s t -> s g t"), n_rows[rows, :, rows]).then_inc(sub_stored, 16)
                        sp.wait_ge(sub_stored, 16 * SUBS)
                        sp.dma_start(sub_n, by_partition(sub_in)).then_inc(sub_loaded, 16)
                        sp.wait_ge(sub_solved, 1)
                        sp.dma_start(by_partition(sub_out_w), sub_w).then_inc(inv_stored, 16)
                        sp.wait_ge(sub_solved, 2)
                        sp.dma_start(by_partition(sub_out_t), sub_t).then_inc(inv_stored, 16)
                        sp.wait_ge(inv_stored, 32)
                        sp.wait_ge(inv_zeroed, 2)
                        for src, dst in ((sub_out_t, tinv), (sub_out_w, winv)):
                            dst = dst[:, :, :, :].rearrange("p s i t -> p (s i) t")
                            for k in range(SUBS):
                                rows = slice(SUB * k, SUB * (k + 1))
                                cols = slice(SUB * k % HALF, SUB * k % HALF + SUB)
                                sp.dma_start(dst[rows, :, cols], src[:, k].rearrange("g s t -> s g t")).then_inc(inv_loaded, 16)
                    if experts:
                        sp.wait_ge(out_ready, TILES)
                        sp.dma_start(tiles_of_seq(out, b_out), xn2[:, :, :]).then_inc(out_stored, 16)
                        sp.wait_ge(out_stored, 16)

                @block.tensor
                def _(pe):
                    T = nc.tensor

                    def mm(o, l, r, start=True, stop=True):
                        return T.matmul(o, l, r, start=start, stop=stop)

                    def experts_input():
                        claim(pe, "hT", 0)
                        pe.wait_ge(x2_normed, 1)
                        for c in range(TILES):
                            last = T.transpose(bank("hT", 0)[:, c * P:(c + 1) * P], xn2[:, c, :], ident)
                        last.then_inc(full("hT", 0), 1)
                        claim(pe, "route", 0)
                        pe.wait_ge(hT_ready, 1)
                        for c in range(TILES):
                            last = mm(bank("route", 0)[:, EXPERTS * c:EXPERTS * (c + 1)], hT[:, c * P:(c + 1) * P], w_route[:, :])
                        last.then_inc(full("route", 0), 1)

                    def up(u):
                        k, c = units[u]
                        for what, w in (("up1", w_up1), ("up2", w_up2)):
                            claim(pe, what, k, c)
                            mm(bank(what, k, c)[:, 0:UNIT], hT[:, c * P:(c + 1) * P],
                               w[:, UNIT * k:UNIT * (k + 1)]).then_inc(full(what, k, c), 1)

                    def flip(u):
                        k, c = units[u]
                        claim(pe, "zT", k, c)
                        pe.wait_ge(z_ready, u + 1)
                        for j in range(3):
                            w = min(P, UNIT - j * P)
                            last = T.transpose(bank("zT", k, c)[0:w, j * P:(j + 1) * P], zf[u % 2][:, j * P:j * P + w], ident)
                        last.then_inc(full("zT", k, c), 1)

                    def down(u):
                        k, c = units[u]
                        pe.wait_ge(zT_ready, u + 1)
                        for j in range(3):
                            w = min(P, UNIT - j * P)
                            last = mm(bank("down", c)[:, 0:P], zT[u % 2][0:w, j * P:(j + 1) * P], w_down[0:w, k, j, :],
                                      start=(k == 0 and j == 0), stop=(k == CHUNKS - 1 and j == 2))
                        if k == CHUNKS - 1:
                            last.then_inc(full("down", c), 1)
                        else:
                            last.then_inc(zT_used, 1)

                    def expert_units():
                        claim(pe, "down", 0)
                        claim(pe, "down", 1)
                        for u in range(len(units) + 2):
                            if u < len(units):
                                up(u)
                            if 1 <= u <= len(units):
                                flip(u - 1)
                            if u >= 2:
                                down(u - 2)

                    if not attention:
                        experts_input()
                        expert_units()
                        return

                    claim(pe, "xT", 0)
                    pe.wait_ge(x_normed, 1)
                    for c in range(TILES):
                        last = T.transpose(bank("xT", 0)[:, c * P:(c + 1) * P], xn[:, c, :], ident)
                    last.then_inc(full("xT", 0), 1)
                    claim(pe, "ab", 0)
                    pe.wait_ge(xT_ready, 1)
                    for c in range(TILES):
                        last = mm(bank("ab", 0)[:, 32 * c:32 * (c + 1)], xT[:, c * P:(c + 1) * P], w_ab[:, :])
                    last.then_inc(full("ab", 0), 1)

                    def project(what, i, w):
                        claim(pe, what, i)
                        for j in range(2):
                            last = mm(bank(what, i)[:, TOK * j:TOK * (j + 1)], w[:, (2 * i + j) * P:(2 * i + j + 1) * P], xT[:, :])
                        last.then_inc(full(what, i), 1)

                    for i in range(BLOCKS // 2):
                        project("qk", i, w_qk)
                    for i in range(GROUPS):
                        c, n = i // 4, i % 4
                        claim(pe, "gate", i)
                        mm(bank("gate", i)[:, :], xT[:, c * P:(c + 1) * P],
                           w_gate[:, 512 * n:512 * (n + 1)]).then_inc(full("gate", i), 1)
                    claim(pe, "gam", 0)
                    pe.wait_ge(g_ready, 1)
                    mm(bank("gam", 0)[:, 0:HEADS], le_mask, g_tok[:, 1, :]).then_inc(full("gam", 0), 1)
                    for g in range(GROUPS):
                        claim(pe, "decay", g)
                        pe.wait_ge(gm_ready, g + 1)
                        mm(bank("decay", g)[:, :], gt_mask, gm[g % 2].rearrange("p h t -> p (h t)")).then_inc(full("decay", g), 1)
                    if experts:
                        experts_input()
                    claim(pe, "norms", 0)
                    for j in range(BLOCKS):
                        pe.wait_ge(sq_ready, j // 2 + 1)
                        at = C_IND + 2 * HEADS - 2 - 2 * j
                        last = mm(bank("norms", 0)[0:2 * HEADS, 0:TOK], con[:, at:at + 2 * HEADS], sq[:, j, :],
                                  start=(j == 0), stop=(j == BLOCKS - 1))
                    last.then_inc(full("norms", 0), 1)
                    claim(pe, "normsT", 0)
                    pe.wait_ge(norm_copied, 1)
                    for c in range(TILES):
                        last = T.transpose(bank("normsT", 0)[:, 32 * c:32 * (c + 1)], norm_rows[:, c * P:(c + 1) * P],
                                           con[0:2 * HEADS, C_ID:C_ID + 2 * HEADS])
                    last.then_inc(full("normsT", 0), 1)

                    def head_T(h, c, block0):
                        po = DK * (h % 2)
                        return qkT[po:po + DK, block0 + h // 2, c * P:(c + 1) * P]

                    for g in range(GROUPS):
                        claim(pe, "kk", g)
                        pe.wait_ge(qk_ready, BLOCKS // 2)
                        for k, h in enumerate(heads_of(g)):
                            kT = head_T(h, g // 4, QBLOCKS)
                            last = mm(bank("kk", g)[:, k * P:(k + 1) * P], kT, kT)
                        last.then_inc(full("kk", g), 1)
                    for i in range(4):
                        project("v", i, w_val)
                    for g in range(GROUPS):
                        claim(pe, "qk_", g)
                        for k, h in enumerate(heads_of(g)):
                            last = mm(bank("qk_", g)[:, k * P:(k + 1) * P], head_T(h, g // 4, QBLOCKS), head_T(h, g // 4, 0))
                        last.then_inc(full("qk_", g), 1)
                    for i in range(4, 8):
                        project("v", i, w_val)
                    for q in range(2):
                        claim(pe, "ktok", q)
                        for j in range(4):
                            last = T.transpose(bank("ktok", q)[:, j * P:(j + 1) * P], qkT[:, QBLOCKS + 4 * q + j, 0:P], ident)
                        last.then_inc(full("ktok", q), 1)
                    for i in range(GROUPS):
                        c, n = i // 4, i % 4
                        claim(pe, "vt", i)
                        pe.wait_ge(vT_ready, 2 * n + 2)
                        for k in range(4):
                            last = T.transpose(bank("vt", i)[:, k * P:(k + 1) * P], vT[:, 4 * n + k, c * P:(c + 1) * P], ident)
                        last.then_inc(full("vt", i), 1)
                    if experts:
                        expert_units()
                    for l, n in enumerate(LEVELS):
                        for s in range(SUPERS):
                            claim(pe, "Y", n, s)
                            if l == 0:
                                pe.wait_ge(inv_loaded, 16 * 2 * SUBS)
                            else:
                                pe.wait_ge(t_ready, SUPERS * (l - 1) + s + 1)
                            for i in range(8):
                                for lo in (0, HALF):
                                    r = slice(lo, lo + HALF)
                                    last = mm(bank("Y", n, s)[r, HALF * i:HALF * (i + 1)],
                                              nt[r, 2 * s + i // 4, i % 4, lo:lo + HALF], tinv[r, s, i, :])
                            last.then_inc(full("Y", n, s), 1)
                        for s in range(SUPERS):
                            claim(pe, "TY", n, s)
                            pe.wait_ge(y_masked, SUPERS * l + s + 1)
                            if l:
                                pe.wait_ge(w_ready, SUPERS * (l - 1) + s + 1)
                            for i in range(8):
                                for lo in (0, HALF):
                                    r = slice(lo, lo + HALF)
                                    last = mm(bank("TY", n, s)[r, HALF * i:HALF * (i + 1)], winv[r, s, i, :], ymid[r, s, i, :])
                            last.then_inc(full("TY", n, s), 1)
                            claim(pe, "WY", n, s)
                            for i in range(8):
                                for lo in (0, HALF):
                                    r = slice(lo, lo + HALF)
                                    last = mm(bank("WY", n, s)[r, HALF * i:HALF * (i + 1)], ymid[r, s, i, :], winv[r, s, i, :])
                            last.then_inc(full("WY", n, s), 1)
                    hi, lo_ = slice(HALF, P), slice(0, HALF)
                    done = SUPERS * (len(LEVELS) - 1)
                    for s in range(SUPERS):
                        claim(pe, "Y64", s)
                        pe.wait_ge(t_ready, done + s + 1)
                        for i in range(8):
                            last = mm(bank("Y64", s)[hi, HALF * i:HALF * (i + 1)], nt[lo_, 2 * s + i // 4, i % 4, hi], tinv[lo_, s, i, :])
                        last.then_inc(full("Y64", s), 1)
                    for s in range(SUPERS):
                        claim(pe, "W64", s)
                        pe.wait_ge(y64_ready, s + 1)
                        pe.wait_ge(w_ready, done + s + 1)
                        for i in range(8):
                            last = mm(bank("W64", s)[lo_, HALF * i:HALF * (i + 1)], ymid[hi, s, i, :], nt[hi, 2 * s + i // 4, i % 4, hi])
                        last.then_inc(full("W64", s), 1)

                    def solve(g):
                        c, q = g // 4, (g % 4) // 2
                        claim(pe, "y", g)
                        pe.wait_ge(full_ready, g // 2 + 1)
                        if c == 0:
                            pe.wait_ge(r_ready, 2 * q + 2)
                        else:
                            pe.wait_ge(r1_ready, g - 3)
                        for k, h in enumerate(heads_of(g)):
                            last = mm(bank("y", g)[:, k * P:(k + 1) * P], nt[:, g, k, :], vr[:, c, h, :])
                        last.then_inc(full("y", g), 1)

                    def attend(g):
                        claim(pe, "o", g)
                        pe.wait_ge(p_ready, g + 1)
                        pe.wait_ge(y_ready, g + 1)
                        for k, h in enumerate(heads_of(g)):
                            last = mm(bank("o", g)[:, k * P:(k + 1) * P], eb[:, g, k, :], ysol[:, g // 4, h, :])
                        last.then_inc(full("o", g), 1)

                    def read_state(what, g, block0):
                        claim(pe, what, g)
                        pe.wait_ge(state_ready, (g - 4) // 2 + 1)
                        for k, h in enumerate(heads_of(g)):
                            po = DK * (h % 2)
                            last = mm(bank(what, g)[:, k * P:(k + 1) * P], head_T(h, 1, block0), state[po:po + DK, h // 2, :])
                        last.then_inc(full(what, g), 1)

                    for g in range(4):
                        solve(g)
                    for q in range(2):
                        claim(pe, "state", q)
                        pe.wait_ge(ktok_ready, q + 1)
                        pe.wait_ge(y_ready, 2 * q + 2)
                        for h in range(8 * q, 8 * q + 8):
                            po, j = DK * (h % 2), (h % 8) // 2
                            last = mm(bank("state", q)[po:po + DK, j * DV:(j + 1) * DV], ktok[:, h, :], ysol[:, 0, h, :])
                        last.then_inc(full("state", q), 1)
                    for g in range(4, 8):
                        read_state("ks", g, QBLOCKS)
                    for g in range(4):
                        attend(g)
                    for g in range(4, 8):
                        solve(g)
                    for g in range(4, 8):
                        attend(g)
                        read_state("qs", g, 0)
                    for c in range(TILES):
                        for g in range(4 * c, 4 * c + 4):
                            claim(pe, "oT", g)
                            pe.wait_ge(gated, g + 1)
                            for k, h in enumerate(heads_of(g)):
                                last = T.transpose(bank("oT", g)[:, k * P:(k + 1) * P], vr[:, c, h, :], ident)
                            last.then_inc(full("oT", g), 1)
                        claim(pe, "attn", c)
                        for g in range(4 * c, 4 * c + 4):
                            pe.wait_ge(oT_ready, g + 1)
                            for k, h in enumerate(heads_of(g)):
                                last = mm(bank("attn", c)[:, 0:P], oT[:, g, k, :], w_o[:, h, :],
                                          start=(g % 4 == 0 and k == 0), stop=(g % 4 == 3 and k == 3))
                        last.then_inc(full("attn", c), 1)

                @block.scalar
                def _(act):
                    A = nc.scalar

                    def copy_hT():
                        await_fill(act, "hT", 0)
                        A.activation(hT, bank("hT", 0)[:, 0:TOK], ACT.Copy).then_inc(hT_ready, 1)

                    def route_exp():
                        act.wait_ge(route_args, 1)
                        A.activation(rt[1], rt[0], ACT.Exp).then_inc(route_exps, 1)

                    def expert_units():
                        for u in range(len(units) + 1):
                            if u < len(units):
                                k, c = units[u]
                                await_fill(act, "up1", k, c)
                                if u >= 2:
                                    await_fill(act, "zT", *units[u - 2])
                                A.activation(zf[u % 2], bank("up1", k, c)[:, 0:UNIT], ACT.Silu).then_inc(sg_ready, 1)
                            if u >= 1:
                                k, c = units[u - 1]
                                await_fill(act, "zT", k, c)
                                if u - 1 >= 2:
                                    act.wait_ge(zT_used, u - 2)
                                A.activation(zT[(u - 1) % 2][:, 0:2 * P], bank("zT", k, c)[:, 0:2 * P], ACT.Copy)
                                w = UNIT - 2 * P
                                A.activation(zT[(u - 1) % 2][0:w, 2 * P:3 * P], bank("zT", k, c)[0:w, 2 * P:3 * P],
                                             ACT.Copy).then_inc(zT_ready, 1)

                    if not attention:
                        copy_hT()
                        route_exp()
                        expert_units()
                        return

                    await_fill(act, "xT", 0)
                    A.activation(xT[:, :], bank("xT", 0)[:, 0:TOK], ACT.Copy).then_inc(xT_ready, 1)
                    act.wait_ge(ab_args, 1)
                    A.activation(ab_exp, ab_arg, ACT.Exp, scale=-1.0).then_inc(ab_exps, 1)

                    def newest_tap(what, i, dst, first_block, done):
                        await_fill(act, what, i)
                        for j in range(2):
                            last = A.activation(dst[:, 2 * i + j, :], bank(what, i)[:, TOK * j:TOK * (j + 1)], ACT.Copy,
                                                scale=taps[:, first_block + 2 * i + j, TAPS - 1:TAPS])
                        last.then_inc(done, 1)

                    for i in range(BLOCKS // 2):
                        newest_tap("qk", i, qkT, 0, tap3_done)
                    for i in range(GROUPS):
                        act.wait_ge(conv_done, i + 1)
                        v = qkT[:, 2 * i:2 * i + 2, :]
                        A.activation(v, v, ACT.Silu).then_inc(qk_ready, 1)
                        c, n = i // 4, i % 4
                        await_fill(act, "gate", i)
                        A.activation(sgate[:, c, 4 * n:4 * n + 4, :].rearrange("p h d -> p (h d)"), bank("gate", i)[:, :],
                                     ACT.Silu).then_inc(sgate_ready, 1)
                    await_fill(act, "gam", 0)
                    A.activation(gamma, bank("gam", 0)[:, 0:HEADS], ACT.Exp).then_inc(gamma_ready, 1)
                    for g in range(GROUPS):
                        await_fill(act, "decay", g)
                        A.activation(eb[:, g, :, :].rearrange("p k t -> p (k t)"), bank("decay", g)[:, :],
                                     ACT.Exp).then_inc(decay_ready, 1)
                    if experts:
                        copy_hT()
                    await_fill(act, "norms", 0)
                    A.activation(norm_rows[:, :], bank("norms", 0)[0:2 * HEADS, 0:TOK], ACT.Copy).then_inc(norm_copied, 1)
                    if experts:
                        route_exp()
                    for lot in (range(4), range(4, 8)):
                        for i in lot:
                            newest_tap("v", i, vT, BLOCKS, v_tap3)
                        for i in lot:
                            act.wait_ge(v_conv_done, i + 1)
                            v = vT[:, 2 * i:2 * i + 2, :]
                            A.activation(v, v, ACT.Silu).then_inc(vT_ready, 1)
                    for i in range(GROUPS):
                        c, n = i // 4, i % 4
                        await_fill(act, "vt", i)
                        A.activation(vr[:, c, 4 * n:4 * n + 4, :].rearrange("p h d -> p (h d)"), bank("vt", i)[:, :],
                                     ACT.Copy).then_inc(v_ready, 1)
                    if experts:
                        expert_units()
                    for s in range(SUPERS):
                        await_fill(act, "Y64", s)
                        A.activation(ymid[HALF:P, s, :, :].rearrange("p i t -> p (i t)"), bank("Y64", s)[HALF:P, :],
                                     ACT.Copy).then_inc(y64_ready, 1)
                    for s in range(SUPERS):
                        await_fill(act, "W64", s)
                        A.activation(nt[0:HALF, 2 * s:2 * s + 2, :, HALF:P].rearrange("p a k t -> p (a k) t"),
                                     bank("W64", s)[0:HALF, :].rearrange("p (i t) -> p i t", i=8),
                                     ACT.Copy).then_inc(full_ready, 1)

                    def copy_y(g):
                        await_fill(act, "y", g)
                        A.activation(by_group(ysol, g), bank("y", g)[:, :].rearrange("p (k d) -> p k d", k=4),
                                     ACT.Copy).then_inc(y_ready, 1)

                    def copy_o(g):
                        await_fill(act, "o", g)
                        A.activation(by_group(vr, g), bank("o", g)[:, :].rearrange("p (k d) -> p k d", k=4),
                                     ACT.Copy).then_inc(o_copied, 1)

                    def squares(g):
                        scratch = (winv if g < 4 else tinv)[:, g % 4].rearrange("p i t -> p (i t)")
                        for k, h in enumerate(heads_of(g)):
                            last = A.activation(scratch[:, k * DV:(k + 1) * DV], vr[:, g // 4, h, :], ACT.Square,
                                                accum_out=o_ssq[:, g // 4, h:h + 1])
                        last.then_inc(o_squares, 1)

                    for g in range(4):
                        copy_y(g)
                    for q in range(2):
                        await_fill(act, "state", q)
                        A.activation(state[:, 4 * q:4 * q + 4, :].rearrange("p j d -> p (j d)"), bank("state", q)[:, :],
                                     ACT.Copy).then_inc(state_ready, 1)
                    for g in range(4):
                        copy_o(g)
                    for g in range(4):
                        act.wait_ge(o_copied, g + 1)
                        squares(g)
                    for g in range(4, 8):
                        copy_y(g)
                    for g in range(4, 8):
                        copy_o(g)

                    def copy_oT(g):
                        await_fill(act, "oT", g)
                        A.activation(oT[:, g, :, :].rearrange("p k t -> p (k t)"), bank("oT", g)[:, :],
                                     ACT.Copy).then_inc(oT_ready, 1)

                    for g in range(4, 8):
                        act.wait_ge(o_ready, g - 3)
                        squares(g)
                    for g in range(GROUPS):
                        copy_oT(g)

                @block.vector
                def _(dve):
                    V = nc.vector
                    steps = [0]

                    def link(ins):
                        steps[0] += 1
                        ins.then_inc(dve_step, 1)
                        dve.wait_ge(dve_step, steps[0])

                    def rsqrt(y, z, tmp):
                        link(V.tensor_scalar(tmp.bitcast(I32), z.bitcast(I32), 1, None, ALU.logical_shift_right))
                        link(V.tensor_scalar(y.bitcast(I32), tmp.bitcast(I32), -1.0, RSQRT_MAGIC, ALU.mult, ALU.add))
                        for _ in range(3):
                            link(V.tensor_tensor(tmp, y, y, ALU.mult))
                            link(V.scalar_tensor_tensor(out=tmp, in0=tmp, scalar=-0.5, in1=z, op0=ALU.mult, op1=ALU.mult))
                            link(V.scalar_tensor_tensor(out=y, in0=tmp, scalar=1.5, in1=y, op0=ALU.add, op1=ALU.mult))

                    def layernorm(src, dst, done):
                        for c in range(TILES):
                            V.bn_stats(stats[:, c, 0:6], src[:, c, :]).then_inc(dve_step, 1)
                        steps[0] += TILES
                        dve.wait_ge(dve_step, steps[0])
                        for c in range(TILES):
                            V.bn_aggr(mv[:, c, :], stats[:, c, 0:6]).then_inc(dve_step, 1)
                        steps[0] += TILES
                        dve.wait_ge(dve_step, steps[0])
                        var, rstd, tmp = nw1[:, 0:TILES], nw1[:, 8:8 + TILES], nw1[:, 16:16 + TILES]
                        link(V.tensor_scalar(var, mv[:, :, 1], LN_EPS, None, ALU.add))
                        rsqrt(rstd, var, tmp)
                        for c in range(TILES):
                            last = V.tensor_scalar(dst[:, c, :], src[:, c, :], mv[:, c, 0:1], rstd[:, c:c + 1],
                                                   ALU.subtract, ALU.mult)
                        last.then_inc(done, 1)

                    def row_max(dst, src):
                        link(V.tensor_reduce(out=dst, in_=src, axis=AX_X, op=ALU.max))

                    def row_sum(dst, src):
                        link(V.tensor_reduce(out=dst, in_=src, axis=AX_X, op=ALU.add))

                    def route_logits():
                        await_fill(dve, "route", 0)
                        logits = bank("route", 0)[:, 0:TILES * EXPERTS].rearrange("p (c e) -> p c e", c=TILES)
                        row_max(rtmax, logits)
                        V.tensor_tensor(rt[0], logits, over_cols(rtmax, EXPERTS), ALU.subtract).then_inc(route_args, 1)

                    def route_weights():
                        dve.wait_ge(route_exps, 1)
                        row_sum(rtsum, rt[1])
                        link(V.reciprocal(rtsum, rtsum))
                        link(V.tensor_tensor(rt[2], rt[1], over_cols(rtsum, EXPERTS), ALU.mult))

                        def pick(dst, scores):
                            row_max(rtmax, scores)
                            link(V.tensor_tensor(dst, scores, over_cols(rtmax, EXPERTS), ALU.is_equal))
                            link(V.tensor_tensor(dst, dst, over_heads(rank_row[:, :], TILES), ALU.mult))
                            row_max(rtmax, dst)
                            link(V.tensor_tensor(dst, dst, over_cols(rtmax, EXPERTS), ALU.is_equal))

                        pick(rt[3], rt[2])
                        link(V.scalar_tensor_tensor(out=rt[4], in0=rt[3], scalar=-2.0, in1=rt[2], op0=ALU.mult, op1=ALU.add))
                        pick(rt[5], rt[4])
                        link(V.tensor_tensor(rt[3], rt[3], rt[5], ALU.add))
                        link(V.tensor_tensor(rt[3], rt[3], rt[2], ALU.mult))
                        row_sum(rtsum, rt[3])
                        link(V.tensor_scalar(rtsum, rtsum, 1e-20, None, ALU.add))
                        link(V.reciprocal(rtsum, rtsum))
                        V.tensor_tensor(wexp[:, :, 0:EXPERTS], rt[3], over_cols(rtsum, EXPERTS), ALU.mult).then_inc(w_exp_ready, 1)

                    def expert_units():
                        for u, (k, c) in enumerate(units):
                            await_fill(dve, "up2", k, c)
                            dve.wait_ge(sgw_ready, u + 1)
                            V.tensor_tensor(zf[u % 2], bank("up2", k, c)[:, 0:UNIT], zf[u % 2], ALU.mult).then_inc(z_ready, 1)
                        for c in range(TILES):
                            await_fill(dve, "down", c)
                            V.tensor_tensor(xn2[:, c, :], bank("down", c)[:, 0:P], x2[:, c, :], ALU.add).then_inc(out_ready, 1)

                    if not attention:
                        layernorm(x2, xn2, x2_normed)
                        route_logits()
                        route_weights()
                        expert_units()
                        return

                    dve.wait_ge(x_loaded, 16)
                    layernorm(xin, xn, x_normed)
                    await_fill(dve, "ab", 0)
                    ab = bank("ab", 0)[:, 0:64].rearrange("p (c n) -> p c n", c=TILES)
                    lin = sm(2)[:, :, 0:HEADS]
                    link(V.tensor_tensor(lin, ab[:, :, 0:HEADS], over_heads(dt_row[:, :], TILES), ALU.add))
                    V.tensor_copy(ab_arg[:, :, HEADS:], ab[:, :, HEADS:])
                    V.scalar_tensor_tensor(out=ab_arg[:, :, 0:HEADS], in0=lin, scalar=-1.0, in1=lin, op0=ALU.mult,
                                           op1=ALU.max).then_inc(ab_args, 1)

                    def conv(what, i, dst, first_block, tap3, step, done):
                        await_fill(dve, what, i)
                        dve.wait_ge(tap3, i + 1)
                        for d in range(1, TAPS):
                            for j in range(2):
                                blk = 2 * i + j
                                if d > 1:
                                    dve.wait_ge(step, 5 * i + 2 * (d - 2) + j + 1)
                                w = taps[:, first_block + blk, TAPS - 1 - d:TAPS - d]
                                ins = V.scalar_tensor_tensor(
                                    out=dst[:, blk, d:], in0=bank(what, i)[:, TOK * j:TOK * (j + 1) - d],
                                    scalar=w, in1=dst[:, blk, d:], op0=ALU.mult, op1=ALU.add)
                                if d == TAPS - 1 and j == 1:
                                    ins.then_inc(done, 1)
                                else:
                                    ins.then_inc(step, 1)

                    def conv_qk(i):
                        conv("qk", i, qkT, 0, tap3_done, conv_step, conv_done)

                    def conv_v(i):
                        conv("v", i, vT, BLOCKS, v_tap3, v_conv_step, v_conv_done)

                    conv_qk(0)
                    conv_qk(1)
                    dve.wait_ge(ab_exps, 1)
                    e_a, e_b = ab_exp[:, :, 0:HEADS], ab_exp[:, :, HEADS:]
                    t1, t2, t3 = (sm(i)[:, :, 0:HEADS] for i in (3, 4, 5))
                    tb = sm(3)[:, :, HEADS:]
                    link(V.tensor_scalar(tb, e_b, 1.0, None, ALU.add))
                    link(V.reciprocal(tb, tb))
                    link(V.tensor_scalar(beta_tok, tb, 2.0, None, ALU.mult))
                    link(V.tensor_scalar(t1, e_a, 2.0, None, ALU.add))
                    link(V.reciprocal(t1, t1))
                    link(V.tensor_tensor(t1, t1, e_a, ALU.mult))
                    link(V.tensor_tensor(t2, t1, t1, ALU.mult))
                    link(V.tensor_scalar(t3, t2, 1.0 / 17, None, ALU.mult))
                    for k in (15, 13, 11, 9, 7, 5, 3):
                        link(V.scalar_tensor_tensor(out=t3, in0=t3, scalar=1.0 / k, in1=t2, op0=ALU.add, op1=ALU.mult))
                    link(V.scalar_tensor_tensor(out=t3, in0=t3, scalar=1.0, in1=t1, op0=ALU.add, op1=ALU.mult))
                    link(V.tensor_scalar(lin, lin, 0.0, None, ALU.max))
                    link(V.scalar_tensor_tensor(out=t3, in0=t3, scalar=2.0, in1=lin, op0=ALU.mult, op1=ALU.add))
                    V.tensor_tensor(g_tok, t3, over_heads(decay_row[:, :], TILES), ALU.mult).then_inc(g_ready, 1)
                    for i in range(2, BLOCKS // 2):
                        conv_qk(i)
                    if experts:
                        layernorm(x2, xn2, x2_normed)
                    await_fill(dve, "normsT", 0)
                    V.tensor_scalar(z_qk, bank("normsT", 0)[:, 0:64].rearrange("p (c n) -> p c n", c=TILES), L2_EPS, None,
                                    ALU.add).then_inc(norms_read, 1)
                    dve.wait_ge(norms_read, 1)
                    rsqrt(rs_qk, z_qk, sm(16))
                    zk, rk = z_qk[:, :, HEADS:], rs_qk[:, :, HEADS:]
                    link(V.tensor_tensor(m_tok, zk, rk, ALU.mult))
                    link(V.tensor_tensor(b_tok, rk, rk, ALU.mult))
                    V.tensor_tensor(b_tok, b_tok, beta_tok, ALU.mult).then_inc(b_ready, 1)
                    link(V.tensor_scalar(rs_qk[:, :, 0:HEADS], rs_qk[:, :, 0:HEADS], Q_SCALE, None, ALU.mult))
                    dve.wait_ge(gamma_ready, 1)
                    link(V.tensor_scalar(neg_gamma, gamma, -1.0, None, ALU.mult))
                    if experts:
                        route_logits()
                    for g in range(GROUPS):
                        dve.wait_ge(decay_ready, g + 1)
                        dve.wait_ge(bm_ready, g + 1)
                        V.tensor_tensor(eb[:, g], eb[:, g], bm[g % 2], ALU.mult).then_inc(B_ready, 1)
                        await_fill(dve, "kk", g)
                        dve.wait_ge(B_ready, g + 1)
                        V.scalar_tensor_tensor(out=nt[:, g], in0=bank("kk", g)[:, :].rearrange("p (k t) -> p k t", k=4),
                                               scalar=-1.0, in1=eb[:, g], op0=ALU.mult, op1=ALU.mult).then_inc(nt_ready, 1)
                    for g in range(4):
                        q, par = g // 2, g % 2
                        ks = kscale[:, 8 * q:8 * q + 8].rearrange("p (k two) -> p two k", two=2)[:, par]
                        V.tensor_copy(ks, eb[:, g, :, P - 1]).then_inc(kscale_ready, 1)
                    if experts:
                        route_weights()
                    for i in range(4):
                        conv_v(i)
                    link(V.tensor_copy(sub_w, con[:, C_SUB:C_END].rearrange("p (a b) -> p a b", a=SUB).unsqueeze(1)
                                       .broadcast_to([P, 2, SUB, SUB])))
                    dve.wait_ge(sub_loaded, 16)
                    link(V.tensor_copy(sub_w[:, :, 0, 1], sub_n[:, :, 0, 1]))
                    for i in range(2, SUB):
                        prod = sub_prod[:, 0:2 * i * i].rearrange("p (q c j) -> p q c j", q=2, c=i)
                        link(V.tensor_tensor(prod, sub_w[:, :, 0:i, 0:i],
                                             sub_n[:, :, 0:i, i].unsqueeze(2).broadcast_to([P, 2, i, i]), ALU.mult))
                        ins = V.tensor_reduce(out=sub_w[:, :, 0:i, i], in_=prod, axis=AX_X, op=ALU.add)
                        if i < SUB - 1:
                            link(ins)
                    ins.then_inc(sub_solved, 1)
                    dve.wait_ge(sub_solved, 1)
                    V.tensor_copy(sub_t, sub_w.rearrange("p q a b -> p q b a")).then_inc(sub_solved, 1)
                    dve.wait_ge(kscale_ready, 4)
                    for g in range(GROUPS):
                        await_fill(dve, "qk_", g)
                        V.tensor_tensor(eb[:, g], bank("qk_", g)[:, :].rearrange("p (k t) -> p k t", k=4), eb[:, g],
                                        ALU.mult).then_inc(p_ready, 1)
                    for i in range(4, 8):
                        conv_v(i)
                    dve.wait_ge(inv_stored, 32)
                    for q in range(2):
                        await_fill(dve, "ktok", q)
                        V.tensor_tensor(ktok[:, 8 * q:8 * q + 8, :], bank("ktok", q)[:, :].rearrange("p (h d) -> p h d", h=8),
                                        over_cols(kscale[:, 8 * q:8 * q + 8], DK), ALU.mult).then_inc(ktok_ready, 1)
                    if experts:
                        expert_units()

                    def as_halves(t):
                        return t.rearrange("p (i t) -> p i t", i=8)

                    for l, n in enumerate(LEVELS):
                        mask = con[:, C_YM + HALF * l:C_YM + HALF * (l + 1)]
                        for s in range(SUPERS):
                            await_fill(dve, "Y", n, s)
                            V.tensor_tensor(ymid[:, s], as_halves(bank("Y", n, s)[:, :]), over_heads(mask, 8),
                                            ALU.mult).then_inc(y_masked, 1)
                        for s in range(SUPERS):
                            await_fill(dve, "TY", n, s)
                            V.tensor_tensor(tinv[:, s], as_halves(bank("TY", n, s)[:, :]), tinv[:, s], ALU.add)\
                                .then_inc(t_ready, 1)
                            await_fill(dve, "WY", n, s)
                            if n < LEVELS[-1]:
                                V.tensor_tensor(winv[:, s], as_halves(bank("WY", n, s)[:, :]), winv[:, s], ALU.add)\
                                    .then_inc(w_ready, 1)
                            else:
                                for lo in (0, HALF):
                                    r = slice(lo, lo + HALF)
                                    last = V.tensor_tensor(
                                        nt[r, 2 * s:2 * s + 2, :, lo:lo + HALF].rearrange("p a k t -> p (a k) t"),
                                        as_halves(bank("WY", n, s)[r, :]), winv[r, s], ALU.add)
                                last.then_inc(w_ready, 1)
                    for g in range(4, 8):
                        await_fill(dve, "ks", g)
                        dve.wait_ge(r_ready, GROUPS)
                        for k, h in enumerate(heads_of(g)):
                            last = V.scalar_tensor_tensor(out=vr[:, 1, h, :], in0=bank("ks", g)[:, k * P:(k + 1) * P],
                                                          scalar=neg_gamma[:, h:h + 1], in1=vr[:, 1, h, :],
                                                          op0=ALU.mult, op1=ALU.add)
                        last.then_inc(r1_ready, 1)

                    def factors(c):
                        dve.wait_ge(o_squares, 4 * c + 4)
                        a = rs_qk[:, c, 0:HEADS]
                        z, f = o_z[:, c, :], o_fac[:, c, :]
                        link(V.tensor_tensor(z, a, a, ALU.mult))
                        link(V.tensor_tensor(z, z, o_ssq[:, c, :], ALU.mult))
                        link(V.tensor_scalar(z, z, 1.0 / DV, RMS_EPS, ALU.mult, ALU.add))
                        rsqrt(f, z, nw2[:, 0:HEADS])
                        link(V.tensor_tensor(f, f, a, ALU.mult))

                    def gate(g):
                        c, q = g // 4, (g % 4) // 2
                        dve.wait_ge(sgate_ready, 4 * c + 2 * q + 2)
                        for h in heads_of(g):
                            last = V.scalar_tensor_tensor(out=vr[:, c, h, :], in0=vr[:, c, h, :], scalar=o_fac[:, c, h:h + 1],
                                                          in1=sgate[:, c, h, :], op0=ALU.mult, op1=ALU.mult)
                        last.then_inc(gated, 1)

                    factors(0)
                    for g in range(4):
                        gate(g)
                    for g in range(4, 8):
                        await_fill(dve, "qs", g)
                        dve.wait_ge(o_copied, g + 1)
                        for k, h in enumerate(heads_of(g)):
                            last = V.scalar_tensor_tensor(out=vr[:, 1, h, :], in0=bank("qs", g)[:, k * P:(k + 1) * P],
                                                          scalar=gamma[:, h:h + 1], in1=vr[:, 1, h, :],
                                                          op0=ALU.mult, op1=ALU.add)
                        last.then_inc(o_ready, 1)
                    factors(1)
                    for g in range(4, 8):
                        gate(g)
                    if experts:
                        dve.wait_ge(out_ready, TILES)
                    for c in range(TILES):
                        await_fill(dve, "attn", c)
                        V.tensor_tensor(x2[:, c, :], bank("attn", c)[:, 0:P], xin[:, c, :], ALU.add).then_inc(x2_done, 1)

                @block.gpsimd
                def _(pool):
                    G = nc.gpsimd

                    def expert_units():
                        pool.wait_ge(w_exp_ready, 1)
                        for u, (k, c) in enumerate(units):
                            pool.wait_ge(sg_ready, u + 1)
                            z = zf[u % 2].rearrange("p (e i) -> p e i", e=2)
                            G.tensor_tensor(z, z, over_cols(wexp[:, c, 2 * k:2 * k + 2], INTER), ALU.mult).then_inc(sgw_ready, 1)

                    if not attention:
                        expert_units()
                        return

                    for t in (tinv, winv):
                        G.memset(t[:, :, :, :], 0.0).then_inc(inv_zeroed, 1)
                    for i in range(BLOCKS // 2):
                        pool.wait_ge(qk_ready, i + 1)
                        G.tensor_tensor(sq[:, 2 * i:2 * i + 2, :], qkT[:, 2 * i:2 * i + 2, :], qkT[:, 2 * i:2 * i + 2, :],
                                        ALU.mult).then_inc(sq_ready, 1)
                        if i == 0:
                            pool.wait_ge(g_ready, 1)
                        g = i
                        if g >= 2:
                            await_fill(pool, "decay", g - 2)
                        G.tensor_tensor(gm[g % 2], over_heads(le_mask, 4), over_cols(by_group(g_tok, g), P),
                                        ALU.mult).then_inc(gm_ready, 1)
                    pool.wait_ge(b_ready, 1)
                    for g in range(GROUPS):
                        if g >= 2:
                            pool.wait_ge(B_ready, g - 1)
                        G.tensor_tensor(bm[g % 2], over_heads(le_mask, 4), over_cols(by_group(b_tok, g), P),
                                        ALU.mult).then_inc(bm_ready, 1)
                    for i in range(GROUPS):
                        c, n = i // 4, i % 4
                        pool.wait_ge(v_ready, i + 1)
                        v = vr[:, c, 4 * n:4 * n + 4, :]
                        G.tensor_tensor(v, v, over_cols(m_tok[:, c, 4 * n:4 * n + 4], DV), ALU.mult).then_inc(r_ready, 1)
                    if experts:
                        expert_units()

            nc.all_engine_barrier()
            nums = sorted(s.num for s in loop_sems)
            assert nums == list(range(nums[0], nums[-1] + 1))
            nc.sync.sem_clear(range(nums[0], nums[-1] + 1))
            nc.all_engine_barrier()

        turn_of(0, None)
        with nc.Fori(1, batches) as b:
            turn_of(b, b - 1)
        turn_of(None, batches - 1)


def layout_constants():
    import numpy as np
    i = np.arange(P)[:, None]
    j = np.arange(P)[None, :]
    r, t = np.arange(P)[:, None] % HALF, np.arange(HALF)[None, :]
    parts = [i == j, i <= j, i > j]
    for n in LEVELS:
        parts.append((r // (2 * n) == t // (2 * n)) & (r // n % 2 == 1) & (t // n % 2 == 0))
    at = np.arange(4 * HEADS - 2)[None, :]
    parts.append(at == 2 * HEADS - 2 + i // HALF)
    parts.append((np.arange(SUB * SUB) % (SUB + 1) == 0)[None, :])
    return np.ascontiguousarray(np.concatenate([np.broadcast_to(p, (P, p.shape[1])) for p in parts], axis=1).astype(np.float32))


_INS = ["L0_attn_x", "L0_attn_w_q", "L0_attn_w_k", "L0_attn_w_v", "L0_attn_w_a", "L0_attn_w_b", "L0_attn_w_g",
        "L0_attn_w_out", "L0_attn_A_log", "L0_attn_dt_bias", "L0_attn_conv_q", "L0_attn_conv_k", "L0_attn_conv_v",
        "L0_attn_norm_w", "L0_ffn_gate_w", "L0_ffn_wg", "L0_ffn_wu", "L0_ffn_wd", "L0_ffn_swg", "L0_ffn_swu",
        "L0_ffn_swd"]


def kernel(**inputs):
    import numpy as np
    import concourse.bacc as bacc
    from concourse.bass_utils import run_bass_kernel_spmd

    nc = bacc.Bacc("TRN2", target_bir_lowering=False, num_devices=1)
    arrays, args = {}, []
    for name in _INS:
        a = np.ascontiguousarray(inputs[name])
        arrays[f"in_{name}"] = a
        args.append(nc.dram_tensor(f"in_{name}", a.shape, mybir.dt.from_np(a.dtype), kind="ExternalInput").ap())
    arrays["in_consts"] = layout_constants()
    args.append(nc.dram_tensor("in_consts", (P, C_END), F32, kind="ExternalInput").ap())
    args.append(nc.dram_tensor("out_x", inputs["L0_attn_x"].shape, F32, kind="ExternalOutput").ap())
    build_layer(nc, *args)
    r = run_bass_kernel_spmd(nc, [arrays], core_ids=[0])
    return r.results[0]["out_x"]
```

```python
from contextlib import ExitStack

import concourse.bass as bass
from concourse import mybir

F32 = mybir.dt.float32
I32 = mybir.dt.int32
ALU = mybir.AluOpType
ACT = mybir.ActivationFunctionType
AX_X = mybir.AxisListType.X

P = 128
HEADS = 16
DK = 64
DV = 128
TAPS = 4
TILES = 2
TOK = TILES * P
PAD = TAPS - 1
BLOCKS = 2 * HEADS * DK // P
QBLOCKS = BLOCKS // 2
GROUPS = 8
SUPERS = 4
HALF = P // 2
SUB = 16
SUBS = P // SUB
LEVELS = (16, 32)
EXPERTS = 8
INTER = 176
UNIT = 2 * INTER
CHUNKS = EXPERTS // 2 + 1
HID = CHUNKS * UNIT
RSQRT_MAGIC = float(0x5F3759DF)
LN_EPS = 1e-5
L2_EPS = 1e-6
RMS_EPS = 1e-5
Q_SCALE = DK ** -0.5

C_ID, C_LE, C_GT, C_YM = 0, 128, 256, 384
C_IND = C_YM + 64 * len(LEVELS)
C_SUB = C_IND + 4 * HEADS - 2
C_END = C_SUB + SUB * SUB


def build_layer(nc, x, w_q, w_k, w_v, w_a, w_b, w_g, w_out, A_log, dt_bias, conv_q, conv_k, conv_v,
                norm_w, gate_w, wg, wu, wd, swg, swu, swd, consts, out):
    batches = x.shape[0]

    with ExitStack() as ctx:
        def sb(name, shape, dt=F32):
            return ctx.enter_context(nc.sbuf_tensor(name, shape, dt))

        def sem(name):
            return ctx.enter_context(nc.semaphore(name))

        w_qk = sb("w_qk", [P, 2 * HEADS * DK])
        w_val = sb("w_val", [P, HEADS * DV])
        w_gate = sb("w_gate", [P, HEADS * DV])
        w_o = sb("w_o", [P, HEADS, P])
        w_ab = sb("w_ab", [P, 2 * HEADS])
        w_up1 = sb("w_up1", [P, HID])
        w_up2 = sb("w_up2", [P, HID])
        w_down = sb("w_down", [P, CHUNKS, 3, P])
        w_route = sb("w_route", [P, EXPERTS])
        taps = sb("taps", [P, BLOCKS + HEADS, TAPS])
        norm_col = sb("norm_col", [P, 1])
        dt_row = sb("dt_row", [P, HEADS])
        decay_row = sb("decay_row", [P, HEADS])
        con = sb("con", [P, C_END])
        rank_row = sb("rank_row", [P, EXPERTS])
        ident = con[:, C_ID:C_ID + P]
        le_mask = con[:, C_LE:C_LE + P]
        gt_mask = con[:, C_GT:C_GT + P]

        xin = sb("xin", [P, TILES, P])
        xnext = sb("xnext", [P, TILES, P])
        xn = sb("xn", [P, TILES, P])
        xT = sb("xT", [P, TOK])
        qkT = sb("qkT", [P, BLOCKS, TOK])
        eb = sb("eb", [P, GROUPS, 4, P])
        nt = sb("nt", [P, GROUPS, 4, P])
        inverses = sb("inverses", [P, 2, SUPERS, 8, HALF])
        tinv = inverses[:, 0]
        winv = inverses[:, 1]
        ymid = sb("ymid", [P, SUPERS, 8, HALF])
        vr = sb("vr", [P, TILES, HEADS, DV])
        ysol = sb("ysol", [P, TILES, HEADS, DV])
        state = sb("state", [P, HEADS // 2, DV])
        ktok = sb("ktok", [P, HEADS, DK])
        kscale = sb("kscale", [P, HEADS])
        small = sb("small", [P, 26, 2 * 32])
        stats = sb("stats", [P, TILES, 8])
        mv = sb("mv", [P, TILES, 2])
        x2 = sb("x2", [P, TILES, P])
        xn2 = sb("xn2", [P, TILES, P])
        sgate = sb("sgate", [P, TILES, HEADS, DV])
        norm_rows = sb("norm_rows", [2 * HEADS, TOK])
        zbuf = sb("zbuf", [P, 2, UNIT])
        zTbuf = sb("zTbuf", [P, 2, 3 * P])
        hTbuf = sb("hTbuf", [P, TOK])

        flat_y = ysol[:, :, :, :].rearrange("p c h d -> p (c h d)")
        flat_v = vr[:, :, :, :].rearrange("p c h d -> p (c h d)")
        sq = nt[:, :, :, :].rearrange("p g k t -> p (g k t)").rearrange("p (j t) -> p j t", t=TOK)
        vT = flat_y.rearrange("p (j t) -> p j t", t=TOK)
        flat_ymid = ymid[:, :, :, :].rearrange("p s i t -> p (s i t)")
        gm = [flat_ymid[:, 512 * i:512 * (i + 1)].rearrange("p (h t) -> p h t", h=4) for i in range(4)]
        oT = eb
        zf = [zbuf[:, i, :] for i in range(2)]
        zT = [zTbuf[:, i, :] for i in range(2)]
        hT = hTbuf[:, :]
        flat_state = state[:, :, :].rearrange("p j d -> p (j d)")
        flat_ktok = ktok[:, :, :].rearrange("p h d -> p (h d)")

        def sub_tile(t, i):
            return t[:, 512 * i:512 * (i + 1)].rearrange("p (q a b) -> p q a b", q=2, a=SUB)

        sub_n, sub_w = sub_tile(flat_state, 0), sub_tile(flat_state, 1)
        sub_t, sub_prod = sub_tile(flat_ktok, 0), flat_ktok[:, 512:1024]
        shape = (GROUPS * 4, SUBS, SUB, SUB)
        sub_in = nc.dram_tensor("sub_in", shape, F32, kind="Internal").ap()
        sub_out = nc.dram_tensor("sub_out", (2, *shape), F32, kind="Internal").ap()

        def by_partition(d):
            return d.rearrange("g b s t -> g (b s t)").rearrange("g (b n) -> (g b) n", b=4)\
                .rearrange("p (q s t) -> p q s t", q=2, s=SUB)

        def heads_of(g):
            q, par = (g % 4) // 2, g % 2
            return [8 * q + par + 2 * k for k in range(4)]

        def by_group(t, g):
            c, q, par = g // 4, (g % 4) // 2, g % 2
            v = t[:, c]
            v = v[:, 8 * q:8 * q + 8]
            if len(v.shape) == 3:
                return v.rearrange("p (k two) d -> p two k d", two=2)[:, par]
            return v.rearrange("p (k two) -> p two k", two=2)[:, par]

        def over_cols(v, n):
            return v.unsqueeze(2).broadcast_to([P, v.shape[1], n])

        def over_heads(v, n):
            return v.unsqueeze(1).broadcast_to([P, n, v.shape[1]])

        banks = [ctx.enter_context(nc.psum_tensor(f"bank{i}", [P, 512], F32)) for i in range(8)]
        units = [(k, c) for k in range(CHUNKS) for c in range(TILES)]
        ACT_SQUARES = 4

        def before_merges(experts):
            if not experts:
                return [("v", 0)] + [("gate", i) for i in range(4)]
            order = [("v", 0), ("up", 0), ("gate", 0), ("gate", 1)]
            for u in range(1, 4):
                order += [("weigh", u - 1)] + expert_steps(u)
                if u in (1, 2):
                    order += [("gate", u + 1)]
            return order

        def merges(experts):
            pairs = []
            for n in LEVELS:
                pairs += [[("Y", n, s), ("Y", n, s + 1)] for s in range(0, SUPERS, 2)]
                pairs += [[("TY", n, s), ("WY", n, s)] for s in range(SUPERS)]
            after = [[("vt", 0)], [("vt", 4)], [("v", 4)], [("vt", 1)], [("v", 5)], [("vt", 5), ("qk_", 4)], [("v", 6)],
                     [], [("v", 7), ("vt", 2)], [("vt", 6)], [("qk_", 5), ("qk_", 6), ("ktok", 0)], [("ktok", 1)]]
            experts_after = {0: 5, 2: 6, 4: 7, 6: 8, 8: 9}
            order = ([("weigh", 3)] if experts else []) + [("v", 1)]
            if experts:
                order += expert_steps(4) + [("weigh", 4)]
            order += [("v", 2), ("v", 3)]
            order += [("gate", i) for i in range(4, GROUPS)]
            due = None
            for i, (pair, extra) in enumerate(zip(pairs, after)):
                order += [pair[0]]
                if experts and due is not None:
                    order += [("weigh", due)]
                    due = None
                order += [pair[1]]
                if experts and i in experts_after:
                    due = experts_after[i]
                    order += expert_steps(due)
                    if extra and extra[0][0] == "v":
                        order += [("weigh", due)]
                        due = None
                order += extra
            order += [("Y64", s) for s in range(SUPERS)]
            if experts:
                order += expert_steps(len(units)) + expert_steps(len(units) + 1)
            order += [("vt", 3), ("vt", 7)] + ([("outputs",)] if experts else []) + [("norm_next",)]
            order += [("W64", 0), ("qk_", 7), ("W64", 1), ("qk_", 0), ("W64", 2), ("qk_", 1), ("W64", 3), ("qk_", 2), ("qk_", 3)]
            return order

        def expert_steps(u):
            out_ = []
            if u < len(units):
                out_ += [("up", u)]
            if 1 <= u <= len(units):
                out_ += [("flip", u - 1)]
            if 2 <= u < len(units) + 2:
                out_ += [("down", u - 2)]
            return out_

        def all_expert_steps():
            out_ = []
            for u in range(len(units) + 2):
                if 1 <= u <= len(units):
                    out_ += [("weigh", u - 1)]
                out_ += expert_steps(u)
            return out_

        qk_order = [at[0] for what, *at in merges(False) if what == "qk_"]
        vt_order = [at[0] for what, *at in merges(False) if what == "vt"]

        def banks_of(steps):
            out_ = []
            for what, *at in steps:
                if what == "up":
                    out_ += [("up1", *at), ("up2", *at)]
                elif what == "flip":
                    out_ += [("zT", *at)]
                elif what not in ("down", "weigh"):
                    out_ += [(what, *at)]
            return out_

        def fill_order(attention, experts, opening):
            if not attention:
                if opening:
                    return [("xT", 0), ("ab", 0)]
                return [("hT", 0), ("route", 0)] + [("down_", 0)] + banks_of(all_expert_steps())
            order = [("qk", 0), ("qk", 1), ("gam", 0), ("decay", 0), ("decay", 1)]
            if experts:
                order += [("hT", 0), ("route", 0)]
            order += [("qk", 2), ("decay", 2), ("decay", 3), ("qk", 3), ("decay", 4), ("decay", 5), ("qk", 4), ("decay", 6),
                      ("decay", 7), ("qk", 5), ("qk", 6), ("qk", 7), ("norms", 0), ("normsT", 0)]
            order += [("kk", g) for g in range(GROUPS)]
            if experts:
                order += [("down_", 0)]
            order += banks_of(before_merges(experts) + merges(experts))
            if opening:
                order += [("xT", 0), ("ab", 0)]
            order += [("y", g) for g in range(4)] + [("state", q) for q in range(2)]
            order += [("ks", g) for g in range(4, 8)] + [("o", g) for g in range(4)]
            order += [("y", g) for g in range(4, 8)]
            order += [(k, g) for g in range(4, 8) for k in ("o", "qs")]
            order += [("oT", g) for g in range(4)] + [("attn", 0)]
            order += [("oT", g) for g in range(4, 8)] + [("attn", 1)]
            return order

        def assign(order):
            fill_at, before, last_in, turns, held = {}, {}, {}, [0] * 8, {}
            n = 0
            for key in order:
                if key[0] == "outputs":
                    held = {}
                if key[0] in ("outputs", "norm_next"):
                    continue
                while n % 8 in held:
                    n += 1
                b = n % 8
                n += 1
                fill_at[key] = (b, turns[b])
                turns[b] += 1
                if b in last_in:
                    before[key] = last_in[b]
                last_in[b] = key
                if key[0] == "down_":
                    held[b] = key
            return fill_at, before

        fill_at, before = {}, {}

        bank_filled = [sem(f"bank_filled{i}") for i in range(8)]

        def bank(*key):
            return banks[fill_at[key][0]]

        def full(*key):
            return bank_filled[fill_at[key][0]]

        def await_fill(eng, *key):
            b, t = fill_at[key]
            eng.wait_ge(bank_filled[b], t + 1)

        x_loaded = sem("x_loaded")
        x_kept = sem("x_kept")
        x_normed = sem("x_normed")
        xT_ready = sem("xT_ready")
        ab_args = sem("ab_args")
        ab_exps = sem("ab_exps")
        tap3_done = sem("tap3_done")
        conv_done = sem("conv_done")
        qk_ready = sem("qk_ready")
        sq_ready = sem("sq_ready")
        last_sq_ready = sem("last_sq_ready")
        v_ready = sem("v_ready")
        gm_ready = sem("gm_ready")
        gamma_ready = sem("gamma_ready")
        decay_ready = sem("decay_ready")
        b_ready = sem("b_ready")
        decay_masked = sem("decay_masked")
        m_ready = sem("m_ready")
        nt_ready = sem("nt_ready")
        w_ready = sem("w_ready")
        t_ready = sem("t_ready")
        y_masked = sem("y_masked")
        p_ready = sem("p_ready")
        kscale_ready = sem("kscale_ready")
        ktok_ready = sem("ktok_ready")
        y64_ready = sem("y64_ready")
        full_ready = sem("full_ready")
        r_ready = sem("r_ready")
        r1_ready = sem("r1_ready")
        v_tap3 = sem("v_tap3")
        v_conv_step = sem("v_conv_step")
        v_conv_done = sem("v_conv_done")
        vT_ready = sem("vT_ready")
        norm_copied = sem("norm_copied")
        sub_stored = sem("sub_stored")
        sub_loaded = sem("sub_loaded")
        sub_solved = sem("sub_solved")
        inv_stored = sem("inv_stored")
        inv_loaded = sem("inv_loaded")
        inv_zeroed = sem("inv_zeroed")
        y_ready = sem("y_ready")
        state_ready = sem("state_ready")
        o_copied = sem("o_copied")
        o_ready = sem("o_ready")
        o_squares = sem("o_squares")
        squares_ready = sem("squares_ready")
        sums_ready = sem("sums_ready")
        sgate_ready = sem("sgate_ready")
        gated = sem("gated")
        oT_ready = sem("oT_ready")
        x2_normed = sem("x2_normed")
        hT_ready = sem("hT_ready")
        route_args = sem("route_args")
        route_exps = sem("route_exps")
        w_exp_ready = sem("w_exp_ready")
        sg_ready = sem("sg_ready")
        sgw_ready = sem("sgw_ready")
        z_ready = sem("z_ready")
        zT_ready = sem("zT_ready")
        out_ready = sem("out_ready")
        out_stored = sem("out_stored")
        dve_step = sem("dve_step")
        conv_step = sem("conv_step")
        norms_read = sem("norms_read")
        x2_done = sem("x2_done")
        zT_used = sem("zT_used")
        w_part = sem("w_part")
        loop_sems = bank_filled + [squares_ready, sums_ready,
            v_tap3, v_conv_step, v_conv_done, vT_ready, norm_copied, sub_stored, sub_loaded, sub_solved,
            inv_stored, inv_loaded, inv_zeroed, conv_step, norms_read, x2_done, zT_used, w_part, x_loaded, x_normed, xT_ready, ab_args, ab_exps, x_kept, tap3_done, conv_done, qk_ready, sq_ready,
            v_ready, gm_ready, gamma_ready, decay_ready, b_ready, decay_masked, m_ready, last_sq_ready, nt_ready,
            w_ready, t_ready, y_masked, p_ready, kscale_ready, ktok_ready, y64_ready, full_ready, r_ready, r1_ready,
            y_ready, state_ready, o_copied, o_ready, o_squares, sgate_ready, gated, oT_ready, x2_normed, hT_ready,
            route_args, route_exps, w_exp_ready, sg_ready, sgw_ready, z_ready, zT_ready, out_ready, out_stored,
            dve_step]
        weights_in = sem("weights_in")
        raw_in = sem("raw_in")
        prep_done = sem("prep_done")

        def level(n):
            return LEVELS.index(n)

        read_by = {
            "xT": lambda i: (xT_ready, 1), "ab": lambda i: (ab_args, 1), "qk": lambda i: (conv_done, i + 1),
            "v": lambda i: (v_conv_done, i + 1), "vt": lambda i: (v_ready, vt_order.index(i) + 1), "gam": lambda i: (gamma_ready, 1), "decay": lambda g: (decay_ready, g + 1),
            "norms": lambda i: (norm_copied, 1), "normsT": lambda i: (norms_read, 1), "kk": lambda g: (nt_ready, g + 1),
            "qk_": lambda g: (p_ready, qk_order.index(g) + 1), "ktok": lambda q: (ktok_ready, q + 1),
            "Y": lambda n, s: (y_masked, SUPERS * level(n) + s + 1),
            "TY": lambda n, s: (t_ready, SUPERS * level(n) + s + 1),
            "WY": lambda n, s: (w_ready, SUPERS * level(n) + s + 1),
            "Y64": lambda s: (y64_ready, s + 1), "W64": lambda s: (full_ready, s + 1),
            "y": lambda g: (y_ready, g + 1), "state": lambda q: (state_ready, q + 1), "o": lambda g: (o_copied, g + 1),
            "ks": lambda g: (r1_ready, g - 3), "qs": lambda g: (o_ready, g - 3), "gate": lambda i: (sgate_ready, i + 1),
            "oT": lambda g: (oT_ready, g + 1), "attn": lambda c: (x2_done, c + 1), "hT": lambda i: (hT_ready, 1),
            "route": lambda i: (route_args, 1), "down_": lambda i: (out_ready, TILES),
            "up1": lambda u: (sg_ready, u + 1), "up2": lambda u: (z_ready, u + 1), "zT": lambda u: (zT_ready, u + 1),
        }

        def claim(pe, *key):
            if key in before:
                what, *at = before[key]
                pe.wait_ge(*read_by[what](*at))

        def sm(i, n=32):
            return small[:, i, 0:TILES * n].rearrange("p (c n) -> p c n", c=TILES)

        ab_arg, ab_exp = sm(0), sm(1)
        g_tok, beta_tok, m_tok, b_tok = (sm(6 + i, HEADS) for i in range(4))
        z_qk, rs_qk = sm(10), sm(11)
        neg_b = small[:, 6, 32:64].rearrange("p (c n) -> p c n", c=TILES)
        gamma = small[:, 12, 0:HEADS]
        neg_gamma = small[:, 12, HEADS:2 * HEADS]
        o_ssq, o_fac, o_z = sm(13, HEADS), sm(14, HEADS), sm(15, HEADS)
        nw1, nw2 = small[:, 16, :], small[:, 17, :]
        rt = [sm(18 + i, EXPERTS) for i in range(7)]
        rtmax = small[:, 25, 0:2]
        rtsum = small[:, 25, 2:4]
        wexp = sb("wexp", [P, TILES, EXPERTS + 2])

        with nc.Block() as block:
            @block.sync
            def _(sp):
                loads = [
                    (w_qk[:, 0:HEADS * DK], w_q), (w_qk[:, HEADS * DK:], w_k), (w_gate[:, :], w_g),
                    (w_ab[:, 0:HEADS], w_a), (w_ab[:, HEADS:], w_b),
                    (taps[:, 0:QBLOCKS, :], conv_q.rearrange("(j p) w -> p j w", p=P)),
                    (taps[:, QBLOCKS:BLOCKS, :], conv_k.rearrange("(j p) w -> p j w", p=P)),
                    (w_val[:, :], w_v), (taps[:, BLOCKS:, :], conv_v.rearrange("(j p) w -> p j w", p=P)),
                    (dt_row[:, :], dt_bias.partition_broadcast(P)),
                    (w_up1[:, 0:EXPERTS * INTER].rearrange("p (e i) -> p e i", e=EXPERTS), wg.rearrange("e h i -> h e i")),
                    (w_up2[:, 0:EXPERTS * INTER].rearrange("p (e i) -> p e i", e=EXPERTS), wu.rearrange("e h i -> h e i")),
                    (w_up1[:, EXPERTS * INTER:], swg), (w_up2[:, EXPERTS * INTER:], swu),
                    (con[:, :], consts),
                    (w_route[:, :], gate_w.rearrange("e h -> h e")),
                ]
                flat_wd = wd.rearrange("e i h -> (e i) h")
                for k in range(CHUNKS):
                    src = flat_wd[UNIT * k:UNIT * (k + 1), :] if k < CHUNKS - 1 else swd
                    loads.append((w_down[:, k, 0:2, :], src[0:2 * P, :].rearrange("(j p) h -> p j h", p=P)))
                    loads.append((w_down[0:UNIT - 2 * P, k, 2, :], src[2 * P:UNIT, :]))
                with nc.allow_non_contiguous_dma(reason="the router's weights are small"):
                    for dst, src in loads:
                        sp.dma_start(dst, src).then_inc(weights_in, 16)
                sp.wait_ge(weights_in, 16 * len(loads))

            @block.scalar
            def _(act):
                raw = [
                    (w_o[:, :, :], w_out.rearrange("(h d) n -> d h n", d=DV)),
                    (norm_col[:, :], norm_w.rearrange("(d one) -> d one", one=1)),
                    (decay_row[:, :], A_log.partition_broadcast(P)),
                ]
                for dst, src in raw:
                    act.dma_start(dst, src).then_inc(raw_in, 16)
                act.wait_ge(raw_in, 16 * len(raw))
                nc.scalar.activation(decay_row[:, :], decay_row[:, :], ACT.Exp).then_inc(prep_done, 1)

            @block.vector
            def _(dve):
                nc.vector.memset(wexp[:, :, EXPERTS:EXPERTS + 2], 1.0)
                for e in range(EXPERTS):
                    nc.vector.memset(rank_row[:, e:e + 1], float(EXPERTS - e))
                dve.wait_ge(raw_in, 16 * 3)
                nc.vector.tensor_scalar(w_o[:, :, :], w_o[:, :, :], norm_col[:, 0:1], None, ALU.mult)
                dve.wait_ge(prep_done, 1)
                nc.vector.tensor_scalar(decay_row[:, :], decay_row[:, :], -1.0, None, ALU.mult)

        def turn_of(b_in, b_out, b_next):
            attention, experts, opening = b_in is not None, b_out is not None, b_next is not None
            order = fill_order(attention, experts, opening)
            found = assign(order)
            fill_at.clear()
            fill_at.update(found[0])
            before.clear()
            before.update(found[1])

            def tiles_of_seq(t, b):
                at = slice(b, b + 1) if isinstance(b, int) else bass.ds(b, 1)
                return t[at, :, :].rearrange("o (c p) d -> p (o c) d", p=P)

            with nc.Block() as block:
                @block.sync
                def _(sp):
                    if opening:
                        if attention:
                            sp.wait_ge(x_kept, 1)
                        sp.dma_start(xnext[:, :, :], tiles_of_seq(x, b_next)).then_inc(x_loaded, 16)
                        if not attention:
                            sp.wait_ge(x_loaded, 16)
                    if attention:
                        sp.wait_ge(nt_ready, GROUPS)
                        n_rows = nt[:, :, :, :].rearrange("p g k t -> p (g k) t")
                        for k in range(SUBS):
                            rows = slice(SUB * k, SUB * (k + 1))
                            sp.dma_start(sub_in[:, k].rearrange("g s t -> s g t"), n_rows[rows, :, rows]).then_inc(sub_stored, 16)
                        sp.wait_ge(sub_stored, 16 * SUBS)
                        sp.dma_start(sub_n, by_partition(sub_in)).then_inc(sub_loaded, 16)
                        sp.wait_ge(sub_solved, 2)
                        sp.dma_start(by_partition(sub_out[1]), sub_w).then_inc(inv_stored, 16)
                        sp.wait_ge(sub_solved, 3)
                        sp.dma_start(by_partition(sub_out[0]), sub_t).then_inc(inv_stored, 16)
                        sp.wait_ge(inv_stored, 32)
                        sp.wait_ge(inv_zeroed, 1)
                        blocks = inverses[:, :, :, :, :].rearrange("p m s i t -> p (m s i) t")
                        for k in range(SUBS):
                            rows = slice(SUB * k, SUB * (k + 1))
                            cols = slice(SUB * k % HALF, SUB * k % HALF + SUB)
                            sp.dma_start(blocks[rows, :, cols], sub_out.rearrange("m g b s t -> (m g) b s t")[:, k]
                                         .rearrange("g s t -> s g t")).then_inc(inv_loaded, 16)
                    if experts:
                        sp.wait_ge(out_ready, TILES)
                        sp.dma_start(tiles_of_seq(out, b_out), xn2[:, :, :]).then_inc(out_stored, 16)
                        sp.wait_ge(out_stored, 16)

                @block.tensor
                def _(pe):
                    T = nc.tensor

                    def mm(o, l, r, start=True, stop=True):
                        return T.matmul(o, l, r, start=start, stop=stop)

                    def experts_input():
                        claim(pe, "hT", 0)
                        pe.wait_ge(x2_normed, 1)
                        for c in range(TILES):
                            last = T.transpose(bank("hT", 0)[:, c * P:(c + 1) * P], xn2[:, c, :], ident)
                        last.then_inc(full("hT", 0), 1)
                        claim(pe, "route", 0)
                        pe.wait_ge(hT_ready, 1)
                        for c in range(TILES):
                            last = mm(bank("route", 0)[:, EXPERTS * c:EXPERTS * (c + 1)], hT[:, c * P:(c + 1) * P], w_route[:, :])
                        last.then_inc(full("route", 0), 1)

                    def up(u):
                        k, c = units[u]
                        for what, w in (("up1", w_up1), ("up2", w_up2)):
                            claim(pe, what, u)
                            mm(bank(what, u)[:, 0:UNIT], hT[:, c * P:(c + 1) * P],
                               w[:, UNIT * k:UNIT * (k + 1)]).then_inc(full(what, u), 1)

                    def flip(u):
                        k, c = units[u]
                        claim(pe, "zT", u)
                        pe.wait_ge(z_ready, u + 1)
                        for j in range(3):
                            w = min(P, UNIT - j * P)
                            last = T.transpose(bank("zT", u)[0:w, j * P:(j + 1) * P], zf[u % 2][:, j * P:j * P + w], ident)
                        last.then_inc(full("zT", u), 1)

                    def down(u):
                        k, c = units[u]
                        pe.wait_ge(zT_ready, u + 1)
                        for j in range(3):
                            w = min(P, UNIT - j * P)
                            last = mm(bank("down_", 0)[:, c * P:(c + 1) * P], zT[u % 2][0:w, j * P:(j + 1) * P], w_down[0:w, k, j, :],
                                      start=(u == 0 and j == 0), stop=(u == len(units) - 1 and j == 2))
                        if u == len(units) - 1:
                            last.then_inc(full("down_", 0), 1)
                        else:
                            last.then_inc(zT_used, 1)

                    fill = {"up": up, "flip": flip, "down": down}
                    def opening_products():
                        claim(pe, "xT", 0)
                        pe.wait_ge(x_normed, 1)
                        for c in range(TILES):
                            last = T.transpose(bank("xT", 0)[:, c * P:(c + 1) * P], xn[:, c, :], ident)
                        last.then_inc(full("xT", 0), 1)
                        claim(pe, "ab", 0)
                        pe.wait_ge(xT_ready, 1)
                        for c in range(TILES):
                            last = mm(bank("ab", 0)[:, 32 * c:32 * (c + 1)], xT[:, c * P:(c + 1) * P], w_ab[:, :])
                        last.then_inc(full("ab", 0), 1)

                    if not attention and opening:
                        opening_products()
                        return
                    if not attention:
                        experts_input()
                        claim(pe, "down_", 0)
                        for what, *at in all_expert_steps():
                            if what in fill:
                                fill[what](*at)
                        return

                    def project(what, i, w):
                        claim(pe, what, i)
                        for j in range(2):
                            last = mm(bank(what, i)[:, TOK * j:TOK * (j + 1)], w[:, (2 * i + j) * P:(2 * i + j + 1) * P], xT[:, :])
                        last.then_inc(full(what, i), 1)

                    def fill_gate(i):
                        c, n = i // 4, i % 4
                        claim(pe, "gate", i)
                        mm(bank("gate", i)[:, :], xT[:, c * P:(c + 1) * P],
                           w_gate[:, 512 * n:512 * (n + 1)]).then_inc(full("gate", i), 1)

                    def decays(g):
                        claim(pe, "decay", g)
                        pe.wait_ge(gm_ready, g + 1)
                        mm(bank("decay", g)[:, :], gt_mask, gm[g % 4].rearrange("p h t -> p (h t)")).then_inc(full("decay", g), 1)

                    project("qk", 0, w_qk)
                    project("qk", 1, w_qk)
                    claim(pe, "gam", 0)
                    mm(bank("gam", 0)[:, 0:HEADS], le_mask, g_tok[:, 1, :]).then_inc(full("gam", 0), 1)
                    decays(0)
                    decays(1)
                    if experts:
                        experts_input()
                    for i in range(2, 5):
                        project("qk", i, w_qk)
                        decays(2 * i - 2)
                        decays(2 * i - 1)
                    for i in range(5, BLOCKS // 2):
                        project("qk", i, w_qk)
                    claim(pe, "norms", 0)
                    for j in range(BLOCKS):
                        if j // 2 < ACT_SQUARES:
                            pe.wait_ge(sq_ready, j // 2 + 1)
                        else:
                            pe.wait_ge(last_sq_ready, j // 2 + 1 - ACT_SQUARES)
                        at = C_IND + 2 * HEADS - 2 - 2 * j
                        last = mm(bank("norms", 0)[0:2 * HEADS, 0:TOK], con[:, at:at + 2 * HEADS], sq[:, j, :],
                                  start=(j == 0), stop=(j == BLOCKS - 1))
                    last.then_inc(full("norms", 0), 1)
                    claim(pe, "normsT", 0)
                    pe.wait_ge(norm_copied, 1)
                    for c in range(TILES):
                        last = T.transpose(bank("normsT", 0)[:, 32 * c:32 * (c + 1)], norm_rows[:, c * P:(c + 1) * P],
                                           con[0:2 * HEADS, C_ID:C_ID + 2 * HEADS])
                    last.then_inc(full("normsT", 0), 1)
                    def head_T(h, c, block0):
                        po = DK * (h % 2)
                        return qkT[po:po + DK, block0 + h // 2, c * P:(c + 1) * P]

                    for g in range(GROUPS):
                        claim(pe, "kk", g)
                        pe.wait_ge(qk_ready, BLOCKS // 2)
                        for k, h in enumerate(heads_of(g)):
                            kT = head_T(h, g // 4, QBLOCKS)
                            last = mm(bank("kk", g)[:, k * P:(k + 1) * P], kT, kT)
                        last.then_inc(full("kk", g), 1)
                    if experts:
                        claim(pe, "down_", 0)

                    def fill_v(i):
                        project("v", i, w_val)

                    def fill_qk(g):
                        claim(pe, "qk_", g)
                        for k, h in enumerate(heads_of(g)):
                            last = mm(bank("qk_", g)[:, k * P:(k + 1) * P], head_T(h, g // 4, QBLOCKS), head_T(h, g // 4, 0))
                        last.then_inc(full("qk_", g), 1)

                    def fill_ktok(q):
                        claim(pe, "ktok", q)
                        for j in range(4):
                            last = T.transpose(bank("ktok", q)[:, j * P:(j + 1) * P], qkT[:, QBLOCKS + 4 * q + j, 0:P], ident)
                        last.then_inc(full("ktok", q), 1)

                    def fill_vt(i):
                        c, n = i // 4, i % 4
                        claim(pe, "vt", i)
                        pe.wait_ge(vT_ready, 2 * n + 2)
                        for k in range(4):
                            last = T.transpose(bank("vt", i)[:, k * P:(k + 1) * P], vT[:, 4 * n + k, c * P:(c + 1) * P], ident)
                        last.then_inc(full("vt", i), 1)

                    def fill_Y(n, s):
                        claim(pe, "Y", n, s)
                        if level(n) == 0:
                            pe.wait_ge(inv_loaded, 16 * SUBS)
                        else:
                            pe.wait_ge(t_ready, SUPERS * (level(n) - 1) + s + 1)
                        for i in range(8):
                            for lo in (0, HALF):
                                r = slice(lo, lo + HALF)
                                last = mm(bank("Y", n, s)[r, HALF * i:HALF * (i + 1)],
                                          nt[r, 2 * s + i // 4, i % 4, lo:lo + HALF], tinv[r, s, i, :])
                        last.then_inc(full("Y", n, s), 1)

                    def fill_TY(n, s):
                        claim(pe, "TY", n, s)
                        pe.wait_ge(y_masked, SUPERS * level(n) + s + 1)
                        if level(n):
                            pe.wait_ge(w_ready, SUPERS * (level(n) - 1) + s + 1)
                        for i in range(8):
                            for lo in (0, HALF):
                                r = slice(lo, lo + HALF)
                                last = mm(bank("TY", n, s)[r, HALF * i:HALF * (i + 1)], winv[r, s, i, :], ymid[r, s, i, :])
                        last.then_inc(full("TY", n, s), 1)

                    def fill_WY(n, s):
                        claim(pe, "WY", n, s)
                        for i in range(8):
                            for lo in (0, HALF):
                                r = slice(lo, lo + HALF)
                                last = mm(bank("WY", n, s)[r, HALF * i:HALF * (i + 1)], ymid[r, s, i, :], winv[r, s, i, :])
                        last.then_inc(full("WY", n, s), 1)

                    hi, lo_ = slice(HALF, P), slice(0, HALF)
                    done = SUPERS * (len(LEVELS) - 1)

                    def fill_Y64(s):
                        claim(pe, "Y64", s)
                        pe.wait_ge(t_ready, done + s + 1)
                        for i in range(8):
                            last = mm(bank("Y64", s)[hi, HALF * i:HALF * (i + 1)], nt[lo_, 2 * s + i // 4, i % 4, hi], tinv[lo_, s, i, :])
                        last.then_inc(full("Y64", s), 1)

                    def fill_W64(s):
                        claim(pe, "W64", s)
                        pe.wait_ge(y64_ready, s + 1)
                        pe.wait_ge(w_ready, done + s + 1)
                        for i in range(8):
                            last = mm(bank("W64", s)[lo_, HALF * i:HALF * (i + 1)], ymid[hi, s, i, :], nt[hi, 2 * s + i // 4, i % 4, hi])
                        last.then_inc(full("W64", s), 1)

                    fill.update({"v": fill_v, "vt": fill_vt, "Y": fill_Y, "TY": fill_TY, "WY": fill_WY, "Y64": fill_Y64,
                                 "W64": fill_W64, "ktok": fill_ktok, "qk_": fill_qk, "gate": fill_gate})
                    for what, *at in before_merges(experts) + merges(experts):
                        if what in fill:
                            fill[what](*at)

                    def solve(g):
                        c, q = g // 4, (g % 4) // 2
                        claim(pe, "y", g)
                        pe.wait_ge(full_ready, g // 2 + 1)
                        if c == 0:
                            pe.wait_ge(r_ready, max(vt_order.index(2 * q), vt_order.index(2 * q + 1)) + 1)
                        else:
                            pe.wait_ge(r1_ready, g - 3)
                        for k, h in enumerate(heads_of(g)):
                            last = mm(bank("y", g)[:, k * P:(k + 1) * P], nt[:, g, k, :], vr[:, c, h, :])
                        last.then_inc(full("y", g), 1)

                    def attend(g):
                        claim(pe, "o", g)
                        pe.wait_ge(p_ready, qk_order.index(g) + 1)
                        pe.wait_ge(y_ready, g + 1)
                        for k, h in enumerate(heads_of(g)):
                            last = mm(bank("o", g)[:, k * P:(k + 1) * P], eb[:, g, k, :], ysol[:, g // 4, h, :])
                        last.then_inc(full("o", g), 1)

                    def read_state(what, g, block0):
                        claim(pe, what, g)
                        pe.wait_ge(state_ready, (g - 4) // 2 + 1)
                        for k, h in enumerate(heads_of(g)):
                            po = DK * (h % 2)
                            last = mm(bank(what, g)[:, k * P:(k + 1) * P], head_T(h, 1, block0), state[po:po + DK, h // 2, :])
                        last.then_inc(full(what, g), 1)

                    if opening:
                        opening_products()
                    for g in range(4):
                        solve(g)
                    for q in range(2):
                        claim(pe, "state", q)
                        pe.wait_ge(ktok_ready, q + 1)
                        pe.wait_ge(y_ready, 2 * q + 2)
                        for h in range(8 * q, 8 * q + 8):
                            po, j = DK * (h % 2), (h % 8) // 2
                            last = mm(bank("state", q)[po:po + DK, j * DV:(j + 1) * DV], ktok[:, h, :], ysol[:, 0, h, :])
                        last.then_inc(full("state", q), 1)
                    for g in range(4, 8):
                        read_state("ks", g, QBLOCKS)
                    for g in range(4):
                        attend(g)
                    for g in range(4, 8):
                        solve(g)
                    for g in range(4, 8):
                        attend(g)
                        read_state("qs", g, 0)
                    for c in range(TILES):
                        for g in range(4 * c, 4 * c + 4):
                            claim(pe, "oT", g)
                            pe.wait_ge(gated, g + 1)
                            for k, h in enumerate(heads_of(g)):
                                last = T.transpose(bank("oT", g)[:, k * P:(k + 1) * P], vr[:, c, h, :], ident)
                            last.then_inc(full("oT", g), 1)
                        claim(pe, "attn", c)
                        for g in range(4 * c, 4 * c + 4):
                            pe.wait_ge(oT_ready, g + 1)
                            for k, h in enumerate(heads_of(g)):
                                last = mm(bank("attn", c)[:, 0:P], oT[:, g, k, :], w_o[:, h, :],
                                          start=(g % 4 == 0 and k == 0), stop=(g % 4 == 3 and k == 3))
                        last.then_inc(full("attn", c), 1)

                @block.scalar
                def _(act):
                    A = nc.scalar

                    def copy_hT():
                        await_fill(act, "hT", 0)
                        A.activation(hT, bank("hT", 0)[:, 0:TOK], ACT.Copy).then_inc(hT_ready, 1)

                    def route_exp():
                        act.wait_ge(route_args, 1)
                        A.activation(rt[1], rt[0], ACT.Exp).then_inc(route_exps, 1)

                    def silu_up(u):
                        await_fill(act, "up1", u)
                        if u >= 2:
                            await_fill(act, "zT", u - 2)
                        A.activation(zf[u % 2], bank("up1", u)[:, 0:UNIT], ACT.Silu).then_inc(sg_ready, 1)

                    def copy_zT(u):
                        await_fill(act, "zT", u)
                        if u >= 2:
                            act.wait_ge(zT_used, u - 1)
                        A.activation(zT[u % 2][:, 0:2 * P], bank("zT", u)[:, 0:2 * P], ACT.Copy)
                        w = UNIT - 2 * P
                        A.activation(zT[u % 2][0:w, 2 * P:3 * P], bank("zT", u)[0:w, 2 * P:3 * P],
                                     ACT.Copy).then_inc(zT_ready, 1)

                    def copy_xT():
                        await_fill(act, "xT", 0)
                        A.activation(xT[:, :], bank("xT", 0)[:, 0:TOK], ACT.Copy).then_inc(xT_ready, 1)

                    def decay_beta_exp():
                        act.wait_ge(ab_args, 1)
                        A.activation(ab_exp, ab_arg, ACT.Exp, scale=-1.0).then_inc(ab_exps, 1)

                    if not attention and opening:
                        copy_xT()
                        decay_beta_exp()
                        return
                    if not attention:
                        copy_hT()
                        route_exp()
                        for what, *at in all_expert_steps():
                            if what == "up":
                                silu_up(*at)
                            elif what == "flip":
                                copy_zT(*at)
                        return

                    def newest_tap(what, i, dst, first_block, done):
                        await_fill(act, what, i)
                        for j in range(2):
                            last = A.activation(dst[:, 2 * i + j, :], bank(what, i)[:, TOK * j:TOK * (j + 1)], ACT.Copy,
                                                scale=taps[:, first_block + 2 * i + j, TAPS - 1:TAPS])
                        last.then_inc(done, 1)

                    def silu_gate(i):
                        c, n = i // 4, i % 4
                        await_fill(act, "gate", i)
                        A.activation(sgate[:, c, 4 * n:4 * n + 4, :].rearrange("p h d -> p (h d)"), bank("gate", i)[:, :],
                                     ACT.Silu).then_inc(sgate_ready, 1)

                    def silu_qk(i):
                        act.wait_ge(conv_done, i + 1)
                        v = qkT[:, 2 * i:2 * i + 2, :]
                        A.activation(v, v, ACT.Silu).then_inc(qk_ready, 1)
                        if i < ACT_SQUARES:
                            act.wait_ge(qk_ready, i + 1)
                            A.activation(sq[:, 2 * i:2 * i + 2, :], v, ACT.Square).then_inc(sq_ready, 1)

                    def decay_exp(g):
                        await_fill(act, "decay", g)
                        A.activation(eb[:, g, :, :].rearrange("p k t -> p (k t)"), bank("decay", g)[:, :],
                                     ACT.Exp).then_inc(decay_ready, 1)

                    newest_tap("qk", 0, qkT, 0, tap3_done)
                    newest_tap("qk", 1, qkT, 0, tap3_done)
                    await_fill(act, "gam", 0)
                    A.activation(gamma, bank("gam", 0)[:, 0:HEADS], ACT.Exp).then_inc(gamma_ready, 1)
                    decay_exp(0)
                    decay_exp(1)
                    if experts:
                        copy_hT()
                    for i in range(2, 5):
                        newest_tap("qk", i, qkT, 0, tap3_done)
                        decay_exp(2 * i - 2)
                        decay_exp(2 * i - 1)
                    newest_tap("qk", 5, qkT, 0, tap3_done)
                    if experts:
                        route_exp()
                    newest_tap("qk", 6, qkT, 0, tap3_done)
                    newest_tap("qk", 7, qkT, 0, tap3_done)
                    for i in range(BLOCKS // 2):
                        silu_qk(i)
                    await_fill(act, "norms", 0)
                    A.activation(norm_rows[:, :], bank("norms", 0)[0:2 * HEADS, 0:TOK], ACT.Copy).then_inc(norm_copied, 1)

                    def silu_v(i):
                        act.wait_ge(v_conv_done, i + 1)
                        v = vT[:, 2 * i:2 * i + 2, :]
                        A.activation(v, v, ACT.Silu).then_inc(vT_ready, 1)

                    silus = 0
                    for what, *at in before_merges(experts) + merges(experts):
                        if what == "v":
                            i, = at
                            newest_tap("v", i, vT, BLOCKS, v_tap3)
                            if i >= 4:
                                silu_v(silus)
                                silus += 1
                        elif what == "gate":
                            silu_gate(*at)
                        elif what == "up":
                            silu_up(*at)
                        elif what == "flip":
                            copy_zT(*at)
                        elif what == "vt":
                            c, n = at[0] // 4, at[0] % 4
                            while silus < 2 * n + 2:
                                silu_v(silus)
                                silus += 1
                            await_fill(act, "vt", *at)
                            A.activation(vr[:, c, 4 * n:4 * n + 4, :].rearrange("p h d -> p (h d)"), bank("vt", *at)[:, :],
                                         ACT.Copy).then_inc(v_ready, 1)
                        elif what == "Y64":
                            s, = at
                            await_fill(act, "Y64", s)
                            A.activation(ymid[HALF:P, s, :, :].rearrange("p i t -> p (i t)"), bank("Y64", s)[HALF:P, :],
                                         ACT.Copy).then_inc(y64_ready, 1)
                        elif what == "W64":
                            s, = at
                            await_fill(act, "W64", s)
                            A.activation(nt[0:HALF, 2 * s:2 * s + 2, :, HALF:P].rearrange("p a k t -> p (a k) t"),
                                         bank("W64", s)[0:HALF, :].rearrange("p (i t) -> p i t", i=8),
                                         ACT.Copy).then_inc(full_ready, 1)

                    def copy_y(g):
                        await_fill(act, "y", g)
                        A.activation(by_group(ysol, g), bank("y", g)[:, :].rearrange("p (k d) -> p k d", k=4),
                                     ACT.Copy).then_inc(y_ready, 1)

                    def copy_o(g):
                        await_fill(act, "o", g)
                        A.activation(by_group(vr, g), bank("o", g)[:, :].rearrange("p (k d) -> p k d", k=4),
                                     ACT.Copy).then_inc(o_copied, 1)

                    def squares(g):
                        scratch = tinv[:, g % 4].rearrange("p i t -> p (i t)")
                        for k, h in enumerate(heads_of(g)):
                            last = A.activation(scratch[:, k * DV:(k + 1) * DV], vr[:, g // 4, h, :], ACT.Square,
                                                accum_out=o_ssq[:, g // 4, h:h + 1])
                        last.then_inc(o_squares, 1)

                    if opening:
                        copy_xT()
                        decay_beta_exp()
                    for g in range(4):
                        copy_y(g)
                    for q in range(2):
                        await_fill(act, "state", q)
                        A.activation(state[:, 4 * q:4 * q + 4, :].rearrange("p j d -> p (j d)"), bank("state", q)[:, :],
                                     ACT.Copy).then_inc(state_ready, 1)
                    for g in range(4):
                        copy_o(g)
                    for g in range(4, 8):
                        copy_y(g)
                    for g in range(4, 8):
                        copy_o(g)
                    def copy_oT(g):
                        await_fill(act, "oT", g)
                        A.activation(oT[:, g, :, :].rearrange("p k t -> p (k t)"), bank("oT", g)[:, :],
                                     ACT.Copy).then_inc(oT_ready, 1)

                    for g in range(4, 8):
                        act.wait_ge(o_ready, g - 3)
                        squares(g)
                    for g in range(GROUPS):
                        copy_oT(g)

                @block.vector
                def _(dve):
                    V = nc.vector
                    steps = [0]

                    def link(ins):
                        steps[0] += 1
                        ins.then_inc(dve_step, 1)
                        dve.wait_ge(dve_step, steps[0])

                    def rsqrt(y, z, tmp):
                        link(V.tensor_scalar(tmp.bitcast(I32), z.bitcast(I32), 1, None, ALU.logical_shift_right))
                        link(V.tensor_scalar(y.bitcast(I32), tmp.bitcast(I32), -1.0, RSQRT_MAGIC, ALU.mult, ALU.add))
                        for _ in range(3):
                            link(V.tensor_tensor(tmp, y, y, ALU.mult))
                            link(V.scalar_tensor_tensor(out=tmp, in0=tmp, scalar=-0.5, in1=z, op0=ALU.mult, op1=ALU.mult))
                            link(V.scalar_tensor_tensor(out=y, in0=tmp, scalar=1.5, in1=y, op0=ALU.add, op1=ALU.mult))

                    def layernorm(src, dst, done):
                        for c in range(TILES):
                            V.bn_stats(stats[:, c, 0:6], src[:, c, :]).then_inc(dve_step, 1)
                        steps[0] += TILES
                        dve.wait_ge(dve_step, steps[0])
                        for c in range(TILES):
                            V.bn_aggr(mv[:, c, :], stats[:, c, 0:6]).then_inc(dve_step, 1)
                        steps[0] += TILES
                        dve.wait_ge(dve_step, steps[0])
                        var, rstd, tmp = nw1[:, 0:TILES], nw1[:, 8:8 + TILES], nw1[:, 16:16 + TILES]
                        link(V.tensor_scalar(var, mv[:, :, 1], LN_EPS, None, ALU.add))
                        rsqrt(rstd, var, tmp)
                        for c in range(TILES):
                            last = V.tensor_scalar(dst[:, c, :], src[:, c, :], mv[:, c, 0:1], rstd[:, c:c + 1],
                                                   ALU.subtract, ALU.mult)
                        last.then_inc(done, 1)

                    def row_max(dst, src):
                        link(V.tensor_reduce(out=dst, in_=src, axis=AX_X, op=ALU.max))

                    def row_sum(dst, src):
                        link(V.tensor_reduce(out=dst, in_=src, axis=AX_X, op=ALU.add))

                    def route_logits():
                        await_fill(dve, "route", 0)
                        logits = bank("route", 0)[:, 0:TILES * EXPERTS].rearrange("p (c e) -> p c e", c=TILES)
                        row_max(rtmax, logits)
                        V.tensor_tensor(rt[0], logits, over_cols(rtmax, EXPERTS), ALU.subtract).then_inc(route_args, 1)

                    def route_weights():
                        dve.wait_ge(route_exps, 1)
                        row_sum(rtsum, rt[1])
                        link(V.reciprocal(rtsum, rtsum))
                        link(V.tensor_tensor(rt[2], rt[1], over_cols(rtsum, EXPERTS), ALU.mult))

                        def pick(dst, scores):
                            row_max(rtmax, scores)
                            link(V.tensor_tensor(dst, scores, over_cols(rtmax, EXPERTS), ALU.is_equal))
                            link(V.tensor_tensor(dst, dst, over_heads(rank_row[:, :], TILES), ALU.mult))
                            row_max(rtmax, dst)
                            link(V.tensor_tensor(dst, dst, over_cols(rtmax, EXPERTS), ALU.is_equal))

                        pick(rt[3], rt[2])
                        link(V.scalar_tensor_tensor(out=rt[4], in0=rt[3], scalar=-2.0, in1=rt[2], op0=ALU.mult, op1=ALU.add))
                        pick(rt[5], rt[4])
                        link(V.tensor_tensor(rt[3], rt[3], rt[5], ALU.add))
                        link(V.tensor_tensor(rt[3], rt[3], rt[2], ALU.mult))
                        row_sum(rtsum, rt[3])
                        link(V.tensor_scalar(rtsum, rtsum, 1e-20, None, ALU.add))
                        link(V.reciprocal(rtsum, rtsum))
                        V.tensor_tensor(wexp[:, :, 0:EXPERTS], rt[3], over_cols(rtsum, EXPERTS), ALU.mult).then_inc(w_exp_ready, 1)

                    def expert_unit(u):
                        await_fill(dve, "up2", u)
                        dve.wait_ge(sgw_ready, u + 1)
                        V.tensor_tensor(zf[u % 2], bank("up2", u)[:, 0:UNIT], zf[u % 2], ALU.mult).then_inc(z_ready, 1)

                    def expert_outputs():
                        for c in range(TILES):
                            await_fill(dve, "down_", 0)
                            V.tensor_tensor(xn2[:, c, :], bank("down_", 0)[:, c * P:(c + 1) * P], x2[:, c, :], ALU.add).then_inc(out_ready, 1)

                    def normalise_next():
                        dve.wait_ge(x_loaded, 16)
                        layernorm(xnext, xn, x_normed)

                    lin = sm(2)[:, :, 0:HEADS]

                    def decay_beta_args():
                        await_fill(dve, "ab", 0)
                        ab = bank("ab", 0)[:, 0:64].rearrange("p (c n) -> p c n", c=TILES)
                        link(V.tensor_tensor(lin, ab[:, :, 0:HEADS], over_heads(dt_row[:, :], TILES), ALU.add))
                        V.tensor_copy(ab_arg[:, :, HEADS:], ab[:, :, HEADS:])
                        V.scalar_tensor_tensor(out=ab_arg[:, :, 0:HEADS], in0=lin, scalar=-1.0, in1=lin, op0=ALU.mult,
                                               op1=ALU.max).then_inc(ab_args, 1)

                    def decay_beta():
                        dve.wait_ge(ab_exps, 1)
                        e_a, e_b = ab_exp[:, :, 0:HEADS], ab_exp[:, :, HEADS:]
                        t1, t2, t3 = (sm(i)[:, :, 0:HEADS] for i in (3, 4, 5))
                        tb = sm(3)[:, :, HEADS:]
                        link(V.tensor_scalar(tb, e_b, 1.0, None, ALU.add))
                        link(V.reciprocal(tb, tb))
                        link(V.tensor_scalar(beta_tok, tb, 2.0, None, ALU.mult))
                        link(V.tensor_scalar(t1, e_a, 2.0, None, ALU.add))
                        link(V.reciprocal(t1, t1))
                        link(V.tensor_tensor(t1, t1, e_a, ALU.mult))
                        link(V.tensor_tensor(t2, t1, t1, ALU.mult))
                        link(V.tensor_scalar(t3, t2, 1.0 / 17, None, ALU.mult))
                        for k in (15, 13, 11, 9, 7, 5, 3):
                            link(V.scalar_tensor_tensor(out=t3, in0=t3, scalar=1.0 / k, in1=t2, op0=ALU.add, op1=ALU.mult))
                        link(V.scalar_tensor_tensor(out=t3, in0=t3, scalar=1.0, in1=t1, op0=ALU.add, op1=ALU.mult))
                        link(V.tensor_scalar(lin, lin, 0.0, None, ALU.max))
                        link(V.scalar_tensor_tensor(out=t3, in0=t3, scalar=2.0, in1=lin, op0=ALU.mult, op1=ALU.add))
                        V.tensor_tensor(g_tok, t3, over_heads(decay_row[:, :], TILES), ALU.mult)

                    if not attention and opening:
                        normalise_next()
                        decay_beta_args()
                        decay_beta()
                        return
                    if not attention:
                        layernorm(x2, xn2, x2_normed)
                        route_logits()
                        route_weights()
                        for u in range(len(units)):
                            expert_unit(u)
                        expert_outputs()
                        return

                    if experts:
                        layernorm(x2, xn2, x2_normed)

                    def conv(what, i, dst, first_block, tap3, step, done):
                        await_fill(dve, what, i)
                        dve.wait_ge(tap3, i + 1)
                        for d in range(1, TAPS):
                            for j in range(2):
                                blk = 2 * i + j
                                if d > 1:
                                    dve.wait_ge(step, 5 * i + 2 * (d - 2) + j + 1)
                                w = taps[:, first_block + blk, TAPS - 1 - d:TAPS - d]
                                ins = V.scalar_tensor_tensor(
                                    out=dst[:, blk, d:], in0=bank(what, i)[:, TOK * j:TOK * (j + 1) - d],
                                    scalar=w, in1=dst[:, blk, d:], op0=ALU.mult, op1=ALU.add)
                                if d == TAPS - 1 and j == 1:
                                    ins.then_inc(done, 1)
                                else:
                                    ins.then_inc(step, 1)

                    def conv_qk(i):
                        conv("qk", i, qkT, 0, tap3_done, conv_step, conv_done)

                    def conv_v(i):
                        conv("v", i, vT, BLOCKS, v_tap3, v_conv_step, v_conv_done)

                    for i in range(BLOCKS // 2):
                        conv_qk(i)
                        if experts and i == 0:
                            route_logits()
                    for i in range(ACT_SQUARES, BLOCKS // 2):
                        dve.wait_ge(qk_ready, i + 1)
                        v = qkT[:, 2 * i:2 * i + 2, :]
                        V.tensor_tensor(sq[:, 2 * i:2 * i + 2, :], v, v, ALU.mult).then_inc(last_sq_ready, 1)
                    await_fill(dve, "normsT", 0)
                    V.tensor_scalar(z_qk, bank("normsT", 0)[:, 0:64].rearrange("p (c n) -> p c n", c=TILES), L2_EPS, None,
                                    ALU.add).then_inc(norms_read, 1)
                    dve.wait_ge(norms_read, 1)
                    zk, rk = z_qk[:, :, HEADS:], rs_qk[:, :, HEADS:]
                    link(V.reciprocal(rk, zk))
                    link(V.scalar_tensor_tensor(out=neg_b, in0=rk, scalar=-1.0, in1=beta_tok, op0=ALU.mult, op1=ALU.mult))
                    V.tensor_tensor(b_tok, rk, beta_tok, ALU.mult).then_inc(b_ready, 1)
                    for g in range(GROUPS):
                        dve.wait_ge(decay_masked, g + 1)
                        await_fill(dve, "kk", g)
                        for k, h in enumerate(heads_of(g)):
                            last = V.scalar_tensor_tensor(out=nt[:, g, k, :], in0=bank("kk", g)[:, k * P:(k + 1) * P],
                                                          scalar=neg_b[:, g // 4, h:h + 1], in1=eb[:, g, k, :],
                                                          op0=ALU.mult, op1=ALU.mult)
                        last.then_inc(nt_ready, 1)
                    dve.wait_ge(b_ready, 1)
                    for g in range(4):
                        q, par = g // 2, g % 2
                        ks = kscale[:, 8 * q:8 * q + 8].rearrange("p (k two) -> p two k", two=2)[:, par]
                        V.tensor_tensor(ks, eb[:, g, :, P - 1], by_group(b_tok, g), ALU.mult).then_inc(kscale_ready, 1)
                    if experts:
                        route_weights()
                    conv_v(0)
                    link(V.tensor_copy(sub_w, con[:, C_SUB:C_END].rearrange("p (a b) -> p a b", a=SUB).unsqueeze(1)
                                       .broadcast_to([P, 2, SUB, SUB])))
                    dve.wait_ge(sub_loaded, 16)
                    link(V.tensor_copy(sub_w[:, :, 0, 1], sub_n[:, :, 0, 1]))
                    def then_step(ins):
                        steps[0] += 1
                        ins.then_inc(dve_step, 1)
                        return steps[0]

                    reduced = [steps[0], steps[0]]
                    units_at = {3: 0, 9: 1, 13: 2} if experts else {}
                    for i in range(2, SUB):
                        if i in units_at:
                            expert_unit(units_at[i])
                        prods = [sub_prod[:, q * 256:q * 256 + i * i].rearrange("p (c j) -> p c j", c=i) for q in range(2)]
                        multiplied = [0, 0]
                        for q in range(2):
                            dve.wait_ge(dve_step, reduced[q])
                            multiplied[q] = then_step(V.tensor_tensor(
                                prods[q], sub_w[:, q, 0:i, 0:i],
                                sub_n[:, q, 0:i, i].unsqueeze(1).broadcast_to([P, i, i]), ALU.mult))
                        for q in range(2):
                            dve.wait_ge(dve_step, multiplied[q])
                            ins = V.tensor_reduce(out=sub_w[:, q, 0:i, i], in_=prods[q], axis=AX_X, op=ALU.add)
                            if i < SUB - 1:
                                reduced[q] = then_step(ins)
                            else:
                                ins.then_inc(sub_solved, 1)
                    dve.wait_ge(sub_solved, 2)
                    V.tensor_copy(sub_t, sub_w.rearrange("p q a b -> p q b a")).then_inc(sub_solved, 1)
                    def as_halves(t):
                        return t.rearrange("p (i t) -> p i t", i=8)

                    def weigh_qk(g):
                        dve.wait_ge(kscale_ready, 4)
                        await_fill(dve, "qk_", g)
                        for k, h in enumerate(heads_of(g)):
                            last = V.scalar_tensor_tensor(out=eb[:, g, k, :], in0=bank("qk_", g)[:, k * P:(k + 1) * P],
                                                          scalar=b_tok[:, g // 4, h:h + 1], in1=eb[:, g, k, :],
                                                          op0=ALU.mult, op1=ALU.mult)
                        last.then_inc(p_ready, 1)

                    def norm_factors():
                        rsqrt(rs_qk, z_qk, sm(16))
                        link(V.tensor_scalar(rs_qk[:, :, 0:HEADS], rs_qk[:, :, 0:HEADS], Q_SCALE, None, ALU.mult))
                        dve.wait_ge(gamma_ready, 1)
                        link(V.tensor_scalar(neg_gamma, gamma, -1.0, None, ALU.mult))
                        V.tensor_tensor(m_tok, zk, rk, ALU.mult).then_inc(m_ready, 1)

                    for what, *at in merges(experts):
                        if what == "v":
                            conv_v(*at)
                            if at[0] == 3:
                                norm_factors()
                        elif what == "qk_":
                            weigh_qk(*at)
                        elif what == "weigh":
                            expert_unit(*at)
                        elif what == "outputs":
                            expert_outputs()
                        elif what == "norm_next" and opening:
                            normalise_next()
                        elif what == "ktok":
                            q, = at
                            dve.wait_ge(inv_stored, 32)
                            await_fill(dve, "ktok", q)
                            V.tensor_tensor(ktok[:, 8 * q:8 * q + 8, :], bank("ktok", q)[:, :].rearrange("p (h d) -> p h d", h=8),
                                            over_cols(kscale[:, 8 * q:8 * q + 8], DK), ALU.mult).then_inc(ktok_ready, 1)
                        elif what == "Y":
                            n, s = at
                            mask = con[:, C_YM + HALF * level(n):C_YM + HALF * (level(n) + 1)]
                            await_fill(dve, "Y", n, s)
                            V.tensor_tensor(ymid[:, s], as_halves(bank("Y", n, s)[:, :]), over_heads(mask, 8),
                                            ALU.mult).then_inc(y_masked, 1)
                        elif what == "TY":
                            n, s = at
                            await_fill(dve, "TY", n, s)
                            V.tensor_tensor(tinv[:, s], as_halves(bank("TY", n, s)[:, :]), tinv[:, s], ALU.add)\
                                .then_inc(t_ready, 1)
                        elif what == "WY":
                            n, s = at
                            await_fill(dve, "WY", n, s)
                            if n < LEVELS[-1]:
                                V.tensor_tensor(winv[:, s], as_halves(bank("WY", n, s)[:, :]), winv[:, s], ALU.add)\
                                    .then_inc(w_ready, 1)
                            else:
                                for lo in (0, HALF):
                                    r = slice(lo, lo + HALF)
                                    last = V.tensor_tensor(
                                        nt[r, 2 * s:2 * s + 2, :, lo:lo + HALF].rearrange("p a k t -> p (a k) t"),
                                        as_halves(bank("WY", n, s)[r, :]), winv[r, s], ALU.add)
                                last.then_inc(w_ready, 1)
                    if opening:
                        decay_beta_args()
                        decay_beta()
                    for g in range(4, 8):
                        await_fill(dve, "ks", g)
                        dve.wait_ge(r_ready, GROUPS)
                        for k, h in enumerate(heads_of(g)):
                            last = V.scalar_tensor_tensor(out=vr[:, 1, h, :], in0=bank("ks", g)[:, k * P:(k + 1) * P],
                                                          scalar=neg_gamma[:, h:h + 1], in1=vr[:, 1, h, :],
                                                          op0=ALU.mult, op1=ALU.add)
                        last.then_inc(r1_ready, 1)
                    for g in range(4):
                        dve.wait_ge(squares_ready, g + 1)
                        V.tensor_reduce(out=by_group(o_ssq, g), in_=winv[:, g].rearrange("p i t -> p (i t)")
                                        .rearrange("p (k d) -> p k d", k=4), axis=AX_X, op=ALU.add).then_inc(sums_ready, 1)

                    def factors(c):
                        if c == 0:
                            dve.wait_ge(sums_ready, 4)
                        else:
                            dve.wait_ge(o_squares, 4)
                        a = rs_qk[:, c, 0:HEADS]
                        z, f = o_z[:, c, :], o_fac[:, c, :]
                        link(V.tensor_tensor(z, a, a, ALU.mult))
                        link(V.tensor_tensor(z, z, o_ssq[:, c, :], ALU.mult))
                        link(V.tensor_scalar(z, z, 1.0 / DV, RMS_EPS, ALU.mult, ALU.add))
                        rsqrt(f, z, nw2[:, 0:HEADS])
                        link(V.tensor_tensor(f, f, a, ALU.mult))

                    def gate(g):
                        c, q = g // 4, (g % 4) // 2
                        dve.wait_ge(sgate_ready, 4 * c + 2 * q + 2)
                        for h in heads_of(g):
                            last = V.scalar_tensor_tensor(out=vr[:, c, h, :], in0=vr[:, c, h, :], scalar=o_fac[:, c, h:h + 1],
                                                          in1=sgate[:, c, h, :], op0=ALU.mult, op1=ALU.mult)
                        last.then_inc(gated, 1)

                    factors(0)
                    for g in range(4, 8):
                        await_fill(dve, "qs", g)
                        dve.wait_ge(o_copied, g + 1)
                        for k, h in enumerate(heads_of(g)):
                            last = V.scalar_tensor_tensor(out=vr[:, 1, h, :], in0=bank("qs", g)[:, k * P:(k + 1) * P],
                                                          scalar=gamma[:, h:h + 1], in1=vr[:, 1, h, :],
                                                          op0=ALU.mult, op1=ALU.add)
                        last.then_inc(o_ready, 1)
                        gate(g - 4)
                    factors(1)
                    for g in range(4, 8):
                        gate(g)
                    if experts:
                        dve.wait_ge(out_ready, TILES)
                    for c in range(TILES):
                        await_fill(dve, "attn", c)
                        V.tensor_tensor(x2[:, c, :], bank("attn", c)[:, 0:P], xin[:, c, :], ALU.add).then_inc(x2_done, 1)

                @block.gpsimd
                def _(pool):
                    G = nc.gpsimd

                    def expert_units():
                        pool.wait_ge(w_exp_ready, 1)
                        for u, (k, c) in enumerate(units):
                            pool.wait_ge(sg_ready, u + 1)
                            z = zf[u % 2].rearrange("p (e i) -> p e i", e=2)
                            G.tensor_tensor(z, z, over_cols(wexp[:, c, 2 * k:2 * k + 2], INTER), ALU.mult).then_inc(sgw_ready, 1)

                    if not attention:
                        if experts:
                            expert_units()
                        return

                    def keep_later(g):
                        if g >= 4:
                            await_fill(pool, "decay", g - 4)
                        G.tensor_tensor(gm[g % 4], over_heads(le_mask, 4), over_cols(by_group(g_tok, g), P),
                                        ALU.mult).then_inc(gm_ready, 1)

                    def mask_decay(g):
                        pool.wait_ge(decay_ready, g + 1)
                        G.tensor_tensor(eb[:, g], eb[:, g], over_heads(le_mask, 4), ALU.mult).then_inc(decay_masked, 1)

                    for g in range(4):
                        keep_later(g)
                    G.tensor_copy(xin[:, :, :], xnext[:, :, :]).then_inc(x_kept, 1)
                    for g in range(4, GROUPS):
                        keep_later(g)
                        mask_decay(g - 4)
                    for g in range(4, GROUPS):
                        mask_decay(g)
                    G.memset(inverses[:, :, :, :, :], 0.0).then_inc(inv_zeroed, 1)
                    if experts:
                        expert_units()
                    pool.wait_ge(m_ready, 1)
                    for j, i in enumerate(vt_order):
                        c, n = i // 4, i % 4
                        pool.wait_ge(v_ready, j + 1)
                        v = vr[:, c, 4 * n:4 * n + 4, :]
                        G.tensor_tensor(v, v, over_cols(m_tok[:, c, 4 * n:4 * n + 4], DV), ALU.mult).then_inc(r_ready, 1)
                    for g in range(4):
                        pool.wait_ge(o_copied, g + 1)
                        o = by_group(vr, g)
                        G.tensor_tensor(winv[:, g].rearrange("p i t -> p (i t)").rearrange("p (k d) -> p k d", k=4), o, o,
                                        ALU.mult).then_inc(squares_ready, 1)

            nc.all_engine_barrier()
            nums = sorted(s.num for s in loop_sems)
            assert nums == list(range(nums[0], nums[-1] + 1))
            nc.sync.sem_clear(range(nums[0], nums[-1] + 1))
            nc.all_engine_barrier()

        turn_of(None, None, 0)
        turn_of(0, None, 1)
        with nc.Fori(1, batches - 1) as b:
            turn_of(b, b - 1, b + 1)
        turn_of(batches - 1, batches - 2, None)
        turn_of(None, batches - 1, None)


def layout_constants():
    import numpy as np
    i = np.arange(P)[:, None]
    j = np.arange(P)[None, :]
    r, t = np.arange(P)[:, None] % HALF, np.arange(HALF)[None, :]
    parts = [i == j, i <= j, i > j]
    for n in LEVELS:
        parts.append((r // (2 * n) == t // (2 * n)) & (r // n % 2 == 1) & (t // n % 2 == 0))
    at = np.arange(4 * HEADS - 2)[None, :]
    parts.append(at == 2 * HEADS - 2 + i // HALF)
    parts.append((np.arange(SUB * SUB) % (SUB + 1) == 0)[None, :])
    return np.ascontiguousarray(np.concatenate([np.broadcast_to(p, (P, p.shape[1])) for p in parts], axis=1).astype(np.float32))


_INS = ["L0_attn_x", "L0_attn_w_q", "L0_attn_w_k", "L0_attn_w_v", "L0_attn_w_a", "L0_attn_w_b", "L0_attn_w_g",
        "L0_attn_w_out", "L0_attn_A_log", "L0_attn_dt_bias", "L0_attn_conv_q", "L0_attn_conv_k", "L0_attn_conv_v",
        "L0_attn_norm_w", "L0_ffn_gate_w", "L0_ffn_wg", "L0_ffn_wu", "L0_ffn_wd", "L0_ffn_swg", "L0_ffn_swu",
        "L0_ffn_swd"]


def kernel(**inputs):
    import numpy as np
    import concourse.bacc as bacc
    from concourse.bass_utils import run_bass_kernel_spmd

    nc = bacc.Bacc("TRN2", target_bir_lowering=False, num_devices=1)
    arrays, args = {}, []
    for name in _INS:
        a = np.ascontiguousarray(inputs[name])
        arrays[f"in_{name}"] = a
        args.append(nc.dram_tensor(f"in_{name}", a.shape, mybir.dt.from_np(a.dtype), kind="ExternalInput").ap())
    arrays["in_consts"] = layout_constants()
    args.append(nc.dram_tensor("in_consts", (P, C_END), F32, kind="ExternalInput").ap())
    args.append(nc.dram_tensor("out_x", inputs["L0_attn_x"].shape, F32, kind="ExternalOutput").ap())
    build_layer(nc, *args)
    r = run_bass_kernel_spmd(nc, [arrays], core_ids=[0])
    return r.results[0]["out_x"]
```
